# Optimizing a Trainium2 kernel written in Bass

```python
import numpy as np
import jax
import jax.numpy as jnp

def _softmax(x, axis=-1):
    return jax.nn.softmax(x, axis=axis)

def _gelu(x):
    return jax.nn.gelu(x, approximate=True)

def _silu(x):
    return jax.nn.silu(x)

def _sigmoid(x):
    return jax.nn.sigmoid(x)

def _layernorm(x, axis=-1, eps=1e-05):
    m = jnp.mean(x, axis=axis, keepdims=True)
    v = jnp.var(x, axis=axis, keepdims=True)
    return (x - m) / jnp.sqrt(v + eps)

def _scatter_add(tgt, idx, src, axis=0):
    return tgt.at[idx].add(src)

def _segment_sum(src, seg, n):
    return jax.ops.segment_sum(src, seg, n)
kernel_name = 'mk_cond_resid_d4_seqx_r4_4c448d'

def setup_inputs(seed: int=0):
    np.random.seed(seed)
    _w = jnp.asarray

    def _rec_inputs():
        import jax
        import jax.numpy as jnp
        _rk = jax.random.key(seed)
        x = -7.109e-05 + 0.9999 * jax.random.normal(jax.random.fold_in(_rk, 1), (4, 512, 256), jnp.float32)
        _lenS = 512 - jax.random.randint(jax.random.fold_in(_rk, 7), (4,), 0, max(1, 512 // 4) + 1, jnp.int32)
        _lenS2 = 512 - jax.random.randint(jax.random.fold_in(_rk, 8), (4,), 0, max(1, 512 // 4) + 1, jnp.int32)
        itok_B_0_8 = jax.random.randint(jax.random.fold_in(_rk, 11), (4,), 0, 9, jnp.int32)
        itok_B_0_7 = jax.random.randint(jax.random.fold_in(_rk, 12), (4,), 0, 8, jnp.int32)
        itok_B_0_2 = jax.random.randint(jax.random.fold_in(_rk, 13), (4,), 0, 3, jnp.int32)
        return (x, itok_B_0_8, itok_B_0_7, itok_B_0_2)
    x, itok_B_0_8, itok_B_0_7, itok_B_0_2 = _rec_inputs()

    def _L0_cond_setup():
        import jax, jax.numpy as jnp
        import numpy as np
        LN_EPS = 1e-05
        key = jax.random.key(seed)
        ks = jax.random.split(key, 8)
        B, S, H, A, L = (32, 512, 256, 64, 10)
        return {'hidden_states': jax.random.normal(ks[0], (B, S, H), dtype=jnp.float32), 'language_ids': jax.random.randint(ks[1], (B,), 0, L, dtype=jnp.int64), 'W1': jax.random.normal(ks[2], (L, H, A), dtype=jnp.float32) * (1.0 / np.sqrt(H)), 'b1': jnp.zeros((L, A), dtype=jnp.float32), 'W2': jax.random.normal(ks[3], (L, A, H), dtype=jnp.float32) * (1.0 / np.sqrt(A)), 'b2': jnp.zeros((L, H), dtype=jnp.float32), 'gamma': jnp.ones((L, H), dtype=jnp.float32), 'beta': jnp.zeros((L, H), dtype=jnp.float32)}
    _L0_cond_all = _L0_cond_setup()
    _L0_cond_in = {k: v for k, v in _L0_cond_all.items() if k in ('W1', 'b1', 'W2', 'b2', 'gamma', 'beta')}
    del _L0_cond_all

    def _L1_cond_setup():
        import jax, jax.numpy as jnp
        import numpy as np
        S, O, H = (8, 256, 256)
        B, N = (32, 128)
        key = jax.random.key(seed)
        k1, k2, k3, k4 = jax.random.split(key, 4)
        x = jax.random.normal(k1, (B, N, H), dtype=jnp.float32)
        subject_id = jax.random.randint(k2, (B,), 0, S)
        wbound = jnp.sqrt(2.0 / 6.0) * jnp.sqrt(3.0 / H)
        weight = jax.random.uniform(k3, (S, O, H), minval=-wbound, maxval=wbound, dtype=jnp.float32)
        bbound = 1.0 / jnp.sqrt(H)
        bias = jax.random.uniform(k4, (S, O), minval=-bbound, maxval=bbound, dtype=jnp.float32)
        return {'x': x, 'subject_id': subject_id, 'weight': weight, 'bias': bias}
    _L1_cond_all = _L1_cond_setup()
    _L1_cond_in = {k: v for k, v in _L1_cond_all.items() if k in ('weight', 'bias')}
    del _L1_cond_all

    def _L2_cond_setup():
        import jax, jax.numpy as jnp
        import numpy as np
        B, S, D, F, E = (8, 256, 256, 1024, 4)

        def _dense(x, wi, wo):
            return jax.nn.relu(x @ wi) @ wo
        key = jax.random.key(seed)
        ks = jax.random.split(key, 10)
        scale = 0.02
        return {'hidden_states': jax.random.normal(ks[0], (B, S, D), jnp.float32), 'type_idx': jax.random.randint(ks[1], (B,), 0, 3, jnp.int32), 'expert_wi': jax.random.normal(ks[2], (E, D, F), jnp.float32) * scale, 'expert_wo': jax.random.normal(ks[3], (E, F, D), jnp.float32) * scale, 'share_wi': jax.random.normal(ks[4], (3, D, F), jnp.float32) * scale, 'share_wo': jax.random.normal(ks[5], (3, F, D), jnp.float32) * scale, 'gate_vecs': jnp.array([[0.22, 0.22, 0.2, 0.2], [0.2, 0.22, 0.22, 0.2], [0.2, 0.2, 0.22, 0.22]], jnp.float32), 'gate_w1': jax.random.normal(ks[6], (4 * D, D), jnp.float32) * scale, 'gate_w2': jax.random.normal(ks[7], (D, 4), jnp.float32) * scale}
    _L2_cond_all = _L2_cond_setup()
    _L2_cond_in = {k: v for k, v in _L2_cond_all.items() if k in ('expert_wi', 'expert_wo', 'share_wi', 'share_wo', 'gate_vecs', 'gate_w1', 'gate_w2')}
    del _L2_cond_all

    def _L3_cond_setup():
        import jax, jax.numpy as jnp
        import numpy as np
        NEG_INF = -1e+30
        key = jax.random.key(seed)
        k1, k2, k3, k4, k5 = jax.random.split(key, 5)
        B, S, D, A = (16, 256, 256, 64)
        hidden = jax.random.normal(k1, (B, S, D), dtype=jnp.float32)
        W1 = jax.random.normal(k2, (D, A), dtype=jnp.float32) / np.sqrt(D)
        b1 = jax.random.normal(k3, (A,), dtype=jnp.float32) * 0.01
        v = jax.random.normal(k4, (A,), dtype=jnp.float32) / np.sqrt(A)
        prompt_type_ids = jax.random.randint(k5, (B,), 0, 3, dtype=jnp.int32)
        return {'hidden': hidden, 'W1': W1, 'b1': b1, 'v': v, 'prompt_type_ids': prompt_type_ids}
    _L3_cond_all = _L3_cond_setup()
    _L3_cond_in = {k: v for k, v in _L3_cond_all.items() if k in ('W1', 'b1', 'v')}
    del _L3_cond_all
    return {'x': x, 'itok_B_0_8': itok_B_0_8, 'itok_B_0_7': itok_B_0_7, 'itok_B_0_2': itok_B_0_2, 'L0_cond_W1': _L0_cond_in['W1'], 'L0_cond_b1': _L0_cond_in['b1'], 'L0_cond_W2': _L0_cond_in['W2'], 'L0_cond_b2': _L0_cond_in['b2'], 'L0_cond_gamma': _L0_cond_in['gamma'], 'L0_cond_beta': _L0_cond_in['beta'], 'L1_cond_weight': _L1_cond_in['weight'], 'L1_cond_bias': _L1_cond_in['bias'], 'L2_cond_expert_wi': _L2_cond_in['expert_wi'], 'L2_cond_expert_wo': _L2_cond_in['expert_wo'], 'L2_cond_share_wi': _L2_cond_in['share_wi'], 'L2_cond_share_wo': _L2_cond_in['share_wo'], 'L2_cond_gate_vecs': _L2_cond_in['gate_vecs'], 'L2_cond_gate_w1': _L2_cond_in['gate_w1'], 'L2_cond_gate_w2': _L2_cond_in['gate_w2'], 'L3_cond_W1': _L3_cond_in['W1'], 'L3_cond_b1': _L3_cond_in['b1'], 'L3_cond_v': _L3_cond_in['v']}

def reference(x, itok_B_0_8, itok_B_0_7, itok_B_0_2, L0_cond_W1, L0_cond_b1, L0_cond_W2, L0_cond_b2, L0_cond_gamma, L0_cond_beta, L1_cond_weight, L1_cond_bias, L2_cond_expert_wi, L2_cond_expert_wo, L2_cond_share_wi, L2_cond_share_wo, L2_cond_gate_vecs, L2_cond_gate_w1, L2_cond_gate_w2, L3_cond_W1, L3_cond_b1, L3_cond_v):
    import jax
    import jax.numpy as jnp

    def _L0_cond_ref(hidden_states, language_ids, W1, b1, W2, b2, gamma, beta):
        import jax, jax.numpy as jnp
        import numpy as np
        LN_EPS = 1e-05
        w1 = W1[language_ids]
        w2 = W2[language_ids]
        h = jnp.einsum('bsh,bha->bsa', hidden_states, w1) + b1[language_ids][:, None, :]
        h = jax.nn.relu(h)
        adapted = jnp.einsum('bsa,bah->bsh', h, w2) + b2[language_ids][:, None, :]
        x = hidden_states + adapted
        mean = jnp.mean(x, axis=-1, keepdims=True)
        var = jnp.mean(jnp.square(x - mean), axis=-1, keepdims=True)
        normed = (x - mean) * jax.lax.rsqrt(var + LN_EPS)
        return normed * gamma[language_ids][:, None, :] + beta[language_ids][:, None, :]

    def _L1_cond_ref(x, subject_id, weight, bias):
        import jax, jax.numpy as jnp
        import numpy as np
        S, O, H = (8, 256, 256)
        B, N = (32, 128)
        W = weight[subject_id]
        b = bias[subject_id]
        y = jnp.einsum('bnh,boh->bno', x, W) + b[:, None, :]
        return y

    def _L2_cond_ref(hidden_states, type_idx, expert_wi, expert_wo, share_wi, share_wo, gate_vecs, gate_w1, gate_w2):
        import jax, jax.numpy as jnp
        import numpy as np
        B, S, D, F, E = (8, 256, 256, 1024, 4)

        def _dense(x, wi, wo):
            return jax.nn.relu(x @ wi) @ wo
        s0 = _dense(hidden_states, share_wi[0], share_wo[0])
        s1 = _dense(hidden_states, share_wi[1], share_wo[1])
        s2 = _dense(hidden_states, share_wi[2], share_wo[2])
        idx_a = type_idx
        idx_b = type_idx + 1
        out_a = jnp.einsum('bsf,bfd->bsd', jax.nn.relu(jnp.einsum('bsd,bdf->bsf', hidden_states, expert_wi[idx_a])), expert_wo[idx_a])
        out_b = jnp.einsum('bsf,bfd->bsd', jax.nn.relu(jnp.einsum('bsd,bdf->bsf', hidden_states, expert_wi[idx_b])), expert_wo[idx_b])
        p = jax.nn.softmax(gate_vecs / 0.1, axis=-1)
        wa = p[type_idx, idx_a][:, None, None]
        wb = p[type_idx, idx_b][:, None, None]
        expert_out = out_a * wa + out_b * wb
        gi = jnp.concatenate([expert_out[:, 0], s0[:, 0], s1[:, 0], s2[:, 0]], axis=-1)
        g = jax.nn.softmax(jax.nn.relu(gi @ gate_w1) @ gate_w2, axis=-1)
        out = expert_out * g[:, 0, None, None] + s0 * g[:, 1, None, None] + s1 * g[:, 2, None, None] + s2 * g[:, 3, None, None]
        return out

    def _L3_cond_ref(hidden, W1, b1, v, prompt_type_ids):
        import jax, jax.numpy as jnp
        import numpy as np
        NEG_INF = -1e+30
        B, S, D = hidden.shape
        attn_in = jnp.tanh(jnp.einsum('bsd,da->bsa', hidden, W1) + b1)
        scores = jnp.einsum('bsa,a->bs', attn_in, v)
        idx = jnp.arange(S)
        j = idx[:, None]
        l = idx[None, :]
        prefix_m = l <= j
        postfix_m = l >= j
        cloze_m = l != j
        pt = prompt_type_ids[:, None, None]
        mask = jnp.where(pt == 0, prefix_m[None], jnp.where(pt == 1, postfix_m[None], cloze_m[None]))
        masked_scores = jnp.where(mask, scores[:, None, :], NEG_INF)
        p = jax.nn.softmax(masked_scores, axis=-1)
        cnt = jnp.sum(mask, axis=-1).astype(hidden.dtype)
        pooled = jnp.einsum('bjl,bld->bjd', p, hidden) / cnt[..., None]
        return pooled
    x = x + _L0_cond_ref(x, itok_B_0_8, L0_cond_W1, L0_cond_b1, L0_cond_W2, L0_cond_b2, L0_cond_gamma, L0_cond_beta)
    x = x + _L1_cond_ref(x, itok_B_0_7, L1_cond_weight, L1_cond_bias)
    x = x + _L2_cond_ref(x, itok_B_0_2, L2_cond_expert_wi, L2_cond_expert_wo, L2_cond_share_wi, L2_cond_share_wo, L2_cond_gate_vecs, L2_cond_gate_w1, L2_cond_gate_w2)
    x = x + _L3_cond_ref(x, L3_cond_W1, L3_cond_b1, L3_cond_v, itok_B_0_2)
    return x

_drawn_inputs = setup_inputs


def setup_inputs(seed=0):
    import zlib

    import numpy as np

    out = dict(_drawn_inputs(seed))
    spreads = {'L0_cond_b1': (0.0, 0.267),
     'L0_cond_b2': (0.0, 0.1),
     'L0_cond_gamma': (1.0, 0.2),
     'L0_cond_beta': (0.0, 0.1)}
    factors = {'L1_cond_bias': 3.563,
     'L2_cond_expert_wi': 4.949,
     'L2_cond_expert_wo': 4.105,
     'L2_cond_gate_vecs': 44.819,
     'L2_cond_gate_w1': 8.0,
     'L2_cond_gate_w2': 8.0,
     'L3_cond_W1': 13.357,
     'L3_cond_b1': 64.0,
     'L3_cond_v': 3.926}
    for name, (base, spread) in spreads.items():
        noise = np.random.default_rng([zlib.crc32(name.encode()), seed]).standard_normal(out[name].shape)
        drawn = base * np.exp(spread * noise) if base else spread * noise
        out[name] = jnp.asarray(drawn.astype(out[name].dtype))
    for name, factor in factors.items():
        out[name] = (out[name] * factor).astype(out[name].dtype)
    return out
```

```python
from contextlib import ExitStack

import concourse.bass as bass
from concourse import mybir

ALU = mybir.AluOpType
ACT = mybir.ActivationFunctionType
AX = mybir.AxisListType
F32 = mybir.dt.float32
F32R = mybir.dt.float32r
BF16 = mybir.dt.bfloat16
I32 = mybir.dt.int32

P = 128
NEG = -1e30
LN_EPS = 1e-5
GATE_TEMP = 0.1


class Steps:

    def __init__(self, sem, names):
        self.sem, self.names = sem, names.split()

    def at(self, i, name):
        return i * len(self.names) + (self.names.index(name) + 1)


def cond_resid_program(
    nc, x, lang_id, subj_id, type_id,
    L0_W1, L0_b1, L0_W2, L0_b2, L0_gamma, L0_beta,
    L1_weight, L1_bias,
    L2_expert_wi, L2_expert_wo, L2_share_wi, L2_share_wo, L2_gate_vecs, L2_gate_w1, L2_gate_w2,
    L3_W1, L3_b1, L3_v, out,
):
    B, S, D = x.shape
    KD = D // P
    R = S // P
    A = L0_W1.shape[2]
    F = L2_share_wi.shape[2]
    CH = F // P
    NETS = 2 + L2_share_wi.shape[0]
    NG = NETS - 1
    SLOTS = NETS * CH
    PAIRS = SLOTS // 2
    RING = 4
    AHEAD = RING - 1
    HALVES = 2 * NETS
    HP = CH // 4
    NT = L2_gate_vecs.shape[0]
    NE = L2_gate_vecs.shape[1]
    assert PAIRS % RING == 0 and HALVES % 2 == 0 and HP == 2

    with ExitStack() as ctx:
        def sb(name, shape, dt=F32):
            return ctx.enter_context(nc.sbuf_tensor(name, shape, dt))

        def psum(name, shape):
            return ctx.enter_context(nc.psum_tensor(name, shape, F32))

        def sem(name):
            return ctx.enter_context(nc.semaphore(name))

        ident = sb("ident", [P, P])
        ones = sb("ones", [P, P])
        rel_sign = sb("rel_sign", [P, R, S], BF16)
        jcol_i = sb("jcol_i", [P, R], I32)
        jcol = sb("jcol", [P, 2, R])
        half_pow = sb("half_pow", [P, R])
        ids = sb("ids", [1, 2, B], I32)
        type_bc_i = sb("type_bc_i", [P, B], I32)
        type_bc = sb("type_bc", [P, B])
        gate_vecs = sb("gate_vecs", [P, NT * NE])
        gate_prob = sb("gate_prob", [P, NT * NE])
        gv_max = sb("gv_max", [P, NT])
        gv_sum = sb("gv_sum", [P, NT])
        onehot = sb("onehot", [P, B, NT])
        pick = sb("pick", [P, B, NT])
        NPAR = 6 + R
        par = sb("par", [P, B * NPAR])
        par_l2 = sb("par_l2", [P, NPAR])
        par_l3 = sb("par_l3", [P, NPAR])
        gate_w1 = sb("gate_w1", [P, NG * KD, D])
        gate_w2 = sb("gate_w2", [P, KD, NG])
        att_w = sb("att_w", [P, KD, A])
        att_w_hi = sb("att_w_hi", [P, KD, A], F32R)
        att_w_lo = sb("att_w_lo", [P, KD, A], F32R)
        att_b = sb("att_b", [A, 1])
        att_v = sb("att_v", [A, 1])
        att_v_bc = sb("att_v_bc", [A, P])

        x_rows = sb("x_rows", [P, R, D])
        w1 = sb("w1", [P, KD, A])
        w1_hi = sb("w1_hi", [P, KD, A], F32R)
        w1_lo = sb("w1_lo", [P, KD, A], F32R)
        w2 = sb("w2", [A, D])
        w2_hi = sb("w2_hi", [A, D], F32R)
        w2_lo = sb("w2_lo", [A, D], F32R)
        b1 = sb("b1", [A, 1])
        b2_bc = sb("b2_bc", [P, D])
        gamma = sb("gamma", [P, KD])
        beta = sb("beta", [P, KD])
        subj_w = sb("subj_w", [P, KD, D])
        subj_wT_hi = sb("subj_wT_hi", [P, KD, D], F32R)
        subj_wT_lo = sb("subj_wT_lo", [P, KD, D], F32R)
        subj_b = sb("subj_b", [P, KD])
        xb_rows = sb("xb_rows", [P, R, D])
        xbT = sb("xbT", [P, KD, S])
        hT = sb("hT", [A, S])
        hT_hi = sb("hT_hi", [A, S], F32R)
        hT_lo = sb("hT_lo", [A, S], F32R)
        norm = sb("norm", [P, R, D])
        stats = sb("stats", [P, R, 6])
        mean = sb("mean", [P, R])
        mean_gap = sb("mean_gap", [P, R])
        var_eps = sb("var_eps", [P, R])
        rstd = sb("rstd", [P, R])
        x1T = sb("x1T", [P, KD, S])
        next_x2T = sb("next_x2T", [P, KD, S])
        opT_hi = sb("opT_hi", [P, KD, S], F32R)
        opT_lo = sb("opT_lo", [P, KD, S], F32R)

        x2T_hi = sb("x2T_hi", [P, KD, S], F32R)
        x2T_lo = sb("x2T_lo", [P, KD, S], F32R)
        raw_wi = sb("raw_wi", [P, 2, KD, F // 2])
        raw_wo = sb("raw_wo", [P, 2, CH // 2, D])
        wi_hi = sb("wi_hi", [P, RING, KD, 2 * P], F32R)
        wi_lo = sb("wi_lo", [P, RING, KD, 2 * P], F32R)
        wo_hi = sb("wo_hi", [P, RING, 2, D], F32R)
        wo_lo = sb("wo_lo", [P, RING, 2, D], F32R)
        hid_hi = sb("hid_hi", [P, 2, S], F32R)
        hid_lo = sb("hid_lo", [P, 2, S], F32R)
        netT = sb("netT", [P, NG, KD, S])

        x3T = sb("x3T", [P, KD, S])
        gate_h = sb("gate_h", [P, KD, P])
        neg_gmax = sb("neg_gmax", [P, 1])
        gate_e = sb("gate_e", [P, NG])
        gate_sum = sb("gate_sum", [P, 1])
        gate_rec = sb("gate_rec", [P, 1])
        gates = sb("gates", [P, NG])
        attT = sb("attT", [A, S])
        score_row = sb("score_row", [P, S])
        score_col = sb("score_col", [P, R])
        prefix_max = sb("prefix_max", [P, S + 1])
        suffix_max = sb("suffix_max", [P, S + 1])
        max_row = sb("max_row", [P, S])
        x3_rows = sb("x3_rows", [P, R, D])
        VW = D + 2
        val_hi = sb("val_hi", [P, R, VW], F32R)
        val_lo = sb("val_lo", [P, R, VW], F32R)
        mask = sb("mask", [P, R, S], BF16)
        prob = sb("prob", [P, R, S])
        prob_hi = sb("prob_hi", [P, R, S], F32R)
        prob_lo = sb("prob_lo", [P, R, S], F32R)
        den = sb("den", [P, R])
        rden = sb("rden", [P, R])
        out_rows = sb("out_rows", [P, R, D])

        ps_hid = psum("ps_hid", [P, 2, S])
        ps_net = psum("ps_net", [P, 2, KD, S])
        ps_side = psum("ps_side", [P, 2, S])

        ids_in, small_in, gate_in = sem("ids_in"), sem("small_in"), sem("gate_in")
        x_in, a_in, out_stored = sem("x_in"), sem("a_in"), sem("out_stored")
        raw_in = [sem("raw_in0"), sem("raw_in1")]
        const_ready, const_step, rel_ready, att_w_ready = (
            sem("const_ready"), sem("const_step"), sem("rel_ready"), sem("att_w_ready"))
        par_step, par_exp_done, par_l2_ready = sem("par_step"), sem("par_exp_done"), sem("par_l2_ready")
        x2_hi_ready, x2_lo_ready = sem("x2_hi_ready"), sem("x2_lo_ready")
        w_hi_ready, w_lo_ready = sem("w_hi_ready"), sem("w_lo_ready")
        hid_done, hid_hi_ready, hid_lo_ready = sem("hid_done"), sem("hid_hi_ready"), sem("hid_lo_ready")
        net_chunk_done = sem("net_chunk_done")
        evac_act, evac_dve, base_ready = sem("evac_act"), sem("evac_dve"), sem("base_ready")

        a_pe = Steps(sem("a_pe"), "xT0 xT1 subj_wT hid adapt0 adapt1 normT0 normT1 y0 y1")
        a_act = Steps(sem("a_act"), "xhi0 xb0 xhi1 xb1 subj_w_hi hid x1hi0 x1hi1")
        a_dve = Steps(sem("a_dve"), "w1_hi w2_hi xlo0 xlo1 subj_w_lo hid_hi hid_lo sum0 sum1 stats sums mean var_eps "
                                    "norm x1T0 x1T1 x1lo0 x1lo1 x2T0 x2T1")
        a_pool = Steps(sem("a_pool"), "w1_lo w2_lo xb rstd")
        c_pe = Steps(sem("c_pe"), "gate_h logits att score_row score_col rows0 rows1 out0 out1 out2 out3")
        c_act = Steps(sem("c_act"), "gate_exp x3hi0 x3hi1 att score_col rows0 rows1 exp0 exp1 exp2 exp3")
        c_dve = Steps(sem("c_dve"), "par mask gate_h gate_max gate_rec gates comb0 comb1 comb2 comb3 x3lo0 x3lo1 "
                                    "score_row prefix suffix max0 max1 max2 max3 "
                                    "arg0 arg1 arg2 arg3 val_hi val_lo phi0 phi1 phi2 phi3 "
                                    "den0 rden0 out0 den1 rden1 out1 den2 rden2 out2 den3 rden3 out3")
        c_pool = Steps(sem("c_pool"), "plo0 plo1 plo2 plo3")

        block = ctx.enter_context(nc.Block())

        def f32(ap):
            return ap.bitcast(F32)

        @block.sync
        def _(sp):
            def load_x(i):
                sp.dma_start(x_rows[:], x[bass.ds(i, 1)].rearrange("o (r p) d -> p (o r) d", p=P)).then_inc(x_in, 16)

            def load_params(i):
                lang = sp.value_load(ids[0:1, 0, bass.ds(i, 1)], min_val=0, max_val=L0_W1.shape[0] - 1)
                subj = sp.value_load(ids[0:1, 1, bass.ds(i, 1)], min_val=0, max_val=L1_weight.shape[0] - 1)
                la, su = bass.ds(lang, 1), bass.ds(subj, 1)
                sp.dma_start(w1[:], L0_W1[la].rearrange("o (k p) a -> p (o k) a", p=P)).then_inc(a_in, 16)
                sp.dma_start(w2[:], L0_W2[la].rearrange("o a d -> (o a) d")).then_inc(a_in, 16)
                sp.dma_start(subj_w[:], L1_weight[su].rearrange("o (k p) d -> p (o k) d", p=P)).then_inc(a_in, 16)
                sp.dma_start(b2_bc[:], L0_b2[la].to_broadcast([P, D])).then_inc(a_in, 16)
                with nc.allow_non_contiguous_dma(reason="a few vectors, one element to a partition"):
                    sp.dma_start(b1[:], L0_b1[la].rearrange("o a -> a o")).then_inc(a_in, 16)
                    sp.dma_start(gamma[:], L0_gamma[la].rearrange("o (k p) -> p (o k)", p=P)).then_inc(a_in, 16)
                    sp.dma_start(beta[:], L0_beta[la].rearrange("o (k p) -> p (o k)", p=P)).then_inc(a_in, 16)
                    sp.dma_start(subj_b[:], L1_bias[su].rearrange("o (k p) -> p (o k)", p=P)).then_inc(a_in, 16)

            def load_half(b, h, kind):
                slot, net, part = h % 2, h // 2, h % 2
                if not (isinstance(b, int) and b == 0 and h < 2):
                    sp.wait_ge(w_lo_ready, b * PAIRS + HP * (h - 1))
                cols = slice(part * (F // 2), (part + 1) * (F // 2))
                if net < 2:
                    e = bass.ds(kind + net, 1)
                    wi, wo = L2_expert_wi[e, :, cols], L2_expert_wo[e, cols]
                else:
                    wi, wo = L2_share_wi[net - 2:net - 1, :, cols], L2_share_wo[net - 2:net - 1, cols]
                sp.dma_start(raw_wi[:, slot], wi.rearrange("o (k p) f -> p (o k) f", p=P)).then_inc(raw_in[slot], 16)
                sp.dma_start(raw_wo[:, slot], wo.rearrange("o (c p) d -> p (o c) d", p=P)).then_inc(raw_in[slot], 16)

            def store(i):
                sp.wait_ge(c_dve.sem, c_dve.at(i, "out3"))
                sp.dma_start(out[bass.ds(i, 1)].rearrange("o (r p) d -> p (o r) d", p=P), out_rows[:]).then_inc(out_stored, 16)

            def batch(b, first, last):
                kind = sp.value_load(type_bc_i[0:1, bass.ds(b, 1)], min_val=0, max_val=NT - 1)
                for h in range(HALVES):
                    load_half(b, h, kind)
                    if h == 4 and not last:
                        sp.wait_ge(a_dve.sem, a_dve.at(b, "x2T1"))
                        load_x(b + 1)
                        load_params(b + 1)
                    if h == 7 and not first:
                        store(b - 1)

            load_x(0)
            sp.dma_start(ids[:, 0], lang_id.rearrange("(o b) -> o b", o=1)).then_inc(ids_in, 16)
            sp.dma_start(ids[:, 1], subj_id.rearrange("(o b) -> o b", o=1)).then_inc(ids_in, 16)
            sp.dma_start(type_bc_i[:], type_id.rearrange("(o b) -> o b", o=1).to_broadcast([P, B])).then_inc(ids_in, 16)
            sp.wait_ge(ids_in, 48)
            load_params(0)
            batch(0, True, False)
            with sp.Fori(1, B - 1) as b:
                batch(b, False, False)
            batch(B - 1, False, True)
            store(B - 1)
            sp.wait_ge(out_stored, 16 * B)

        @block.tensor
        def _(pe):
            mm = nc.tensor.matmul

            def product(dst, pairs, n_last=None):
                n = len(pairs)
                for t, (lh, ll, rh, rl) in enumerate(pairs):
                    mm(dst, lh, rh, start=(t == 0), stop=False)
                    mm(dst, lh, rl, start=False, stop=False)
                    last = mm(dst, ll, rh, start=False, stop=(t == n - 1))
                return last

            def stage_a(slot, i, after_c):
                if slot in (19, 20):
                    k = slot - 19
                    if k == 0:
                        pe.wait_ge(x_in, 16 * (i + 1))
                        pe.wait_ge(const_ready, 2)
                    if after_c:
                        pe.wait_ge(c_dve.sem, c_dve.at(i - 2, "out3"))
                    for r in range(R):
                        last = nc.tensor.transpose(ps_side[:, k, r * P:(r + 1) * P], x_rows[:, r, k * P:(k + 1) * P], ident[:])
                    last.then_inc(a_pe.sem, 1)
                if slot == 21:
                    pe.wait_ge(a_in, 128 * (i + 1))
                    pe.wait_ge(a_act.sem, a_act.at(i, "xb0"))
                    pe.wait_ge(a_dve.sem, a_dve.at(i, "xlo0"))
                    for k in range(KD):
                        for o in range(KD):
                            c = k * D + o * P
                            last = nc.tensor.transpose(ps_side[:, 0, c:c + P], subj_w[:, o, k * P:(k + 1) * P], ident[:])
                    last.then_inc(a_pe.sem, 1)
                if slot == 22:
                    pe.wait_ge(a_act.sem, a_act.at(i, "xb1"))
                    pe.wait_ge(a_dve.sem, a_dve.at(i, "xlo1"))
                    pe.wait_ge(a_pool.sem, a_pool.at(i, "w2_lo"))
                    product(ps_side[0:A, 1], [(w1_hi[:, k], w1_lo[:, k], opT_hi[:, k], opT_lo[:, k])
                                              for k in range(KD)]).then_inc(a_pe.sem, 1)
                if slot == 23:
                    for t in range(2):
                        if t == 0:
                            pe.wait_ge(a_dve.sem, a_dve.at(i, "subj_w_lo"))
                            pe.wait_ge(a_dve.sem, a_dve.at(i, "hid_lo"))
                        for r in (2 * t, 2 * t + 1):
                            c = slice((r % 2) * D, (r % 2 + 1) * D)
                            rows = slice(r * P, (r + 1) * P)
                            last = product(ps_side[:, t, c], [(hT_hi[:, rows], hT_lo[:, rows], w2_hi[:], w2_lo[:])])
                        last.then_inc(a_pe.sem, 1)
                if slot in (26, 27):
                    k = slot - 26
                    pe.wait_ge(a_dve.sem, a_dve.at(i, "norm"))
                    for r in range(R):
                        last = nc.tensor.transpose(ps_side[:, k, r * P:(r + 1) * P], norm[:, r, k * P:(k + 1) * P], ident[:])
                    last.then_inc(a_pe.sem, 1)
                if slot in (29, 30):
                    o = slot - 29
                    pe.wait_ge(a_dve.sem, a_dve.at(i, "x1lo1"))
                    product(ps_side[:, o], [(subj_wT_hi[:, k, o * P:(o + 1) * P], subj_wT_lo[:, k, o * P:(o + 1) * P],
                                             opT_hi[:, k], opT_lo[:, k]) for k in range(KD)]).then_inc(a_pe.sem, 1)

            def stage_c(slot, i):
                if slot == 1:
                    pe.wait_ge(evac_act, NG * (i + 1))
                    pe.wait_ge(evac_dve, NG * (i + 1))
                    pe.wait_ge(gate_in, 32)
                    for o in range(KD):
                        for c in range(NG * KD):
                            last = mm(ps_side[:, 0, o:o + 1], gate_w1[:, c, o * P:(o + 1) * P],
                                      netT[:, c // KD, c % KD, 0:1], start=(c == 0), stop=(c == NG * KD - 1))
                    last.then_inc(c_pe.sem, 1)
                if slot == 2:
                    pe.wait_ge(c_dve.sem, c_dve.at(i, "gate_h"))
                    for o in range(KD):
                        last = mm(ps_side[:, 1, 0:NG], gate_h[:, o], gate_w2[:, o], start=(o == 0), stop=(o == KD - 1))
                    last.then_inc(c_pe.sem, 1)
                if slot == 6:
                    pe.wait_ge(att_w_ready, 2)
                    pe.wait_ge(c_act.sem, c_act.at(i, "x3hi1"))
                    pe.wait_ge(c_dve.sem, c_dve.at(i, "x3lo1"))
                    product(ps_side[0:A, 0], [(att_w_hi[:, k], att_w_lo[:, k], opT_hi[:, k], opT_lo[:, k])
                                              for k in range(KD)]).then_inc(c_pe.sem, 1)
                if slot == 7:
                    pe.wait_ge(c_act.sem, c_act.at(i, "att"))
                    mm(ps_side[:, 1], att_v_bc[:], attT[:], start=True, stop=True).then_inc(c_pe.sem, 1)
                    for r in range(R):
                        last = mm(ps_side[:, 0, r:r + 1], attT[:, r * P:(r + 1) * P], att_v[:], start=True, stop=True)
                    last.then_inc(c_pe.sem, 1)
                if slot in (8, 9):
                    t = slot - 8
                    bank = 1 - t
                    if t == 0:
                        pe.wait_ge(c_dve.sem, c_dve.at(i, "score_row"))
                    else:
                        pe.wait_ge(c_act.sem, c_act.at(i, "score_col"))
                    for r in (2 * t, 2 * t + 1):
                        for k in range(KD):
                            c = (r % 2) * D + k * P
                            last = nc.tensor.transpose(ps_side[:, bank, c:c + P], x3T[:, k, r * P:(r + 1) * P], ident[:])
                    last.then_inc(c_pe.sem, 1)
                if slot in (17, 18):
                    for t in (2 * (slot - 17), 2 * (slot - 17) + 1):
                        if t == 0:
                            pe.wait_ge(c_act.sem, c_act.at(i, "rows1"))
                            pe.wait_ge(c_pool.sem, c_pool.at(i, "plo3"))
                        if t >= 2:
                            pe.wait_ge(c_dve.sem, c_dve.at(i, f"out{t - 2}"))
                        cols = slice(t * P, (t + 1) * P)
                        product(ps_side[:, t % 2, 0:VW],
                                [(prob_hi[:, l, cols], prob_lo[:, l, cols], val_hi[:, l], val_lo[:, l])
                                 for l in range(R)]).then_inc(c_pe.sem, 1)

            def first_product(b, q, first):
                if q == 0:
                    pe.wait_ge(x2_hi_ready, KD * (b + 1))
                    pe.wait_ge(x2_lo_ready, KD * (b + 1))
                if q % 2 == 0:
                    pe.wait_ge(w_lo_ready, b * PAIRS + q // 2 + 1)
                if not (first and q < 2):
                    pe.wait_ge(hid_lo_ready, b * SLOTS + q - 1)
                w, c = (q // 2) % RING, slice((q % 2) * P, (q % 2 + 1) * P)
                product(ps_hid[:, q % 2], [(wi_hi[:, w, k, c], wi_lo[:, w, k, c], x2T_hi[:, k], x2T_lo[:, k])
                                           for k in range(KD)]).then_inc(hid_done, 1)

            def second_product(b, q, first):
                net, c = q // CH, q % CH
                if c == 0:
                    if net == 0 and not first:
                        pe.wait_ge(evac_act, NG * b)
                        pe.wait_ge(evac_dve, NG * b)
                    if net == 2:
                        pe.wait_ge(evac_act, NG * b + 1)
                    if net >= 3:
                        pe.wait_ge(evac_act, NG * b + net - 2)
                        pe.wait_ge(evac_dve, NG * b + net - 2)
                pe.wait_ge(hid_hi_ready, b * SLOTS + q + 1)
                w = (q // 2) % RING
                for k in range(KD):
                    cols = slice(k * P, (k + 1) * P)
                    mm(ps_net[:, net % 2, k], wo_hi[:, w, q % 2, cols], hid_hi[:, q % 2], start=(c == 0), stop=False)
                    mm(ps_net[:, net % 2, k], wo_lo[:, w, q % 2, cols], hid_hi[:, q % 2], start=False, stop=False)
                pe.wait_ge(hid_lo_ready, b * SLOTS + q + 1)
                for k in range(KD):
                    cols = slice(k * P, (k + 1) * P)
                    last = mm(ps_net[:, net % 2, k], wo_hi[:, w, q % 2, cols], hid_lo[:, q % 2], start=False, stop=(c == CH - 1))
                last.then_inc(net_chunk_done, 1)

            def batch(b, first, last):
                for q in range(SLOTS):
                    first_product(b, q, first)
                    if not first:
                        stage_c(q, b - 1)
                    if not last:
                        stage_a(q, b + 1, not first)
                    if q >= 1:
                        second_product(b, q - 1, first)
                second_product(b, SLOTS - 1, first)

            for q in range(SLOTS):
                stage_a(q, 0, False)
            batch(0, True, False)
            with pe.Fori(1, B - 1) as b:
                batch(b, False, False)
            batch(B - 1, False, True)
            for q in range(SLOTS):
                stage_c(q, B - 1)

        @block.scalar
        def _(act):
            fn = nc.scalar.activation

            def stage_a(slot, i, after_c):
                if slot in (19, 20):
                    k = slot - 19
                    act.wait_ge(a_pe.sem, a_pe.at(i, f"xT{k}"))
                    if after_c:
                        act.wait_ge(c_pe.sem, c_pe.at(i - 2, "att"))
                    fn(opT_hi[:, k], ps_side[:, k], ACT.Copy).then_inc(a_act.sem, 1)
                    if k == 0:
                        act.wait_ge(a_in, 128 * (i + 1))
                    fn(xbT[:, k], ps_side[:, k], ACT.Identity, bias=beta[:, k:k + 1]).then_inc(a_act.sem, 1)
                if slot == 21:
                    act.wait_ge(a_pe.sem, a_pe.at(i, "subj_wT"))
                    fn(subj_wT_hi[:].rearrange("p k d -> p (k d)"), ps_side[:, 0], ACT.Copy).then_inc(a_act.sem, 1)
                if slot == 22:
                    act.wait_ge(a_pe.sem, a_pe.at(i, "hid"))
                    fn(hT[:], ps_side[0:A, 1], ACT.Relu, bias=b1[:]).then_inc(a_act.sem, 1)
                if slot in (27, 28):
                    k = slot - 27
                    act.wait_ge(a_dve.sem, a_dve.at(i, f"x1T{k}"))
                    fn(opT_hi[:, k], x1T[:, k], ACT.Copy).then_inc(a_act.sem, 1)

            def stage_c(slot, i):
                if slot == 2:
                    act.wait_ge(c_dve.sem, c_dve.at(i, "gate_max"))
                    fn(gate_e[:], ps_side[:, 1, 0:NG], ACT.Exp, bias=neg_gmax[:], accum_out=gate_sum[:]).then_inc(c_act.sem, 1)
                if slot == 5:
                    for k in range(KD):
                        act.wait_ge(c_dve.sem, c_dve.at(i, "comb3"))
                        fn(opT_hi[:, k], x3T[:, k], ACT.Copy).then_inc(c_act.sem, 1)
                if slot == 6:
                    act.wait_ge(c_pe.sem, c_pe.at(i, "att"))
                    fn(attT[:], ps_side[0:A, 0], ACT.Tanh, bias=att_b[:]).then_inc(c_act.sem, 1)
                if slot == 7:
                    act.wait_ge(c_pe.sem, c_pe.at(i, "score_col"))
                    fn(score_col[:], ps_side[:, 0, 0:R], ACT.Copy).then_inc(c_act.sem, 1)
                if slot in (8, 9):
                    t = slot - 8
                    act.wait_ge(c_pe.sem, c_pe.at(i, f"rows{t}"))
                    fn(x3_rows[:, 2 * t:2 * t + 2].rearrange("p r d -> p (r d)"), ps_side[:, 1 - t], ACT.Copy).then_inc(c_act.sem, 1)
                if 12 <= slot < 12 + R:
                    l = slot - 12
                    act.wait_ge(c_dve.sem, c_dve.at(i, f"arg{l}"))
                    act.wait_ge(c_act.sem, c_act.at(i, "score_col"))
                    fn(prob[:, l], prob[:, l], ACT.Exp, bias=score_col[:, l:l + 1]).then_inc(c_act.sem, 1)

            def split_weights(b, p, free):
                w, half = p % RING, p // HP
                act.wait_ge(raw_in[half % 2], 32 * ((HALVES // 2) * b + half // 2 + 1))
                if free:
                    act.wait_ge(net_chunk_done, b * SLOTS + 2 * (p - RING) + 2)
                c = slice((p % HP) * 2 * P, (p % HP + 1) * 2 * P)
                fn(wi_hi[:, w], raw_wi[:, half % 2, :, c], ACT.Copy)
                fn(wo_hi[:, w], raw_wo[:, half % 2, 2 * (p % HP):2 * (p % HP) + 2], ACT.Copy).then_inc(w_hi_ready, 1)

            def split_x2(b):
                for k in range(KD):
                    act.wait_ge(a_dve.sem, a_dve.at(b, f"x2T{k}"))
                    fn(x2T_hi[:, k], next_x2T[:, k], ACT.Copy).then_inc(x2_hi_ready, 1)

            def evacuate(b, net):
                act.wait_ge(net_chunk_done, b * SLOTS + (net + 1) * CH)
                if net == 0:
                    act.wait_ge(par_l2_ready, b + 1)
                    if not (isinstance(b, int) and b == 0):
                        act.wait_ge(c_dve.sem, c_dve.at(b - 1, "comb3"))
                    for k in range(KD):
                        last = fn(netT[:, 0, k], ps_net[:, 0, k], ACT.Copy, scale=par_l2[:, 0:1])
                    last.then_inc(evac_act, 1)
                if net >= 2:
                    fn(netT[:, net - 1, 0], ps_net[:, net % 2, 0], ACT.Copy).then_inc(evac_act, 1)

            def batch(b, first, last):
                for q in range(SLOTS):
                    act.wait_ge(hid_done, b * SLOTS + q + 1)
                    if not (first and q < 2):
                        act.wait_ge(net_chunk_done, b * SLOTS + q - 1)
                    fn(hid_hi[:, q % 2], ps_hid[:, q % 2], ACT.Relu).then_inc(hid_hi_ready, 1)
                    if q % 2 == 1:
                        p = q // 2 + AHEAD
                        if p < PAIRS:
                            split_weights(b, p, not (first and p < RING))
                        elif not last:
                            split_weights(b + 1, p - PAIRS, True)
                    if not first:
                        stage_c(q, b - 1)
                    if not last:
                        stage_a(q, b + 1, not first)
                    if q % CH == 0 and q >= CH:
                        evacuate(b, q // CH - 1)
                if not last:
                    act.wait_ge(base_ready, b + 1)
                    split_x2(b + 1)
                evacuate(b, NETS - 1)

            act.dma_start(gate_vecs[:], L2_gate_vecs.rearrange("(o t) e -> o (t e)", o=1).to_broadcast([P, NT * NE])).then_inc(small_in, 16)
            with nc.allow_non_contiguous_dma(reason="two vectors, one element to a partition"):
                act.dma_start(att_b[:], L3_b1.rearrange("(a o) -> a o", o=1)).then_inc(small_in, 16)
                act.dma_start(att_v[:], L3_v.rearrange("(a o) -> a o", o=1)).then_inc(small_in, 16)
            act.dma_start(att_w[:], L3_W1.rearrange("(k p) a -> p k a", p=P)).then_inc(small_in, 16)
            act.dma_start(gate_w2[:], L2_gate_w2.rearrange("(k p) g -> p k g", p=P)).then_inc(gate_in, 16)
            act.dma_start(gate_w1[:], L2_gate_w1.rearrange("(c p) d -> p c d", p=P)).then_inc(gate_in, 16)
            for q in range(SLOTS):
                stage_a(q, 0, False)
                if q in (21, 23, 25):
                    split_weights(0, (q - 21) // 2, False)
            split_x2(0)
            act.wait_ge(par_step, 2)
            fn(gate_prob[:], gate_prob[:], ACT.Exp, scale=1.0 / GATE_TEMP).then_inc(par_exp_done, 1)
            batch(0, True, False)
            with act.Fori(1, B - 1) as b:
                batch(b, False, False)
            batch(B - 1, False, True)
            for q in range(SLOTS):
                stage_c(q, B - 1)

        @block.vector
        def _(dve):
            v = nc.vector

            def stage_a(slot, i):
                def here(name):
                    dve.wait_ge(a_dve.sem, a_dve.at(i, name))

                if slot == 19:
                    dve.wait_ge(a_in, 128 * (i + 1))
                    v.tensor_copy(w1_hi[:], w1[:]).then_inc(a_dve.sem, 1)
                    v.tensor_copy(w2_hi[:], w2[:]).then_inc(a_dve.sem, 1)
                if slot in (19, 20):
                    k = slot - 19
                    dve.wait_ge(a_act.sem, a_act.at(i, f"xb{k}"))
                    v.tensor_tensor(opT_lo[:, k], ps_side[:, k], f32(opT_hi[:, k]), ALU.subtract).then_inc(a_dve.sem, 1)
                if slot == 21:
                    dve.wait_ge(a_act.sem, a_act.at(i, "subj_w_hi"))
                    v.tensor_tensor(subj_wT_lo[:].rearrange("p k d -> p (k d)"), ps_side[:, 0],
                                    f32(subj_wT_hi[:].rearrange("p k d -> p (k d)")), ALU.subtract).then_inc(a_dve.sem, 1)
                if slot == 22:
                    dve.wait_ge(a_act.sem, a_act.at(i, "hid"))
                    v.tensor_copy(hT_hi[:], hT[:]).then_inc(a_dve.sem, 1)
                    here("hid_hi")
                    v.tensor_tensor(hT_lo[:], hT[:], f32(hT_hi[:]), ALU.subtract).then_inc(a_dve.sem, 1)
                if slot == 23:
                    for t in range(2):
                        dve.wait_ge(a_pe.sem, a_pe.at(i, f"adapt{t}"))
                        if t == 0:
                            dve.wait_ge(a_pool.sem, a_pool.at(i, "xb"))
                        rows = slice(2 * t, 2 * t + 2)
                        v.tensor_tensor(norm[:, rows].rearrange("p r d -> p (r d)"), ps_side[:, t],
                                        xb_rows[:, rows].rearrange("p r d -> p (r d)"), ALU.add).then_inc(a_dve.sem, 1)
                if slot == 24:
                    here("sum1")
                    for r in range(R):
                        last = v.bn_stats(stats[:, r], norm[:, r])
                    last.then_inc(a_dve.sem, 1)
                    here("stats")
                    v.tensor_tensor(mean[:], stats[:, :, 1], stats[:, :, 4], ALU.add)
                    v.tensor_tensor(mean_gap[:], stats[:, :, 1], stats[:, :, 4], ALU.subtract)
                    v.tensor_tensor(var_eps[:], stats[:, :, 2], stats[:, :, 5], ALU.add).then_inc(a_dve.sem, 1)
                    here("sums")
                    v.tensor_scalar(mean[:], mean[:], 0.5, None, ALU.mult)
                    v.scalar_tensor_tensor(out=mean_gap[:], in0=mean_gap[:], scalar=0.25, in1=mean_gap[:], op0=ALU.mult, op1=ALU.mult)
                    v.tensor_scalar(var_eps[:], var_eps[:], 1.0 / D, LN_EPS, ALU.mult, ALU.add).then_inc(a_dve.sem, 1)
                    here("mean")
                    v.tensor_tensor(var_eps[:], var_eps[:], mean_gap[:], ALU.add).then_inc(a_dve.sem, 1)
                if slot == 25:
                    dve.wait_ge(a_pool.sem, a_pool.at(i, "rstd"))
                    for r in range(R):
                        last = v.tensor_scalar(norm[:, r], norm[:, r], mean[:, r:r + 1], rstd[:, r:r + 1], ALU.subtract, ALU.mult)
                    last.then_inc(a_dve.sem, 1)
                if slot in (26, 27):
                    k = slot - 26
                    dve.wait_ge(a_pe.sem, a_pe.at(i, f"normT{k}"))
                    dve.wait_ge(a_act.sem, a_act.at(i, f"xb{k}"))
                    v.scalar_tensor_tensor(out=x1T[:, k], in0=ps_side[:, k], scalar=gamma[:, k:k + 1], in1=xbT[:, k],
                                           op0=ALU.mult, op1=ALU.add).then_inc(a_dve.sem, 1)
                if slot == 28:
                    here("x1T1")
                    for k in range(KD):
                        dve.wait_ge(a_act.sem, a_act.at(i, f"x1hi{k}"))
                        v.tensor_tensor(opT_lo[:, k], x1T[:, k], f32(opT_hi[:, k]), ALU.subtract).then_inc(a_dve.sem, 1)
                if slot in (29, 30):
                    k = slot - 29
                    dve.wait_ge(a_pe.sem, a_pe.at(i, f"y{k}"))
                    v.scalar_tensor_tensor(out=next_x2T[:, k], in0=ps_side[:, k], scalar=subj_b[:, k:k + 1], in1=x1T[:, k],
                                           op0=ALU.add, op1=ALU.add).then_inc(a_dve.sem, 1)

            def stage_c(slot, i):
                def here(name):
                    dve.wait_ge(c_dve.sem, c_dve.at(i, name))

                if slot == 1:
                    v.tensor_copy(par_l3[:], par[:, bass.ds(i * NPAR, NPAR)]).then_inc(c_dve.sem, 1)
                    here("par")
                    dve.wait_ge(rel_ready, 1)
                    v.tensor_scalar(mask[:], rel_sign[:], par_l3[:, 2:3], NEG, ALU.is_equal, ALU.mult).then_inc(c_dve.sem, 1)
                    dve.wait_ge(c_pe.sem, c_pe.at(i, "gate_h"))
                    for o in range(KD):
                        last = v.tensor_scalar(gate_h[:, o], ones[:], ps_side[:, 0, o:o + 1], 0.0, ALU.mult, ALU.max)
                    last.then_inc(c_dve.sem, 1)
                if slot == 2:
                    dve.wait_ge(c_pe.sem, c_pe.at(i, "logits"))
                    v.tensor_reduce(neg_gmax[:], ps_side[:, 1, 0:NG], AX.X, ALU.max, negate=True).then_inc(c_dve.sem, 1)
                if slot == 3:
                    dve.wait_ge(c_act.sem, c_act.at(i, "gate_exp"))
                    v.reciprocal(gate_rec[:], gate_sum[:]).then_inc(c_dve.sem, 1)
                    here("gate_rec")
                    v.tensor_scalar(gates[:], gate_e[:], gate_rec[:, 0:1], None, ALU.mult).then_inc(c_dve.sem, 1)
                    here("gates")
                    dve.wait_ge(base_ready, i + 1)
                if slot in (3, 4):
                    for n in (2 * (slot - 3), 2 * (slot - 3) + 1):
                        if n > 0:
                            here(f"comb{n - 1}")
                        v.scalar_tensor_tensor(out=x3T[:].rearrange("p k s -> p (k s)"), in0=netT[:, n].rearrange("p k s -> p (k s)"),
                                               scalar=gates[:, n:n + 1], in1=x3T[:].rearrange("p k s -> p (k s)"),
                                               op0=ALU.mult, op1=ALU.add).then_inc(c_dve.sem, 1)
                if slot == 5:
                    for k in range(KD):
                        dve.wait_ge(c_act.sem, c_act.at(i, f"x3hi{k}"))
                        here("comb3")
                        v.tensor_tensor(opT_lo[:, k], x3T[:, k], f32(opT_hi[:, k]), ALU.subtract).then_inc(c_dve.sem, 1)
                if slot == 7:
                    dve.wait_ge(c_pe.sem, c_pe.at(i, "score_row"))
                    v.tensor_copy(score_row[:], ps_side[:, 1]).then_inc(c_dve.sem, 1)
                if slot == 8:
                    here("score_row")
                    v.tensor_tensor_scan(prefix_max[:, 1:S + 1], score_row[:], score_row[:], NEG, ALU.max, ALU.max).then_inc(c_dve.sem, 1)
                if slot == 9:
                    back = score_row[:, ::-1]
                    v.tensor_tensor_scan(suffix_max[:, S - 1::-1], back, back, NEG, ALU.max, ALU.max).then_inc(c_dve.sem, 1)
                if slot == 10:
                    here("suffix")
                    v.tensor_scalar(max_row[:], prefix_max[:, 1:S + 1], par_l3[:, 3:4], None, ALU.add).then_inc(c_dve.sem, 1)
                    for n, (side, c) in enumerate([(prefix_max[:, 0:S], 5), (suffix_max[:, 0:S], 4), (suffix_max[:, 1:S + 1], 5)]):
                        here(f"max{n}")
                        v.scalar_tensor_tensor(out=max_row[:], in0=side, scalar=par_l3[:, c:c + 1], in1=max_row[:],
                                               op0=ALU.add, op1=ALU.max).then_inc(c_dve.sem, 1)
                if slot == 11:
                    here("max3")
                    for l in range(R):
                        v.tensor_tensor(prob[:, l], mask[:, l], max_row[:], ALU.subtract).then_inc(c_dve.sem, 1)
                if slot == 12:
                    dve.wait_ge(c_act.sem, c_act.at(i, "rows1"))
                    v.tensor_copy(val_hi[:, :, 0:D], x3_rows[:]).then_inc(c_dve.sem, 1)
                    here("val_hi")
                    v.tensor_tensor(val_lo[:, :, 0:D], x3_rows[:], f32(val_hi[:, :, 0:D]), ALU.subtract).then_inc(c_dve.sem, 1)
                if 13 <= slot < 13 + R:
                    l = slot - 13
                    dve.wait_ge(c_act.sem, c_act.at(i, f"exp{l}"))
                    v.tensor_copy(prob_hi[:, l], prob[:, l]).then_inc(c_dve.sem, 1)
                if slot in (17, 18):
                    for t in (2 * (slot - 17), 2 * (slot - 17) + 1):
                        dve.wait_ge(c_pe.sem, c_pe.at(i, f"out{t}"))
                        v.tensor_scalar(den[:, t:t + 1], ps_side[:, t % 2, D:D + 1], par_l3[:, 6 + t:7 + t], None, ALU.mult).then_inc(c_dve.sem, 1)
                        here(f"den{t}")
                        v.reciprocal(rden[:, t:t + 1], den[:, t:t + 1]).then_inc(c_dve.sem, 1)
                        here(f"rden{t}")
                        if t == 0 and not (isinstance(i, int) and i == 0):
                            dve.wait_ge(out_stored, 16 * i)
                        v.scalar_tensor_tensor(out=out_rows[:, t], in0=ps_side[:, t % 2, 0:D], scalar=rden[:, t:t + 1], in1=x3_rows[:, t],
                                               op0=ALU.mult, op1=ALU.add).then_inc(c_dve.sem, 1)

            step = [0]

            def link(ins):
                step[0] += 1
                ins.then_inc(par_step, 1)
                dve.wait_ge(par_step, step[0])

            def parameters(slot):
                par_v = par[:].rearrange("p (b n) -> p b n", n=NPAR)
                if slot == 1:
                    dve.wait_ge(par_exp_done, 1)
                    link(v.tensor_reduce(gv_sum[:], gate_prob[:].rearrange("p (t e) -> p t e", e=NE), AX.X, ALU.add))
                    link(v.reciprocal(gv_sum[:], gv_sum[:]))
                    for t in range(NT):
                        ins = v.tensor_scalar(gate_prob[:, t * NE:(t + 1) * NE], gate_prob[:, t * NE:(t + 1) * NE],
                                              gv_sum[:, t:t + 1], None, ALU.mult)
                    link(ins)
                if slot == 2:
                    dve.wait_ge(ids_in, 48)
                    link(v.tensor_copy(type_bc[:], type_bc_i[:]))
                    for t in range(NT):
                        ins = v.tensor_scalar(onehot[:, :, t], type_bc[:], float(t), None, ALU.is_equal)
                    link(ins)
                if slot == 3:
                    for e in range(2):
                        diag = gate_prob[:, e:e + (NT - 1) * (NE + 1) + 1:NE + 1]
                        for t in range(NT):
                            ins = v.tensor_scalar(pick[:, :, t], onehot[:, :, t], diag[:, t:t + 1], None, ALU.mult)
                        link(ins)
                        link(v.tensor_reduce(par_v[:, :, e:e + 1], pick[:], AX.X, ALU.add))
                if slot == 4:
                    v.tensor_tensor(par_v[:, :, 2], onehot[:, :, 1], onehot[:, :, 0], ALU.subtract)
                    for t in range(NT):
                        ins = v.tensor_scalar(par_v[:, :, 3 + t], onehot[:, :, t], -NEG, NEG, ALU.mult, ALU.add)
                    link(ins)
                if slot in (5, 6):
                    dve.wait_ge(rel_ready, 1)
                    for r in (2 * (slot - 5), 2 * (slot - 5) + 1):
                        cnt = par_v[:, :, 6 + r]
                        link(v.tensor_scalar(cnt, onehot[:, :, 0], jcol[:, 0, r:r + 1], None, ALU.mult))
                        link(v.scalar_tensor_tensor(out=cnt, in0=onehot[:, :, 1], scalar=jcol[:, 1, r:r + 1], in1=cnt, op0=ALU.mult, op1=ALU.add))
                        link(v.scalar_tensor_tensor(out=cnt, in0=onehot[:, :, 2], scalar=float(S - 1), in1=cnt, op0=ALU.mult, op1=ALU.add))

            def split_x2(b):
                for k in range(KD):
                    dve.wait_ge(x2_hi_ready, KD * b + k + 1)
                    v.tensor_tensor(x2T_lo[:, k], next_x2T[:, k], f32(x2T_hi[:, k]), ALU.subtract).then_inc(x2_lo_ready, 1)

            def evacuate(b, net):
                dve.wait_ge(net_chunk_done, b * SLOTS + (net + 1) * CH)
                if net == 1:
                    dve.wait_ge(evac_act, NG * b + 1)
                    both = netT[:, 0].rearrange("p k s -> p (k s)")
                    v.scalar_tensor_tensor(out=both, in0=ps_net[:, 1].rearrange("p k s -> p (k s)"), scalar=par_l2[:, 1:2], in1=both,
                                           op0=ALU.mult, op1=ALU.add).then_inc(evac_dve, 1)
                if net >= 2:
                    v.tensor_copy(netT[:, net - 1, 1], ps_net[:, net % 2, 1]).then_inc(evac_dve, 1)

            def batch(b, first, last):
                for q in range(SLOTS):
                    dve.wait_ge(hid_hi_ready, b * SLOTS + q + 1)
                    v.scalar_tensor_tensor(out=hid_lo[:, q % 2], in0=ps_hid[:, q % 2], scalar=0.0, in1=f32(hid_hi[:, q % 2]),
                                           op0=ALU.max, op1=ALU.subtract).then_inc(hid_lo_ready, 1)
                    if first:
                        parameters(q)
                    if q == CH - 1:
                        v.tensor_copy(par_l2[:], par[:, bass.ds(b * NPAR, NPAR)]).then_inc(par_l2_ready, 1)
                        dve.wait_ge(par_l2_ready, b + 1)
                    if not first:
                        stage_c(q, b - 1)
                    if not last:
                        stage_a(q, b + 1)
                    if q % CH == 0 and q >= 2 * CH:
                        evacuate(b, q // CH - 1)
                if not last:
                    split_x2(b + 1)
                evacuate(b, NETS - 1)

            v.memset(ones[:], 1.0)
            v.memset(prefix_max[:, 0:1], NEG)
            v.memset(suffix_max[:, S:S + 1], NEG)
            v.memset(f32(val_hi[:, :, D:VW]), 1.0)
            v.memset(f32(val_lo[:, :, D:VW]), 0.0).then_inc(const_step, 1)
            dve.wait_ge(const_step, 1)
            dve.wait_ge(small_in, 64)
            link(v.tensor_reduce(gv_max[:], gate_vecs[:].rearrange("p (t e) -> p t e", e=NE), AX.X, ALU.max))
            for t in range(NT):
                ins = v.tensor_scalar(gate_prob[:, t * NE:(t + 1) * NE], gate_vecs[:, t * NE:(t + 1) * NE], gv_max[:, t:t + 1], None, ALU.subtract)
            link(ins)
            for q in range(SLOTS):
                stage_a(q, 0)
            split_x2(0)
            batch(0, True, False)
            with dve.Fori(1, B - 1) as b:
                batch(b, False, False)
            batch(B - 1, False, True)
            for q in range(SLOTS):
                stage_c(q, B - 1)

        @block.gpsimd
        def _(pool):
            g = nc.gpsimd

            def stage_a(slot, i):
                if slot == 19:
                    pool.wait_ge(a_dve.sem, a_dve.at(i, "w2_hi"))
                    g.tensor_tensor(w1_lo[:], w1[:], f32(w1_hi[:]), ALU.subtract).then_inc(a_pool.sem, 1)
                    g.tensor_tensor(w2_lo[:], w2[:], f32(w2_hi[:]), ALU.subtract).then_inc(a_pool.sem, 1)
                if slot == 20:
                    pool.wait_ge(x_in, 16 * (i + 1))
                    for r in range(R):
                        ins = g.tensor_tensor(xb_rows[:, r], x_rows[:, r], b2_bc[:], ALU.add)
                    ins.then_inc(a_pool.sem, 1)
                if slot == 24:
                    pool.wait_ge(a_dve.sem, a_dve.at(i, "var_eps"))
                    g.tensor_tensor(rstd[:], var_eps[:], half_pow[:], ALU.pow).then_inc(a_pool.sem, 1)

            def stage_c(slot, i):
                if 13 <= slot < 13 + R:
                    l = slot - 13
                    pool.wait_ge(c_dve.sem, c_dve.at(i, f"phi{l}"))
                    g.tensor_tensor(prob_lo[:, l], prob[:, l], f32(prob_hi[:, l]), ALU.subtract).then_inc(c_pool.sem, 1)

            def split_weights(b, p):
                w, half = p % RING, p // HP
                pool.wait_ge(w_hi_ready, b * PAIRS + p + 1)
                c = slice((p % HP) * 2 * P, (p % HP + 1) * 2 * P)
                t = slice(2 * (p % HP), 2 * (p % HP) + 2)
                g.tensor_tensor(wi_lo[:, w], raw_wi[:, half % 2, :, c], f32(wi_hi[:, w]), ALU.subtract)
                g.tensor_tensor(wo_lo[:, w], raw_wo[:, half % 2, t], f32(wo_hi[:, w]), ALU.subtract).then_inc(w_lo_ready, 1)

            def batch(b, first, last):
                for q in range(SLOTS):
                    if q % 2 == 1:
                        p = q // 2 + AHEAD
                        if p < PAIRS:
                            split_weights(b, p)
                        elif not last:
                            split_weights(b + 1, p - PAIRS)
                    if not first:
                        stage_c(q, b - 1)
                    if not last:
                        stage_a(q, b + 1)
                    if q == 32:
                        pool.wait_ge(x2_lo_ready, KD * (b + 1))
                        if not first:
                            pool.wait_ge(c_pe.sem, c_pe.at(b - 1, "rows1"))
                        g.tensor_tensor(x3T[:], f32(x2T_hi[:]), f32(x2T_lo[:]), ALU.add).then_inc(base_ready, 1)

            g.memset(ident[:], 0.0).then_inc(const_ready, 1)
            pool.wait_ge(const_ready, 1)
            g.affine_select(out=ident[:], in_=ident[:], compare_op=ALU.not_equal, fill=1.0, base=0,
                            pattern=[[-1, P]], channel_multiplier=1).then_inc(const_ready, 1)
            g.memset(half_pow[:], -0.5)
            g.iota(jcol_i[:], pattern=[[P, R]], base=0, channel_multiplier=1).then_inc(const_ready, 1)
            pool.wait_ge(const_ready, 3)
            for q in range(SLOTS):
                stage_a(q, 0)
                if q in (21, 23, 25):
                    split_weights(0, (q - 21) // 2)
            pool.wait_ge(small_in, 64)
            g.tensor_copy(att_v_bc[:], att_v[:].to_broadcast([A, P]))
            g.tensor_copy(att_w_hi[:], att_w[:]).then_inc(att_w_ready, 1)
            pool.wait_ge(att_w_ready, 1)
            g.tensor_tensor(att_w_lo[:], att_w[:], f32(att_w_hi[:]), ALU.subtract).then_inc(att_w_ready, 1)
            rel = prob[:].bitcast(I32)
            g.iota(rel, pattern=[[-P, R], [1, S]], base=0, channel_multiplier=-1).then_inc(const_ready, 1)
            pool.wait_ge(const_ready, 4)
            g.tensor_scalar(jcol[:, 0], jcol_i[:], 1.0, None, ALU.add)
            g.tensor_scalar(jcol[:, 1], jcol_i[:], -1.0, float(S), ALU.mult, ALU.add)
            g.tensor_scalar(rel_sign[:], rel, 1.0, -1.0, ALU.min, ALU.max).then_inc(rel_ready, 1)
            batch(0, True, False)
            with pool.Fori(1, B - 1) as b:
                batch(b, False, False)
            batch(B - 1, False, True)
            for q in range(SLOTS):
                stage_c(q, B - 1)


_INS = ["x", "itok_B_0_8", "itok_B_0_7", "itok_B_0_2",
        "L0_cond_W1", "L0_cond_b1", "L0_cond_W2", "L0_cond_b2", "L0_cond_gamma", "L0_cond_beta",
        "L1_cond_weight", "L1_cond_bias",
        "L2_cond_expert_wi", "L2_cond_expert_wo", "L2_cond_share_wi", "L2_cond_share_wo",
        "L2_cond_gate_vecs", "L2_cond_gate_w1", "L2_cond_gate_w2",
        "L3_cond_W1", "L3_cond_b1", "L3_cond_v"]


def kernel(**inputs):
    import numpy as _np
    import concourse.bacc as _bacc
    from concourse import mybir as _mybir
    from concourse.bass_utils import run_bass_kernel_spmd as _run

    nc = _bacc.Bacc("TRN2", target_bir_lowering=False, num_devices=1)
    arrays, args = {}, []
    for name in _INS:
        a = _np.ascontiguousarray(inputs[name])
        arrays[f"in_{name}_dram"] = a
        args.append(nc.dram_tensor(f"in_{name}_dram", a.shape, _mybir.dt.from_np(a.dtype), kind="ExternalInput").ap())
    shape = inputs["x"].shape
    args.append(nc.dram_tensor("out_0_dram", shape, _mybir.dt.float32, kind="ExternalOutput").ap())
    cond_resid_program(nc, *args)
    r = _run(nc, [arrays], core_ids=[0])
    return r.results[0]["out_0_dram"]
```

```python
from contextlib import ExitStack

import concourse.bass as bass
from concourse import mybir

ALU = mybir.AluOpType
ACT = mybir.ActivationFunctionType
AX = mybir.AxisListType
F32 = mybir.dt.float32
F32R = mybir.dt.float32r
BF16 = mybir.dt.bfloat16
I32 = mybir.dt.int32

P = 128
NEG = -1e30
LN_EPS = 1e-5
GATE_TEMP = 0.1


class Steps:

    def __init__(self, sem, names):
        self.sem, self.names = sem, names.split()

    def at(self, i, name):
        return i * len(self.names) + (self.names.index(name) + 1)


def cond_resid_program(
    nc, x, lang_id, subj_id, type_id,
    L0_W1, L0_b1, L0_W2, L0_b2, L0_gamma, L0_beta,
    L1_weight, L1_bias,
    L2_expert_wi, L2_expert_wo, L2_share_wi, L2_share_wo, L2_gate_vecs, L2_gate_w1, L2_gate_w2,
    L3_W1, L3_b1, L3_v, out,
):
    B, S, D = x.shape
    KD = D // P
    R = S // P
    A = L0_W1.shape[2]
    F = L2_share_wi.shape[2]
    CH = F // P
    NETS = 2 + L2_share_wi.shape[0]
    NG = NETS - 1
    SLOTS = NETS * CH
    PAIRS = SLOTS // 2
    RING = 4
    AHEAD = RING - 1
    HALVES = 2 * NETS
    HP = CH // 4
    NT = L2_gate_vecs.shape[0]
    NE = L2_gate_vecs.shape[1]
    assert PAIRS % RING == 0 and HALVES % 2 == 0 and HP == 2

    A_SLOT = dict(xT=22, hid=24, subj_w=25, adapt=26, stats=27, xb=28, norm=28, normT=30, x1_hi=31, x1_lo=33, y=34, base=37)
    PRE_SPLIT = (A_SLOT["stats"] + 1, A_SLOT["normT"] - 1, A_SLOT["normT"])
    GATE_PART = 38
    C_SLOT = dict(gate=1, logits=2, gates=3, comb=3, x3_split=5, rows=6, val=8, att=8, scores=10, prefix=11, suffix=12,
                  max=13, arg=14, exp=14, prob_hi=15, prob_lo=15, out=20)

    WARM_A = {A_SLOT["xT"]: 10, A_SLOT["hid"]: 5, A_SLOT["normT"]: 27}
    WARM_C = {C_SLOT["rows"]: 27, C_SLOT["out"]: 27}

    with ExitStack() as ctx:
        def sb(name, shape, dt=F32):
            return ctx.enter_context(nc.sbuf_tensor(name, shape, dt))

        def psum(name, shape):
            return ctx.enter_context(nc.psum_tensor(name, shape, F32))

        def sem(name):
            return ctx.enter_context(nc.semaphore(name))

        ident = sb("ident", [P, P])
        ones = sb("ones", [P, P])
        rel_sign = sb("rel_sign", [P, R, S], BF16)
        jcol_i = sb("jcol_i", [P, R], I32)
        jcol = sb("jcol", [P, 2, R])
        zeros = sb("zeros", [P, S], BF16)
        half_pow = sb("half_pow", [P, R])
        type_bc_i = sb("type_bc_i", [P, B], I32)
        type_bc = sb("type_bc", [P, B])
        gate_vecs = sb("gate_vecs", [P, NT * NE])
        gate_prob = sb("gate_prob", [P, NT * NE])
        gv_max = sb("gv_max", [P, NT])
        gv_sum = sb("gv_sum", [P, NT])
        onehot = sb("onehot", [P, B, NT])
        pick = sb("pick", [P, B, NT])
        NPAR = 6 + R
        par = sb("par", [P, B * NPAR])
        par_l2 = sb("par_l2", [P, NPAR])
        par_l3 = sb("par_l3", [P, NPAR])
        gate_w1 = sb("gate_w1", [P, NG * KD, D])
        gate_w2 = sb("gate_w2", [P, KD, NG])
        att_w = sb("att_w", [P, KD, A])
        att_w_hi = sb("att_w_hi", [P, KD, A], F32R)
        att_w_lo = sb("att_w_lo", [P, KD, A], F32R)
        att_b = sb("att_b", [A, 1])
        att_v = sb("att_v", [A, 1])
        att_v_bc = sb("att_v_bc", [A, P])

        x_rows = sb("x_rows", [P, R, D])
        w1 = sb("w1", [P, KD, A])
        w1_hi = sb("w1_hi", [P, KD, A], F32R)
        w1_lo = sb("w1_lo", [P, KD, A], F32R)
        w2 = sb("w2", [A, D])
        w2_hi = sb("w2_hi", [A, D], F32R)
        w2_lo = sb("w2_lo", [A, D], F32R)
        b1 = sb("b1", [A, 1])
        b2_bc = sb("b2_bc", [P, D])
        gamma = sb("gamma", [P, KD])
        beta = sb("beta", [P, KD])
        subj_w = sb("subj_w", [P, KD, D])
        subj_wT_hi = sb("subj_wT_hi", [P, KD, D], F32R)
        subj_wT_lo = sb("subj_wT_lo", [P, KD, D], F32R)
        subj_b = sb("subj_b", [P, KD])
        xb_rows = sb("xb_rows", [P, R, D])
        xbT = sb("xbT", [P, KD, S])
        hT = sb("hT", [A, S])
        hT_hi = sb("hT_hi", [A, S], F32R)
        hT_lo = sb("hT_lo", [A, S], F32R)
        norm = sb("norm", [P, R, D])
        stats = sb("stats", [P, R, 6])
        mean = sb("mean", [P, R])
        mean_gap = sb("mean_gap", [P, R])
        var_eps = sb("var_eps", [P, R])
        rstd = sb("rstd", [P, R])
        x1T = sb("x1T", [P, KD, S])
        next_x2T = sb("next_x2T", [P, KD, S])
        opT_hi = sb("opT_hi", [P, KD, S], F32R)
        opT_lo = sb("opT_lo", [P, KD, S], F32R)

        x2T_hi = sb("x2T_hi", [P, KD, S], F32R)
        x2T_lo = sb("x2T_lo", [P, KD, S], F32R)
        raw_wi = sb("raw_wi", [P, 2, KD, F // 2])
        raw_wo = sb("raw_wo", [P, 2, CH // 2, D])
        wi_hi = sb("wi_hi", [P, RING, KD, 2 * P], F32R)
        wi_lo = sb("wi_lo", [P, RING, KD, 2 * P], F32R)
        wo_hi = sb("wo_hi", [P, RING, 2, D], F32R)
        wo_lo = sb("wo_lo", [P, RING, 2, D], F32R)
        hid_hi = sb("hid_hi", [P, 2, S], F32R)
        hid_lo = sb("hid_lo", [P, 2, S], F32R)
        netT = sb("netT", [P, NG, KD, S])

        x3T = sb("x3T", [P, KD, S])
        gate_h = sb("gate_h", [P, KD, P])
        neg_gmax = sb("neg_gmax", [P, 1])
        gate_e = sb("gate_e", [P, NG])
        gate_sum = sb("gate_sum", [P, 1])
        gate_rec = sb("gate_rec", [P, 1])
        gates = sb("gates", [P, NG])
        attT = sb("attT", [A, S])
        floor = sb("floor", [P, S])
        score_col = sb("score_col", [P, R])
        prefix_max = sb("prefix_max", [P, S + 1])
        suffix_max = sb("suffix_max", [P, S + 1])
        max_row = sb("max_row", [P, S])
        x3_rows = sb("x3_rows", [P, R, D])
        VW = D + 2
        val_hi = sb("val_hi", [P, R, VW], F32R)
        val_lo = sb("val_lo", [P, R, VW], F32R)
        mask = sb("mask", [P, R, S], BF16)
        prob = sb("prob", [P, R, S])
        prob_hi = sb("prob_hi", [P, R, S], F32R)
        prob_lo = sb("prob_lo", [P, R, S], F32R)
        den = sb("den", [P, R])
        rden = sb("rden", [P, R])
        out_rows = sb("out_rows", [P, R, D])

        ps_hid = psum("ps_hid", [P, 2, S])
        ps_net = psum("ps_net", [P, 2, KD, S])
        ps_side = psum("ps_side", [P, 2, S])

        types_in, small_in, gate_in = sem("types_in"), sem("small_in"), sem("gate_in")
        x_in, w1_in, a_in, subj_in, out_stored = sem("x_in"), sem("w1_in"), sem("a_in"), sem("subj_in"), sem("out_stored")
        raw_in = [sem("raw_in0"), sem("raw_in1")]
        zeros_ready, const_ready, const_step, rel_ready, att_w_ready = (
            sem("zeros_ready"), sem("const_ready"), sem("const_step"), sem("rel_ready"), sem("att_w_ready"))
        par_step, par_exp_done, par_l2_ready = sem("par_step"), sem("par_exp_done"), sem("par_l2_ready")
        x2_hi_ready, x2_lo_ready = sem("x2_hi_ready"), sem("x2_lo_ready")
        w_hi_ready, w_lo_ready = sem("w_hi_ready"), sem("w_lo_ready")
        hid_done, hid_hi_ready, hid_lo_ready = sem("hid_done"), sem("hid_hi_ready"), sem("hid_lo_ready")
        net_chunk_done = sem("net_chunk_done")
        evac_act, evac_dve, base_ready = sem("evac_act"), sem("evac_dve"), sem("base_ready")

        a_pe = Steps(sem("a_pe"), "xT0 xT1 hid subj_wT adapt0 adapt1 normT0 normT1 y0 y1")
        a_act = Steps(sem("a_act"), "xhi0 xhi1 hid subj_w_hi x1hi0 x1hi1")
        a_dve = Steps(sem("a_dve"), "w1_hi xlo0 xlo1 w2_hi hid_hi hid_lo subj_w_lo sum0 sum1 stats sums mean var_eps "
                                    "xb0 xb1 norm x1T0 x1T1 x1lo0 x1lo1 x2T0 x2T1")
        a_pool = Steps(sem("a_pool"), "w1_lo w2_lo xb rstd")
        c_pe = Steps(sem("c_pe"), "gate_h logits rows0 rows1 att score_row score_col out0 out1 out2 out3")
        c_act = Steps(sem("c_act"), "gate_exp x3hi0 x3hi1 rows0 rows1 att score_col max0 exp0 exp1 exp2 exp3")
        c_dve = Steps(sem("c_dve"), "par mask gate_h gate_max gate_rec gates comb00 comb10 comb01 comb11 comb02 comb12 comb03 comb13 x3lo0 x3lo1 "
                                    "val_hi val_lo prefix suffix max1 max2 max3 "
                                    "arg0 arg1 arg2 phi0 plo0 phi1 phi2 plo2 phi3 plo3 "
                                    "den0 rden0 out0 out1 den1 rden1 out2 out3")
        c_pool = Steps(sem("c_pool"), "arg3 plo1")

        block = ctx.enter_context(nc.Block())

        def f32(ap):
            return ap.bitcast(F32)

        def out_tiles(n, final):
            return ((0, 1, 2, 3), ())[n] if final else (2 * n, 2 * n + 1)

        def out_bank(t, final):
            return ps_hid[:, t - 2, 0:VW] if final and t >= 2 else ps_side[:, t % 2, 0:VW]

        @block.sync
        def _(sp):
            lang_row, subj_row, type_row = (a.rearrange("(o b) -> o b", o=1) for a in (lang_id, subj_id, type_id))

            def load_x(i):
                sp.dma_start(x_rows[:], x[bass.ds(i, 1)].rearrange("o (r p) d -> p (o r) d", p=P)).then_inc(x_in, 16)

            def load_params(i):
                lang = sp.value_load(lang_row[0:1, bass.ds(i, 1)], min_val=0, max_val=L0_W1.shape[0] - 1)
                subj = sp.value_load(subj_row[0:1, bass.ds(i, 1)], min_val=0, max_val=L1_weight.shape[0] - 1)
                la, su = bass.ds(lang, 1), bass.ds(subj, 1)
                with nc.allow_non_contiguous_dma(reason="a few vectors, one element to a partition"):
                    sp.dma_start(w1[:], L0_W1[la].rearrange("o (k p) a -> p (o k) a", p=P)).then_inc(w1_in, 16)
                    sp.dma_start(b1[:], L0_b1[la].rearrange("o a -> a o")).then_inc(w1_in, 16)
                    sp.dma_start(w2[:], L0_W2[la].rearrange("o a d -> (o a) d")).then_inc(a_in, 16)
                    sp.dma_start(b2_bc[:], L0_b2[la].to_broadcast([P, D])).then_inc(a_in, 16)
                    sp.dma_start(gamma[:], L0_gamma[la].rearrange("o (k p) -> p (o k)", p=P)).then_inc(a_in, 16)
                    sp.dma_start(beta[:], L0_beta[la].rearrange("o (k p) -> p (o k)", p=P)).then_inc(a_in, 16)
                    sp.dma_start(subj_w[:], L1_weight[su].rearrange("o (k p) d -> p (o k) d", p=P)).then_inc(subj_in, 16)
                    sp.dma_start(subj_b[:], L1_bias[su].rearrange("o (k p) -> p (o k)", p=P)).then_inc(subj_in, 16)

            def load_half(b, h, kind):
                slot, net, part = h % 2, h // 2, h % 2
                if not (isinstance(b, int) and b == 0 and h < 2):
                    sp.wait_ge(w_lo_ready, b * PAIRS + HP * (h - 1))
                cols = slice(part * (F // 2), (part + 1) * (F // 2))
                if net < 2:
                    e = bass.ds(kind + net, 1)
                    wi, wo = L2_expert_wi[e, :, cols], L2_expert_wo[e, cols]
                else:
                    wi, wo = L2_share_wi[net - 2:net - 1, :, cols], L2_share_wo[net - 2:net - 1, cols]
                sp.dma_start(raw_wi[:, slot], wi.rearrange("o (k p) f -> p (o k) f", p=P)).then_inc(raw_in[slot], 16)
                sp.dma_start(raw_wo[:, slot], wo.rearrange("o (c p) d -> p (o c) d", p=P)).then_inc(raw_in[slot], 16)

            def store(i, half):
                sp.wait_ge(c_dve.sem, c_dve.at(i, f"out{2 * half + 1}"))
                rows = slice(half * (S // 2), (half + 1) * (S // 2))
                sp.dma_start(out[bass.ds(i, 1), rows].rearrange("o (r p) d -> p (o r) d", p=P),
                             out_rows[:, 2 * half:2 * half + 2]).then_inc(out_stored, 16)

            def batch(b, first, last):
                kind = sp.value_load(type_row[0:1, bass.ds(b, 1)], min_val=0, max_val=NT - 1)
                for h in range(HALVES):
                    load_half(b, h, kind)
                    if h == 4 and not last:
                        sp.wait_ge(a_dve.sem, a_dve.at(b, "x2T1"))
                        load_x(b + 1)
                        load_params(b + 1)
                    if h == 8 and not first:
                        for half in range(2):
                            store(b - 1, half)

            load_x(0)
            load_params(0)
            batch(0, True, False)
            with sp.Fori(1, B - 1) as b:
                batch(b, False, False)
            batch(B - 1, False, True)
            for half in range(2):
                store(B - 1, half)
            sp.wait_ge(out_stored, 32 * B)

        @block.tensor
        def _(pe):
            mm = nc.tensor.matmul

            def product(dst, pairs, before_lo=None):
                for t, (lh, ll, rh, _) in enumerate(pairs):
                    mm(dst, ll, rh, start=(t == 0), stop=False)
                    mm(dst, lh, rh, start=False, stop=False)
                if before_lo:
                    pe.wait_ge(*before_lo)
                for t, (lh, _, _, rl) in enumerate(pairs):
                    last = mm(dst, lh, rl, start=False, stop=(t == len(pairs) - 1))
                return last

            def stage_a(slot, i, after_c):
                if 0 <= slot - A_SLOT["xT"] < KD:
                    k = slot - A_SLOT["xT"]
                    if k == 0:
                        pe.wait_ge(x_in, 16 * (i + 1))
                        pe.wait_ge(const_ready, 2)
                    if after_c:
                        pe.wait_ge(c_dve.sem, c_dve.at(i - 2, "out3"))
                    for r in range(R):
                        last = nc.tensor.transpose(ps_side[:, k, r * P:(r + 1) * P], x_rows[:, r, k * P:(k + 1) * P], ident[:])
                    last.then_inc(a_pe.sem, 1)
                if slot == A_SLOT["subj_w"]:
                    pe.wait_ge(subj_in, 32 * (i + 1))
                    pe.wait_ge(a_dve.sem, a_dve.at(i, "xlo1"))
                    for k in range(KD):
                        for o in range(KD):
                            c = k * D + o * P
                            last = nc.tensor.transpose(ps_side[:, 1, c:c + P], subj_w[:, o, k * P:(k + 1) * P], ident[:])
                    last.then_inc(a_pe.sem, 1)
                if slot == A_SLOT["hid"]:
                    pe.wait_ge(a_act.sem, a_act.at(i, "xhi1"))
                    pe.wait_ge(a_dve.sem, a_dve.at(i, "xlo0"))
                    pe.wait_ge(a_pool.sem, a_pool.at(i, "w1_lo"))
                    product(ps_side[0:A, 0], [(w1_hi[:, k], w1_lo[:, k], opT_hi[:, k], opT_lo[:, k]) for k in range(KD)],
                            (a_dve.sem, a_dve.at(i, "xlo1"))).then_inc(a_pe.sem, 1)
                if slot == A_SLOT["adapt"]:
                    for t in range(2):
                        if t == 0:
                            pe.wait_ge(a_pool.sem, a_pool.at(i, "w2_lo"))
                            pe.wait_ge(a_dve.sem, a_dve.at(i, "hid_lo"))
                        else:
                            pe.wait_ge(a_dve.sem, a_dve.at(i, "subj_w_lo"))
                        for r in (2 * t, 2 * t + 1):
                            c = slice((r % 2) * D, (r % 2 + 1) * D)
                            rows = slice(r * P, (r + 1) * P)
                            last = product(ps_side[:, t, c], [(hT_hi[:, rows], hT_lo[:, rows], w2_hi[:], w2_lo[:])])
                        last.then_inc(a_pe.sem, 1)
                if 0 <= slot - A_SLOT["normT"] < KD:
                    k = slot - A_SLOT["normT"]
                    pe.wait_ge(a_dve.sem, a_dve.at(i, "norm"))
                    for r in range(R):
                        last = nc.tensor.transpose(ps_side[:, k, r * P:(r + 1) * P], norm[:, r, k * P:(k + 1) * P], ident[:])
                    last.then_inc(a_pe.sem, 1)
                if 0 <= slot - A_SLOT["y"] < KD:
                    o = slot - A_SLOT["y"]
                    pe.wait_ge(a_act.sem, a_act.at(i, "x1hi1"))
                    product(ps_side[:, o], [(subj_wT_hi[:, k, o * P:(o + 1) * P], subj_wT_lo[:, k, o * P:(o + 1) * P],
                                             opT_hi[:, k], opT_lo[:, k]) for k in range(KD)],
                            (a_dve.sem, a_dve.at(i, "x1lo1"))).then_inc(a_pe.sem, 1)

            def keep_warm(n):
                for _ in range(n):
                    mm(ps_net[:, 1, 1], zeros[:, 0:P], zeros[:], start=True, stop=True)

            def gate_terms(i, first_net, end_net):
                pe.wait_ge(evac_act, NG * i + end_net)
                pe.wait_ge(evac_dve, NG * i + end_net)
                if first_net == 0:
                    pe.wait_ge(gate_in, 32)
                for o in range(KD):
                    for c in range(first_net * KD, end_net * KD):
                        last = mm(ps_side[:, 0, o:o + 1], gate_w1[:, c, o * P:(o + 1) * P], netT[:, c // KD, c % KD, 0:1],
                                  start=(o == 0 and c == 0), stop=(c == NG * KD - 1), skip_group_check=True)
                return last

            def stage_c(slot, i, final=False):
                if slot == C_SLOT["gate"]:
                    gate_terms(i, NG - 1, NG).then_inc(c_pe.sem, 1)
                if slot == C_SLOT["logits"]:
                    pe.wait_ge(c_dve.sem, c_dve.at(i, "gate_h"))
                    for o in range(KD):
                        last = mm(ps_side[:, 1, 0:NG], gate_h[:, o], gate_w2[:, o], start=(o == 0), stop=(o == KD - 1))
                    last.then_inc(c_pe.sem, 1)
                if 0 <= slot - C_SLOT["rows"] < 2:
                    t = slot - C_SLOT["rows"]
                    if t == 0:
                        pe.wait_ge(c_dve.sem, c_dve.at(i, "comb13"))
                    for r in (2 * t, 2 * t + 1):
                        for k in range(KD):
                            c = (r % 2) * D + k * P
                            last = nc.tensor.transpose(ps_side[:, t, c:c + P], x3T[:, k, r * P:(r + 1) * P], ident[:])
                    last.then_inc(c_pe.sem, 1)
                if slot == C_SLOT["att"]:
                    pe.wait_ge(att_w_ready, 2)
                    pe.wait_ge(c_act.sem, c_act.at(i, "rows0"))
                    product(ps_side[0:A, 0], [(att_w_hi[:, k], att_w_lo[:, k], opT_hi[:, k], opT_lo[:, k]) for k in range(KD)],
                            (c_dve.sem, c_dve.at(i, "x3lo1"))).then_inc(c_pe.sem, 1)
                if slot == C_SLOT["scores"]:
                    pe.wait_ge(c_act.sem, c_act.at(i, "att"))
                    mm(ps_side[:, 1], att_v_bc[:], attT[:], start=True, stop=True).then_inc(c_pe.sem, 1)
                    for r in range(R):
                        last = mm(ps_side[:, 0, r:r + 1], attT[:, r * P:(r + 1) * P], att_v[:], start=True, stop=True)
                    last.then_inc(c_pe.sem, 1)
                if 0 <= slot - C_SLOT["out"] < 2:
                    tiles = out_tiles(slot - C_SLOT["out"], final)
                    for l in range(R if tiles else 0):
                        if tiles[0] == 0:
                            by = c_pool if l == 1 else c_dve
                            pe.wait_ge(by.sem, by.at(i, f"plo{l}"))
                        for t in tiles:
                            if l == 0 and tiles[0] == 2:
                                pe.wait_ge(c_dve.sem, c_dve.at(i, f"out{t - 2}"))
                            dst, cols = out_bank(t, final), slice(t * P, (t + 1) * P)
                            mm(dst, prob_lo[:, l, cols], val_hi[:, l], start=(l == 0), stop=False)
                            mm(dst, prob_hi[:, l, cols], val_hi[:, l], start=False, stop=False)
                            last = mm(dst, prob_hi[:, l, cols], val_lo[:, l], start=False, stop=(l == R - 1))
                            if l == R - 1:
                                last.then_inc(c_pe.sem, 1)

            def first_product(b, q, first):
                if q % 2 == 0:
                    pe.wait_ge(w_lo_ready, b * PAIRS + q // 2 + 1)
                if not (first and q < 2):
                    pe.wait_ge(hid_lo_ready, b * SLOTS + q - 1)
                w, c = (q // 2) % RING, slice((q % 2) * P, (q % 2 + 1) * P)
                for k in range(KD):
                    if q == 0:
                        pe.wait_ge(x2_hi_ready, KD * b + k + 1)
                    mm(ps_hid[:, q % 2], wi_lo[:, w, k, c], x2T_hi[:, k], start=(k == 0), stop=False)
                    mm(ps_hid[:, q % 2], wi_hi[:, w, k, c], x2T_hi[:, k], start=False, stop=False)
                for k in range(KD):
                    if q == 0:
                        pe.wait_ge(x2_lo_ready, KD * b + k + 1)
                    last = mm(ps_hid[:, q % 2], wi_hi[:, w, k, c], x2T_lo[:, k], start=False, stop=(k == KD - 1))
                last.then_inc(hid_done, 1)

            def second_product(b, q, first):
                net, c = q // CH, q % CH
                if c == 0:
                    if net == 0 and not first:
                        pe.wait_ge(evac_act, NG * b)
                        pe.wait_ge(evac_dve, NG * b)
                    if net == 2:
                        pe.wait_ge(evac_act, NG * b + 1)
                    if net >= 3:
                        pe.wait_ge(evac_act, NG * b + net - 2)
                        pe.wait_ge(evac_dve, NG * b + net - 2)
                pe.wait_ge(hid_hi_ready, b * SLOTS + q + 1)
                w = (q // 2) % RING
                for k in range(KD):
                    cols = slice(k * P, (k + 1) * P)
                    mm(ps_net[:, net % 2, k], wo_hi[:, w, q % 2, cols], hid_hi[:, q % 2], start=(c == 0), stop=False)
                    mm(ps_net[:, net % 2, k], wo_lo[:, w, q % 2, cols], hid_hi[:, q % 2], start=False, stop=False)
                pe.wait_ge(hid_lo_ready, b * SLOTS + q + 1)
                for k in range(KD):
                    cols = slice(k * P, (k + 1) * P)
                    last = mm(ps_net[:, net % 2, k], wo_hi[:, w, q % 2, cols], hid_lo[:, q % 2], start=False, stop=(c == CH - 1))
                last.then_inc(net_chunk_done, 1)

            def batch(b, first, last):
                for q in range(SLOTS):
                    first_product(b, q, first)
                    if not first:
                        stage_c(q, b - 1)
                    if not last:
                        stage_a(q, b + 1, not first)
                    if q == GATE_PART:
                        if not last:
                            pe.wait_ge(a_dve.sem, a_dve.at(b + 1, "x2T0"))
                        gate_terms(b, 0, NG - 1)
                    if q >= 1:
                        second_product(b, q - 1, first)
                second_product(b, SLOTS - 1, first)

            for q in range(SLOTS):
                if q in WARM_A:
                    pe.wait_ge(zeros_ready, 1)
                    keep_warm(WARM_A[q])
                stage_a(q, 0, False)
            batch(0, True, False)
            with pe.Fori(1, B - 1) as b:
                batch(b, False, False)
            batch(B - 1, False, True)
            for q in range(SLOTS):
                if q in WARM_C:
                    keep_warm(WARM_C[q])
                stage_c(q, B - 1, True)

        @block.scalar
        def _(act):
            fn = nc.scalar.activation

            def stage_a(slot, i, after_c):
                if 0 <= slot - A_SLOT["xT"] < KD:
                    k = slot - A_SLOT["xT"]
                    act.wait_ge(a_pe.sem, a_pe.at(i, f"xT{k}"))
                    if after_c:
                        act.wait_ge(c_pe.sem, c_pe.at(i - 2, "att"))
                    fn(opT_hi[:, k], ps_side[:, k], ACT.Copy).then_inc(a_act.sem, 1)
                if slot == A_SLOT["hid"]:
                    act.wait_ge(a_pe.sem, a_pe.at(i, "hid"))
                    fn(hT[:], ps_side[0:A, 0], ACT.Relu, bias=b1[:]).then_inc(a_act.sem, 1)
                if slot == A_SLOT["subj_w"]:
                    act.wait_ge(a_pe.sem, a_pe.at(i, "subj_wT"))
                    fn(subj_wT_hi[:].rearrange("p k d -> p (k d)"), ps_side[:, 1], ACT.Copy).then_inc(a_act.sem, 1)
                if 0 <= slot - A_SLOT["x1_hi"] < KD:
                    k = slot - A_SLOT["x1_hi"]
                    act.wait_ge(a_dve.sem, a_dve.at(i, f"x1T{k}"))
                    fn(opT_hi[:, k], x1T[:, k], ACT.Copy).then_inc(a_act.sem, 1)

            def stage_c(slot, i, final=False):
                if slot == C_SLOT["logits"]:
                    act.wait_ge(c_dve.sem, c_dve.at(i, "gate_max"))
                    fn(gate_e[:], ps_side[:, 1, 0:NG], ACT.Exp, bias=neg_gmax[:], accum_out=gate_sum[:]).then_inc(c_act.sem, 1)
                if slot == C_SLOT["x3_split"]:
                    for k in range(KD):
                        act.wait_ge(c_dve.sem, c_dve.at(i, f"comb{k}3"))
                        fn(opT_hi[:, k], x3T[:, k], ACT.Copy).then_inc(c_act.sem, 1)
                if 0 <= slot - C_SLOT["rows"] < 2:
                    t = slot - C_SLOT["rows"]
                    act.wait_ge(c_pe.sem, c_pe.at(i, f"rows{t}"))
                    fn(x3_rows[:, 2 * t:2 * t + 2].rearrange("p r d -> p (r d)"), ps_side[:, t], ACT.Copy).then_inc(c_act.sem, 1)
                if slot == C_SLOT["att"]:
                    act.wait_ge(c_pe.sem, c_pe.at(i, "att"))
                    fn(attT[:], ps_side[0:A, 0], ACT.Tanh, bias=att_b[:]).then_inc(c_act.sem, 1)
                if slot == C_SLOT["scores"]:
                    act.wait_ge(c_pe.sem, c_pe.at(i, "score_col"))
                    fn(score_col[:], ps_side[:, 0, 0:R], ACT.Copy).then_inc(c_act.sem, 1)
                if slot == C_SLOT["suffix"]:
                    act.wait_ge(c_dve.sem, c_dve.at(i, "prefix"))
                    fn(max_row[:], prefix_max[:, 1:S + 1], ACT.Identity, bias=par_l3[:, 3:4]).then_inc(c_act.sem, 1)
                if 0 <= slot - C_SLOT["exp"] < R:
                    l = slot - C_SLOT["exp"]
                    act.wait_ge(c_act.sem, c_act.at(i, "score_col"))
                    if l < R - 1:
                        act.wait_ge(c_dve.sem, c_dve.at(i, f"arg{l}"))
                    else:
                        act.wait_ge(c_pool.sem, c_pool.at(i, f"arg{l}"))
                    fn(prob[:, l], prob[:, l], ACT.Exp, bias=score_col[:, l:l + 1]).then_inc(c_act.sem, 1)

            def split_weights(b, p, free):
                w, half = p % RING, p // HP
                act.wait_ge(raw_in[half % 2], 32 * ((HALVES // 2) * b + half // 2 + 1))
                if free:
                    act.wait_ge(net_chunk_done, b * SLOTS + 2 * (p - RING) + 2)
                c = slice((p % HP) * 2 * P, (p % HP + 1) * 2 * P)
                fn(wi_hi[:, w], raw_wi[:, half % 2, :, c], ACT.Copy)
                fn(wo_hi[:, w], raw_wo[:, half % 2, 2 * (p % HP):2 * (p % HP) + 2], ACT.Copy).then_inc(w_hi_ready, 1)

            def split_x2(b):
                for k in range(KD):
                    act.wait_ge(a_dve.sem, a_dve.at(b, f"x2T{k}"))
                    fn(x2T_hi[:, k], next_x2T[:, k], ACT.Copy).then_inc(x2_hi_ready, 1)

            def evacuate(b, net):
                act.wait_ge(net_chunk_done, b * SLOTS + (net + 1) * CH)
                if net == 0:
                    act.wait_ge(par_l2_ready, b + 1)
                    if not (isinstance(b, int) and b == 0):
                        act.wait_ge(c_dve.sem, c_dve.at(b - 1, "comb13"))
                    for k in range(KD):
                        last = fn(netT[:, 0, k], ps_net[:, 0, k], ACT.Copy, scale=par_l2[:, 0:1])
                    last.then_inc(evac_act, 1)
                if net >= 2:
                    fn(netT[:, net - 1, 0], ps_net[:, net % 2, 0], ACT.Copy).then_inc(evac_act, 1)

            def batch(b, first, last):
                for q in range(SLOTS):
                    act.wait_ge(hid_done, b * SLOTS + q + 1)
                    if not (first and q < 2):
                        act.wait_ge(net_chunk_done, b * SLOTS + q - 1)
                    fn(hid_hi[:, q % 2], ps_hid[:, q % 2], ACT.Relu).then_inc(hid_hi_ready, 1)
                    if first and q == 0:
                        act.wait_ge(par_step, 2)
                        fn(gate_prob[:], gate_prob[:], ACT.Exp, scale=1.0 / GATE_TEMP).then_inc(par_exp_done, 1)
                    if q % 2 == 1:
                        p = q // 2 + AHEAD
                        if p < PAIRS:
                            split_weights(b, p, not (first and p < RING))
                        elif not last:
                            split_weights(b + 1, p - PAIRS, True)
                    if not first:
                        stage_c(q, b - 1)
                    if not last:
                        stage_a(q, b + 1, not first)
                    if q % CH == 0 and q >= CH:
                        evacuate(b, q // CH - 1)
                if not last:
                    act.wait_ge(base_ready, b + 1)
                    split_x2(b + 1)
                evacuate(b, NETS - 1)

            for q in range(A_SLOT["adapt"]):
                stage_a(q, 0, False)
            act.wait_ge(subj_in, 32)
            act.dma_start(type_bc_i[:], type_id.rearrange("(o b) -> o b", o=1).to_broadcast([P, B])).then_inc(types_in, 16)
            act.dma_start(gate_vecs[:], L2_gate_vecs.rearrange("(o t) e -> o (t e)", o=1).to_broadcast([P, NT * NE])).then_inc(small_in, 16)
            with nc.allow_non_contiguous_dma(reason="two vectors, one element to a partition"):
                act.dma_start(att_b[:], L3_b1.rearrange("(a o) -> a o", o=1)).then_inc(small_in, 16)
                act.dma_start(att_v[:], L3_v.rearrange("(a o) -> a o", o=1)).then_inc(small_in, 16)
            act.dma_start(att_w[:], L3_W1.rearrange("(k p) a -> p k a", p=P)).then_inc(small_in, 16)
            act.dma_start(gate_w2[:], L2_gate_w2.rearrange("(k p) g -> p k g", p=P)).then_inc(gate_in, 16)
            act.dma_start(gate_w1[:], L2_gate_w1.rearrange("(c p) d -> p c d", p=P)).then_inc(gate_in, 16)
            for q in range(A_SLOT["adapt"], SLOTS):
                stage_a(q, 0, False)
                if q in PRE_SPLIT:
                    split_weights(0, PRE_SPLIT.index(q), False)
            split_x2(0)
            batch(0, True, False)
            with act.Fori(1, B - 1) as b:
                batch(b, False, False)
            batch(B - 1, False, True)
            for q in range(SLOTS):
                stage_c(q, B - 1, True)

        @block.vector
        def _(dve):
            v = nc.vector

            def stage_a(slot, i):
                def here(name):
                    dve.wait_ge(a_dve.sem, a_dve.at(i, name))

                if slot == A_SLOT["xT"]:
                    dve.wait_ge(w1_in, 32 * (i + 1))
                    v.tensor_copy(w1_hi[:], w1[:]).then_inc(a_dve.sem, 1)
                if 0 <= slot - A_SLOT["xT"] < KD:
                    k = slot - A_SLOT["xT"]
                    dve.wait_ge(a_act.sem, a_act.at(i, f"xhi{k}"))
                    v.tensor_tensor(opT_lo[:, k], ps_side[:, k], f32(opT_hi[:, k]), ALU.subtract).then_inc(a_dve.sem, 1)
                if slot == A_SLOT["xT"] + 1:
                    dve.wait_ge(a_in, 64 * (i + 1))
                    v.tensor_copy(w2_hi[:], w2[:]).then_inc(a_dve.sem, 1)
                if slot == A_SLOT["hid"]:
                    dve.wait_ge(a_act.sem, a_act.at(i, "hid"))
                    v.tensor_copy(hT_hi[:], hT[:]).then_inc(a_dve.sem, 1)
                    here("hid_hi")
                    v.tensor_tensor(hT_lo[:], hT[:], f32(hT_hi[:]), ALU.subtract).then_inc(a_dve.sem, 1)
                if slot == A_SLOT["subj_w"]:
                    dve.wait_ge(a_act.sem, a_act.at(i, "subj_w_hi"))
                    v.tensor_tensor(subj_wT_lo[:].rearrange("p k d -> p (k d)"), ps_side[:, 1],
                                    f32(subj_wT_hi[:].rearrange("p k d -> p (k d)")), ALU.subtract).then_inc(a_dve.sem, 1)
                if slot == A_SLOT["adapt"]:
                    for t in range(2):
                        dve.wait_ge(a_pe.sem, a_pe.at(i, f"adapt{t}"))
                        if t == 0:
                            dve.wait_ge(a_pool.sem, a_pool.at(i, "xb"))
                        rows = slice(2 * t, 2 * t + 2)
                        v.tensor_tensor(norm[:, rows].rearrange("p r d -> p (r d)"), ps_side[:, t],
                                        xb_rows[:, rows].rearrange("p r d -> p (r d)"), ALU.add).then_inc(a_dve.sem, 1)
                if slot == A_SLOT["stats"]:
                    here("sum1")
                    for r in range(R):
                        last = v.bn_stats(stats[:, r], norm[:, r])
                    last.then_inc(a_dve.sem, 1)
                    here("stats")
                    v.tensor_tensor(mean[:], stats[:, :, 1], stats[:, :, 4], ALU.add)
                    v.tensor_tensor(mean_gap[:], stats[:, :, 1], stats[:, :, 4], ALU.subtract)
                    v.tensor_tensor(var_eps[:], stats[:, :, 2], stats[:, :, 5], ALU.add).then_inc(a_dve.sem, 1)
                    here("sums")
                    v.tensor_scalar(mean[:], mean[:], 0.5, None, ALU.mult)
                    v.scalar_tensor_tensor(out=mean_gap[:], in0=mean_gap[:], scalar=0.25, in1=mean_gap[:], op0=ALU.mult, op1=ALU.mult)
                    v.tensor_scalar(var_eps[:], var_eps[:], 1.0 / D, LN_EPS, ALU.mult, ALU.add).then_inc(a_dve.sem, 1)
                    here("mean")
                    v.tensor_tensor(var_eps[:], var_eps[:], mean_gap[:], ALU.add).then_inc(a_dve.sem, 1)
                if slot == A_SLOT["xb"]:
                    here("xlo1")
                    for k in range(KD):
                        v.scalar_tensor_tensor(out=xbT[:, k], in0=f32(opT_hi[:, k]), scalar=beta[:, k:k + 1], in1=f32(opT_lo[:, k]),
                                               op0=ALU.add, op1=ALU.add).then_inc(a_dve.sem, 1)
                if slot == A_SLOT["norm"]:
                    dve.wait_ge(a_pool.sem, a_pool.at(i, "rstd"))
                    for r in range(R):
                        last = v.tensor_scalar(norm[:, r], norm[:, r], mean[:, r:r + 1], rstd[:, r:r + 1], ALU.subtract, ALU.mult)
                    last.then_inc(a_dve.sem, 1)
                if 0 <= slot - A_SLOT["normT"] < KD:
                    k = slot - A_SLOT["normT"]
                    dve.wait_ge(a_pe.sem, a_pe.at(i, f"normT{k}"))
                    here(f"xb{k}")
                    v.scalar_tensor_tensor(out=x1T[:, k], in0=ps_side[:, k], scalar=gamma[:, k:k + 1], in1=xbT[:, k],
                                           op0=ALU.mult, op1=ALU.add).then_inc(a_dve.sem, 1)
                if slot == A_SLOT["x1_lo"]:
                    here("x1T1")
                    for k in range(KD):
                        dve.wait_ge(a_act.sem, a_act.at(i, f"x1hi{k}"))
                        v.tensor_tensor(opT_lo[:, k], x1T[:, k], f32(opT_hi[:, k]), ALU.subtract).then_inc(a_dve.sem, 1)
                if 0 <= slot - A_SLOT["y"] < KD:
                    k = slot - A_SLOT["y"]
                    dve.wait_ge(a_pe.sem, a_pe.at(i, f"y{k}"))
                    v.scalar_tensor_tensor(out=next_x2T[:, k], in0=ps_side[:, k], scalar=subj_b[:, k:k + 1], in1=x1T[:, k],
                                           op0=ALU.add, op1=ALU.add).then_inc(a_dve.sem, 1)

            def stage_c(slot, i, final=False):
                def here(name):
                    dve.wait_ge(c_dve.sem, c_dve.at(i, name))

                if slot == C_SLOT["gate"]:
                    v.tensor_copy(par_l3[:], par[:, bass.ds(i * NPAR, NPAR)]).then_inc(c_dve.sem, 1)
                    here("par")
                    dve.wait_ge(rel_ready, 1)
                    v.tensor_scalar(mask[:], rel_sign[:], par_l3[:, 2:3], NEG, ALU.is_equal, ALU.mult).then_inc(c_dve.sem, 1)
                    dve.wait_ge(c_pe.sem, c_pe.at(i, "gate_h"))
                    for o in range(KD):
                        last = v.tensor_scalar(gate_h[:, o], ones[:], ps_side[:, 0, o:o + 1], 0.0, ALU.mult, ALU.max)
                    last.then_inc(c_dve.sem, 1)
                if slot == C_SLOT["logits"]:
                    dve.wait_ge(c_pe.sem, c_pe.at(i, "logits"))
                    v.tensor_reduce(neg_gmax[:], ps_side[:, 1, 0:NG], AX.X, ALU.max, negate=True).then_inc(c_dve.sem, 1)
                if slot == C_SLOT["gates"]:
                    dve.wait_ge(c_act.sem, c_act.at(i, "gate_exp"))
                    v.reciprocal(gate_rec[:], gate_sum[:]).then_inc(c_dve.sem, 1)
                    here("gate_rec")
                    v.tensor_scalar(gates[:], gate_e[:], gate_rec[:, 0:1], None, ALU.mult).then_inc(c_dve.sem, 1)
                    here("gates")
                    dve.wait_ge(base_ready, i + 1)
                if 0 <= slot - C_SLOT["comb"] < 2:
                    for n in (2 * (slot - C_SLOT["comb"]), 2 * (slot - C_SLOT["comb"]) + 1):
                        for k in range(KD):
                            if n > 0:
                                here(f"comb{k}{n - 1}")
                            v.scalar_tensor_tensor(out=x3T[:, k], in0=netT[:, n, k], scalar=gates[:, n:n + 1], in1=x3T[:, k],
                                                   op0=ALU.mult, op1=ALU.add).then_inc(c_dve.sem, 1)
                if slot == C_SLOT["x3_split"]:
                    for k in range(KD):
                        dve.wait_ge(c_act.sem, c_act.at(i, f"x3hi{k}"))
                        v.tensor_tensor(opT_lo[:, k], x3T[:, k], f32(opT_hi[:, k]), ALU.subtract).then_inc(c_dve.sem, 1)
                if slot == C_SLOT["val"]:
                    dve.wait_ge(c_act.sem, c_act.at(i, "rows1"))
                    v.tensor_copy(val_hi[:, :, 0:D], x3_rows[:]).then_inc(c_dve.sem, 1)
                    here("val_hi")
                    v.tensor_tensor(val_lo[:, :, 0:D], x3_rows[:], f32(val_hi[:, :, 0:D]), ALU.subtract).then_inc(c_dve.sem, 1)
                if slot == C_SLOT["prefix"]:
                    dve.wait_ge(c_pe.sem, c_pe.at(i, "score_row"))
                    v.tensor_tensor_scan(prefix_max[:, 1:S + 1], ps_side[:, 1], floor[:], NEG, ALU.max, ALU.max).then_inc(c_dve.sem, 1)
                if slot == C_SLOT["suffix"]:
                    v.tensor_tensor_scan(suffix_max[:, S - 1::-1], ps_side[:, 1, ::-1], floor[:], NEG, ALU.max, ALU.max).then_inc(c_dve.sem, 1)
                if slot == C_SLOT["max"]:
                    dve.wait_ge(c_act.sem, c_act.at(i, "max0"))
                    for n, (side, c) in enumerate([(prefix_max[:, 0:S], 5), (suffix_max[:, 0:S], 4), (suffix_max[:, 1:S + 1], 5)]):
                        here(f"max{n}" if n else "suffix")
                        v.scalar_tensor_tensor(out=max_row[:], in0=side, scalar=par_l3[:, c:c + 1], in1=max_row[:],
                                               op0=ALU.add, op1=ALU.max).then_inc(c_dve.sem, 1)
                if slot == C_SLOT["arg"]:
                    here("max3")
                    for l in range(R - 1):
                        v.tensor_tensor(prob[:, l], mask[:, l], max_row[:], ALU.subtract).then_inc(c_dve.sem, 1)
                if 0 <= slot - C_SLOT["prob_hi"] < R:
                    l = slot - C_SLOT["prob_hi"]
                    dve.wait_ge(c_act.sem, c_act.at(i, f"exp{l}"))
                    v.tensor_copy(prob_hi[:, l], prob[:, l]).then_inc(c_dve.sem, 1)
                    if l != 1:
                        here(f"phi{l}")
                        v.tensor_tensor(prob_lo[:, l], prob[:, l], f32(prob_hi[:, l]), ALU.subtract).then_inc(c_dve.sem, 1)
                if 0 <= slot - C_SLOT["out"] < 2:
                    n = slot - C_SLOT["out"]
                    tiles = (2 * n, 2 * n + 1)
                    dve.wait_ge(c_pe.sem, c_pe.at(i, f"out{tiles[1]}"))
                    for t in tiles:
                        last = v.tensor_scalar(den[:, t:t + 1], out_bank(t, final)[:, D:D + 1], par_l3[:, 6 + t:7 + t], None, ALU.mult)
                    last.then_inc(c_dve.sem, 1)
                    here(f"den{n}")
                    v.reciprocal(rden[:, 2 * n:2 * n + 2], den[:, 2 * n:2 * n + 2]).then_inc(c_dve.sem, 1)
                    here(f"rden{n}")
                    if n == 0 and not (isinstance(i, int) and i == 0):
                        dve.wait_ge(out_stored, 32 * i)
                    for t in tiles:
                        v.scalar_tensor_tensor(out=out_rows[:, t], in0=out_bank(t, final)[:, 0:D], scalar=rden[:, t:t + 1], in1=x3_rows[:, t],
                                               op0=ALU.mult, op1=ALU.add).then_inc(c_dve.sem, 1)

            step = [0]

            def link(ins):
                step[0] += 1
                ins.then_inc(par_step, 1)
                dve.wait_ge(par_step, step[0])

            def parameters(slot):
                par_v = par[:].rearrange("p (b n) -> p b n", n=NPAR)
                if slot == 0:
                    dve.wait_ge(small_in, 64)
                    link(v.tensor_reduce(gv_max[:], gate_vecs[:].rearrange("p (t e) -> p t e", e=NE), AX.X, ALU.max))
                    for t in range(NT):
                        ins = v.tensor_scalar(gate_prob[:, t * NE:(t + 1) * NE], gate_vecs[:, t * NE:(t + 1) * NE], gv_max[:, t:t + 1], None, ALU.subtract)
                    link(ins)
                if slot == 1:
                    dve.wait_ge(par_exp_done, 1)
                    link(v.tensor_reduce(gv_sum[:], gate_prob[:].rearrange("p (t e) -> p t e", e=NE), AX.X, ALU.add))
                    link(v.reciprocal(gv_sum[:], gv_sum[:]))
                    for t in range(NT):
                        ins = v.tensor_scalar(gate_prob[:, t * NE:(t + 1) * NE], gate_prob[:, t * NE:(t + 1) * NE],
                                              gv_sum[:, t:t + 1], None, ALU.mult)
                    link(ins)
                if slot == 2:
                    dve.wait_ge(types_in, 16)
                    link(v.tensor_copy(type_bc[:], type_bc_i[:]))
                    for t in range(NT):
                        ins = v.tensor_scalar(onehot[:, :, t], type_bc[:], float(t), None, ALU.is_equal)
                    link(ins)
                if slot == 3:
                    for e in range(2):
                        diag = gate_prob[:, e:e + (NT - 1) * (NE + 1) + 1:NE + 1]
                        for t in range(NT):
                            ins = v.tensor_scalar(pick[:, :, t], onehot[:, :, t], diag[:, t:t + 1], None, ALU.mult)
                        link(ins)
                        link(v.tensor_reduce(par_v[:, :, e:e + 1], pick[:], AX.X, ALU.add))
                if slot == 4:
                    v.tensor_tensor(par_v[:, :, 2], onehot[:, :, 1], onehot[:, :, 0], ALU.subtract)
                    for t in range(NT):
                        ins = v.tensor_scalar(par_v[:, :, 3 + t], onehot[:, :, t], -NEG, NEG, ALU.mult, ALU.add)
                    link(ins)
                if slot in (5, 6):
                    dve.wait_ge(rel_ready, 1)
                    for r in (2 * (slot - 5), 2 * (slot - 5) + 1):
                        cnt = par_v[:, :, 6 + r]
                        link(v.tensor_scalar(cnt, onehot[:, :, 0], jcol[:, 0, r:r + 1], None, ALU.mult))
                        link(v.scalar_tensor_tensor(out=cnt, in0=onehot[:, :, 1], scalar=jcol[:, 1, r:r + 1], in1=cnt, op0=ALU.mult, op1=ALU.add))
                        link(v.scalar_tensor_tensor(out=cnt, in0=onehot[:, :, 2], scalar=float(S - 1), in1=cnt, op0=ALU.mult, op1=ALU.add))

            def split_x2(b):
                for k in range(KD):
                    dve.wait_ge(x2_hi_ready, KD * b + k + 1)
                    v.tensor_tensor(x2T_lo[:, k], next_x2T[:, k], f32(x2T_hi[:, k]), ALU.subtract).then_inc(x2_lo_ready, 1)

            def evacuate(b, net):
                dve.wait_ge(net_chunk_done, b * SLOTS + (net + 1) * CH)
                if net == 1:
                    dve.wait_ge(evac_act, NG * b + 1)
                    both = netT[:, 0].rearrange("p k s -> p (k s)")
                    v.scalar_tensor_tensor(out=both, in0=ps_net[:, 1].rearrange("p k s -> p (k s)"), scalar=par_l2[:, 1:2], in1=both,
                                           op0=ALU.mult, op1=ALU.add).then_inc(evac_dve, 1)
                if net >= 2:
                    v.tensor_copy(netT[:, net - 1, 1], ps_net[:, net % 2, 1]).then_inc(evac_dve, 1)

            def batch(b, first, last):
                for q in range(SLOTS):
                    dve.wait_ge(hid_hi_ready, b * SLOTS + q + 1)
                    v.scalar_tensor_tensor(out=hid_lo[:, q % 2], in0=ps_hid[:, q % 2], scalar=0.0, in1=f32(hid_hi[:, q % 2]),
                                           op0=ALU.max, op1=ALU.subtract).then_inc(hid_lo_ready, 1)
                    if first:
                        parameters(q)
                    if q == CH - 1:
                        v.tensor_copy(par_l2[:], par[:, bass.ds(b * NPAR, NPAR)]).then_inc(par_l2_ready, 1)
                        dve.wait_ge(par_l2_ready, b + 1)
                    if not first:
                        stage_c(q, b - 1)
                    if not last:
                        stage_a(q, b + 1)
                    if q % CH == 0 and q >= 2 * CH:
                        evacuate(b, q // CH - 1)
                if not last:
                    split_x2(b + 1)
                evacuate(b, NETS - 1)

            v.memset(zeros[:], 0.0).then_inc(zeros_ready, 1)
            v.memset(ones[:], 1.0)
            v.memset(floor[:], NEG)
            v.memset(prefix_max[:, 0:1], NEG)
            v.memset(suffix_max[:, S:S + 1], NEG)
            v.memset(f32(val_hi[:, :, D:VW]), 1.0)
            v.memset(f32(val_lo[:, :, D:VW]), 0.0).then_inc(const_step, 1)
            dve.wait_ge(const_step, 1)
            for q in range(SLOTS):
                stage_a(q, 0)
            split_x2(0)
            batch(0, True, False)
            with dve.Fori(1, B - 1) as b:
                batch(b, False, False)
            batch(B - 1, False, True)
            for q in range(SLOTS):
                stage_c(q, B - 1, True)

        @block.gpsimd
        def _(pool):
            g = nc.gpsimd

            def stage_a(slot, i):
                if slot == A_SLOT["xT"]:
                    pool.wait_ge(a_dve.sem, a_dve.at(i, "w1_hi"))
                    g.tensor_tensor(w1_lo[:], w1[:], f32(w1_hi[:]), ALU.subtract).then_inc(a_pool.sem, 1)
                    pool.wait_ge(a_dve.sem, a_dve.at(i, "w2_hi"))
                    g.tensor_tensor(w2_lo[:], w2[:], f32(w2_hi[:]), ALU.subtract).then_inc(a_pool.sem, 1)
                if slot == A_SLOT["xT"] + 1:
                    pool.wait_ge(x_in, 16 * (i + 1))
                    pool.wait_ge(a_in, 64 * (i + 1))
                    for r in range(R):
                        ins = g.tensor_tensor(xb_rows[:, r], x_rows[:, r], b2_bc[:], ALU.add)
                    ins.then_inc(a_pool.sem, 1)
                if slot == A_SLOT["stats"]:
                    pool.wait_ge(a_dve.sem, a_dve.at(i, "var_eps"))
                    g.tensor_tensor(rstd[:], var_eps[:], half_pow[:], ALU.pow).then_inc(a_pool.sem, 1)

            def stage_c(slot, i, final=False):
                if slot == C_SLOT["arg"]:
                    pool.wait_ge(c_dve.sem, c_dve.at(i, "max3"))
                    g.tensor_tensor(prob[:, R - 1], mask[:, R - 1], max_row[:], ALU.subtract).then_inc(c_pool.sem, 1)
                if slot == C_SLOT["prob_lo"] + 1:
                    l = 1
                    pool.wait_ge(c_dve.sem, c_dve.at(i, f"phi{l}"))
                    g.tensor_tensor(prob_lo[:, l], prob[:, l], f32(prob_hi[:, l]), ALU.subtract).then_inc(c_pool.sem, 1)

            def split_weights(b, p):
                w, half = p % RING, p // HP
                pool.wait_ge(w_hi_ready, b * PAIRS + p + 1)
                c = slice((p % HP) * 2 * P, (p % HP + 1) * 2 * P)
                t = slice(2 * (p % HP), 2 * (p % HP) + 2)
                g.tensor_tensor(wi_lo[:, w], raw_wi[:, half % 2, :, c], f32(wi_hi[:, w]), ALU.subtract)
                g.tensor_tensor(wo_lo[:, w], raw_wo[:, half % 2, t], f32(wo_hi[:, w]), ALU.subtract).then_inc(w_lo_ready, 1)

            def batch(b, first, last):
                for q in range(SLOTS):
                    if q % 2 == 1:
                        p = q // 2 + AHEAD
                        if p < PAIRS:
                            split_weights(b, p)
                        elif not last:
                            split_weights(b + 1, p - PAIRS)
                    if not first:
                        stage_c(q, b - 1)
                    if not last:
                        stage_a(q, b + 1)
                    if q == A_SLOT["base"]:
                        pool.wait_ge(x2_lo_ready, KD * (b + 1))
                        if not first:
                            pool.wait_ge(c_pe.sem, c_pe.at(b - 1, "rows1"))
                        g.tensor_tensor(x3T[:], f32(x2T_hi[:]), f32(x2T_lo[:]), ALU.add).then_inc(base_ready, 1)

            g.memset(ident[:], 0.0).then_inc(const_ready, 1)
            pool.wait_ge(const_ready, 1)
            g.affine_select(out=ident[:], in_=ident[:], compare_op=ALU.not_equal, fill=1.0, base=0,
                            pattern=[[-1, P]], channel_multiplier=1).then_inc(const_ready, 1)
            g.memset(half_pow[:], -0.5)
            g.iota(jcol_i[:], pattern=[[P, R]], base=0, channel_multiplier=1).then_inc(const_ready, 1)
            pool.wait_ge(const_ready, 3)
            for q in range(SLOTS):
                stage_a(q, 0)
                if q in PRE_SPLIT:
                    split_weights(0, PRE_SPLIT.index(q))
            pool.wait_ge(small_in, 64)
            g.tensor_copy(att_v_bc[:], att_v[:].to_broadcast([A, P]))
            g.tensor_copy(att_w_hi[:], att_w[:]).then_inc(att_w_ready, 1)
            pool.wait_ge(att_w_ready, 1)
            g.tensor_tensor(att_w_lo[:], att_w[:], f32(att_w_hi[:]), ALU.subtract).then_inc(att_w_ready, 1)
            rel = prob[:].bitcast(I32)
            g.iota(rel, pattern=[[-P, R], [1, S]], base=0, channel_multiplier=-1).then_inc(const_ready, 1)
            pool.wait_ge(const_ready, 4)
            g.tensor_scalar(jcol[:, 0], jcol_i[:], 1.0, None, ALU.add)
            g.tensor_scalar(jcol[:, 1], jcol_i[:], -1.0, float(S), ALU.mult, ALU.add)
            g.tensor_scalar(rel_sign[:], rel, 1.0, -1.0, ALU.min, ALU.max).then_inc(rel_ready, 1)
            batch(0, True, False)
            with pool.Fori(1, B - 1) as b:
                batch(b, False, False)
            batch(B - 1, False, True)
            for q in range(SLOTS):
                stage_c(q, B - 1, True)


_INS = ["x", "itok_B_0_8", "itok_B_0_7", "itok_B_0_2",
        "L0_cond_W1", "L0_cond_b1", "L0_cond_W2", "L0_cond_b2", "L0_cond_gamma", "L0_cond_beta",
        "L1_cond_weight", "L1_cond_bias",
        "L2_cond_expert_wi", "L2_cond_expert_wo", "L2_cond_share_wi", "L2_cond_share_wo",
        "L2_cond_gate_vecs", "L2_cond_gate_w1", "L2_cond_gate_w2",
        "L3_cond_W1", "L3_cond_b1", "L3_cond_v"]


def kernel(**inputs):
    import numpy as _np
    import concourse.bacc as _bacc
    from concourse import mybir as _mybir
    from concourse.bass_utils import run_bass_kernel_spmd as _run

    nc = _bacc.Bacc("TRN2", target_bir_lowering=False, num_devices=1)
    arrays, args = {}, []
    for name in _INS:
        a = _np.ascontiguousarray(inputs[name])
        arrays[f"in_{name}_dram"] = a
        args.append(nc.dram_tensor(f"in_{name}_dram", a.shape, _mybir.dt.from_np(a.dtype), kind="ExternalInput").ap())
    shape = inputs["x"].shape
    args.append(nc.dram_tensor("out_0_dram", shape, _mybir.dt.float32, kind="ExternalOutput").ap())
    cond_resid_program(nc, *args)
    r = _run(nc, [arrays], core_ids=[0])
    return r.results[0]["out_0_dram"]
```

```python
from contextlib import ExitStack

import concourse.bass as bass
from concourse import mybir

ALU = mybir.AluOpType
ACT = mybir.ActivationFunctionType
AX = mybir.AxisListType
F32 = mybir.dt.float32
F32R = mybir.dt.float32r
BF16 = mybir.dt.bfloat16
I32 = mybir.dt.int32

P = 128
NEG = -1e30
LN_EPS = 1e-5
GATE_TEMP = 0.1


class Steps:

    def __init__(self, sem, names, first=0):
        self.sem, self.names, self.first = sem, names.split(), first

    def at(self, i, name):
        return i * len(self.names) + (self.names.index(name) + 1 - self.first * len(self.names))


def cond_resid_program(
    nc, x, lang_id, subj_id, type_id,
    L0_W1, L0_b1, L0_W2, L0_b2, L0_gamma, L0_beta,
    L1_weight, L1_bias,
    L2_expert_wi, L2_expert_wo, L2_share_wi, L2_share_wo, L2_gate_vecs, L2_gate_w1, L2_gate_w2,
    L3_W1, L3_b1, L3_v, out,
):
    B, S, D = x.shape
    KD = D // P
    R = S // P
    A = L0_W1.shape[2]
    F = L2_share_wi.shape[2]
    CH = F // P
    NETS = 2 + L2_share_wi.shape[0]
    NG = NETS - 1
    SLOTS = NETS * CH
    PAIRS = SLOTS // 2
    RING = 4
    AHEAD = RING - 1
    HALVES = 2 * NETS
    HP = CH // 4
    NT = L2_gate_vecs.shape[0]
    NE = L2_gate_vecs.shape[1]
    assert PAIRS % RING == 0 and HALVES % 2 == 0 and HP == 2

    A_SLOT = dict(xT=22, hid=24, subj_w=25, adapt=26, stats=27, xb=28, norm=28, normT=30, x1_hi=31, x1_lo=33, y=34, base=37)
    GATE_PART = SLOTS - (NG - 1)
    C_SLOT = dict(gate=1, logits=2, gates=3, comb=3, x3_split=5, rows=6, val=8, att=8, scores=10, prefix=11, suffix=12,
                  max=13, arg=14, exp=14, prob_hi=15, prob_lo=15, out=20)

    HS = S // 2
    HALF0_END = SLOTS - CH // 2 - 1
    END_BASE, END_GATE_PART, END_GATE = SLOTS // 2 + 2, SLOTS - CH + 1, HALF0_END + 2

    WARM_XT, WARM_HID, WARM_ADAPT, WARM_SUBJ, WARM_NORM, WARM_HALF, WARM_X2, WARM_OUT = 8, 2, 3, 9, 6, 12, 3, 6

    with ExitStack() as ctx:
        def sb(name, shape, dt=F32):
            return ctx.enter_context(nc.sbuf_tensor(name, shape, dt))

        def psum(name, shape):
            return ctx.enter_context(nc.psum_tensor(name, shape, F32))

        def sem(name):
            return ctx.enter_context(nc.semaphore(name))

        ident = sb("ident", [P, P])
        ones = sb("ones", [P, P])
        rel_sign = sb("rel_sign", [P, R, S], BF16)
        jcol_i = sb("jcol_i", [P, R], I32)
        jcol = sb("jcol", [P, 2, R])
        zeros = sb("zeros", [P, S], BF16)
        half_pow = sb("half_pow", [P, R])
        type_bc_i = sb("type_bc_i", [P, B], I32)
        type_bc = sb("type_bc", [P, B])
        gate_vecs = sb("gate_vecs", [P, NT * NE])
        gate_prob = sb("gate_prob", [P, NT * NE])
        gv_max = sb("gv_max", [P, NT])
        gv_sum = sb("gv_sum", [P, NT])
        onehot = sb("onehot", [P, B, NT])
        pick = sb("pick", [P, B, NT])
        NPAR = 6 + R
        par = sb("par", [P, B * NPAR])
        par_l2 = sb("par_l2", [P, NPAR])
        par_l3 = sb("par_l3", [P, NPAR])
        gate_w1 = sb("gate_w1", [P, NG * KD, D])
        gate_w2 = sb("gate_w2", [P, KD, NG])
        att_w = sb("att_w", [P, KD, A])
        att_w_hi = sb("att_w_hi", [P, KD, A], F32R)
        att_w_lo = sb("att_w_lo", [P, KD, A], F32R)
        att_b = sb("att_b", [A, 1])
        att_v = sb("att_v", [A, 1])
        att_v_bc = sb("att_v_bc", [A, P])

        x_rows = sb("x_rows", [P, R, D])
        w1 = sb("w1", [P, KD, A])
        w1_hi = sb("w1_hi", [P, KD, A], F32R)
        w1_lo = sb("w1_lo", [P, KD, A], F32R)
        w2 = sb("w2", [A + 1, D])
        w2_hi = sb("w2_hi", [A + 1, D], F32R)
        w2_lo = sb("w2_lo", [A + 1, D], F32R)
        b1 = sb("b1", [A, 1])
        gamma = sb("gamma", [P, KD])
        beta = sb("beta", [P, KD])
        subj_w = sb("subj_w", [P, KD, D])
        subj_wT_hi = sb("subj_wT_hi", [P, KD, D], F32R)
        subj_wT_lo = sb("subj_wT_lo", [P, KD, D], F32R)
        subj_b = sb("subj_b", [P, KD])
        xbT = sb("xbT", [P, KD, S])
        hT = sb("hT", [A, S])
        hT_hi = sb("hT_hi", [A + 1, S], F32R)
        hT_lo = sb("hT_lo", [A + 1, S], F32R)
        norm = sb("norm", [P, R, D])
        stats = sb("stats", [P, R, 6])
        mean = sb("mean", [P, R])
        mean_gap = sb("mean_gap", [P, R])
        var_eps = sb("var_eps", [P, R])
        rstd = sb("rstd", [P, R])
        x1T = sb("x1T", [P, KD, S])
        next_x2T = sb("next_x2T", [P, KD, S])
        opT_hi = sb("opT_hi", [P, KD, S], F32R)
        opT_lo = sb("opT_lo", [P, KD, S], F32R)

        x2T_hi = sb("x2T_hi", [P, KD, S], F32R)
        x2T_lo = sb("x2T_lo", [P, KD, S], F32R)
        raw_wi = sb("raw_wi", [P, 2, KD, F // 2])
        raw_wo = sb("raw_wo", [P, 2, CH // 2, D])
        wi_hi = sb("wi_hi", [P, RING, KD, 2 * P], F32R)
        wi_lo = sb("wi_lo", [P, RING, KD, 2 * P], F32R)
        wo_hi = sb("wo_hi", [P, RING, 2, D], F32R)
        wo_lo = sb("wo_lo", [P, RING, 2, D], F32R)
        hid_hi = sb("hid_hi", [P, 2, S], F32R)
        hid_lo = sb("hid_lo", [P, 2, S], F32R)
        netT = sb("netT", [P, NG, KD, S])

        x3T = sb("x3T", [P, KD, S])
        gate_h = sb("gate_h", [P, KD, P])
        neg_gmax = sb("neg_gmax", [P, 1])
        gate_e = sb("gate_e", [P, NG])
        gate_sum = sb("gate_sum", [P, 1])
        gate_rec = sb("gate_rec", [P, 1])
        gates = sb("gates", [P, NG])
        attT = sb("attT", [A, S])
        floor = sb("floor", [P, S])
        score_col = sb("score_col", [P, R])
        prefix_max = sb("prefix_max", [P, S + 1])
        suffix_max = sb("suffix_max", [P, S + 1])
        max_row = sb("max_row", [P, S])
        x3_rows = sb("x3_rows", [P, R, D])
        VW = D + 2
        val_hi = sb("val_hi", [P, R, VW], F32R)
        val_lo = sb("val_lo", [P, R, VW], F32R)
        par_end = sb("par_end", [P, NPAR])
        mask = sb("mask", [P, R, S], BF16)
        prob = sb("prob", [P, R, S])
        prob_hi = sb("prob_hi", [P, R, S], F32R)
        prob_lo = sb("prob_lo", [P, R, S], F32R)
        den = sb("den", [P, R])
        rden = sb("rden", [P, R])
        den_late = sb("den_late", [P, R])
        rden_late = sb("rden_late", [P, R])
        out_rows = sb("out_rows", [P, R, D])

        ps_hid = psum("ps_hid", [P, 2, S])
        ps_net = psum("ps_net", [P, 2, KD, S])
        ps_side = psum("ps_side", [P, 2, S])

        types_in, small_in, gate_in = sem("types_in"), sem("small_in"), sem("gate_in")
        x0_in = [sem("x0_in0"), sem("x0_in1")]
        x_in, w1_in, a_in, subj_in, out_stored = sem("x_in"), sem("w1_in"), sem("a_in"), sem("subj_in"), sem("out_stored")
        raw_in = [sem("raw_in0"), sem("raw_in1")]
        zeros_ready, const_ready, const_step, rel_ready, att_w_ready = (
            sem("zeros_ready"), sem("const_ready"), sem("const_step"), sem("rel_ready"), sem("att_w_ready"))
        par_step, par_exp_done, par_l2_ready = sem("par_step"), sem("par_exp_done"), sem("par_l2_ready")
        x2_hi_ready, x2_lo_ready = sem("x2_hi_ready"), sem("x2_lo_ready")
        w_hi_ready, w_lo_ready = sem("w_hi_ready"), sem("w_lo_ready")
        hid_done, hid_hi_ready, hid_lo_ready = sem("hid_done"), sem("hid_hi_ready"), sem("hid_lo_ready")
        net_chunk_done = sem("net_chunk_done")
        evac_act, evac_dve, base_ready = sem("evac_act"), sem("evac_dve"), sem("base_ready")

        a_pe = Steps(sem("a_pe"), "xT0 xT1 hid subj_wT adapt0 adapt1 normT0 normT1 y0 y1", 1)
        a_act = Steps(sem("a_act"), "xhi0 xhi1 hid subj_w_hi x1hi0 x1hi1", 1)
        a_dve = Steps(sem("a_dve"), "w1_hi xlo0 xlo1 w2_hi hid_hi hid_lo subj_w_lo sum0 sum1 stats sums mean var_eps "
                                    "xb0 xb1 norm x1T0 x1T1 x1lo0 x1lo1 x2T0 x2T1", 1)
        a_pool = Steps(sem("a_pool"), "w1_lo w2_lo rstd", 1)
        p_pe = Steps(sem("p_pe"), "xT0 xT1 hid0 hid1 adapt0 adapt1 subj_wT normT0 normT1 y0 y1")
        p_act = Steps(sem("p_act"), "xhi0 xhi1 hid0 hid1 xb0 xb1 subj_w_hi subj_w x1hi0 x1hi1")
        p_dve = Steps(sem("p_dve"), "w1_hi xlo0 xlo1 w2_hi hhi0 hlo0 hhi1 hlo1 sum0 stats0 sums0 mean0 var_eps0 sum1 norm0 "
                                    "stats1 sums1 mean1 var_eps1 x1T0 norm1 x1lo0 x1T1 x1lo1 x2T0 x2T1")
        p_pool = Steps(sem("p_pool"), "w1_lo w2_lo rstd0 rstd1 subj_w_lo")
        c_pe = Steps(sem("c_pe"), "gate_h logits rows0 rows1 att score_row score_col out0 out1 out2 out3")
        c_act = Steps(sem("c_act"), "gate_exp x3hi0 x3hi1 rows0 rows1 att score_col max0 exp0 exp1 exp2 exp3")
        c_dve = Steps(sem("c_dve"), "par mask gate_h gate_max gate_rec gates comb00 comb10 comb01 comb11 comb02 comb12 comb03 comb13 x3lo0 x3lo1 "
                                    "val_hi val_lo prefix suffix max1 max2 max3 "
                                    "arg0 arg1 arg2 phi0 plo0 phi1 phi2 plo2 phi3 plo3 "
                                    "den0 rden0 out0 out1 den1 rden1 out2 out3")
        c_pool = Steps(sem("c_pool"), "arg3 plo1")
        e_pe = Steps(sem("e_pe"), "gate_h logits rows0 att0 rows1 att1 score_row score_col out0 out1 out2 out3")
        e_act = Steps(sem("e_act"), "last0 gate_exp gated0 gated1 gated2 x3hi0 x3hi1 att0 rows0 att1 rows1 val_hi score_col max0 "
                                    "exp00 exp10 exp20 exp30 exp01 exp11 exp21 exp31 late0 late1 late2 late3")
        e_dve = Steps(sem("e_dve"), "par mask gate_h gate_max gate_rec gates comb0 comb1 comb2 comb3 last1 ones x3lo0 x3lo1 "
                                    "prefix suffix max10 max20 max30 arg00 arg10 arg20 max11 max21 max31 "
                                    "phi00 phi20 plo00 arg01 arg11 arg21 late_den late_rden phi01 plo01 phi21 plo21 "
                                    "den0 rden0 out0 out1 den1 rden1 out2 out3")
        e_pool = Steps(sem("e_pool"), "comb0 comb1 comb2 val_lo arg30 arg31 plo20 late0 late1 late2 late3")

        block = ctx.enter_context(nc.Block())

        def f32(ap):
            return ap.bitcast(F32)

        def c_steps(i, final):
            return (e_pe, e_act, e_dve, e_pool, 0) if final else (c_pe, c_act, c_dve, c_pool, i)

        def score_banks(final):
            return (ps_net[:, 1, 0], ps_net[:, 1, 1]) if final else (ps_side[:, 1], ps_side[:, 0])

        def pair_to_split(q, last):
            if last and q == SLOTS - CH:
                return PAIRS - 1
            return q // 2 + AHEAD if q % 2 == 1 and not (last and q > SLOTS - CH) else None

        def rows_half(h):
            return slice(h * HS, (h + 1) * HS)

        def chunks(q, last):
            if not (last and q >= SLOTS - CH):
                return [(q // 2, q % 2, slice(0, S), slice(0, S))]
            pair, rows = PAIRS - CH // 2 + q % (CH // 2), rows_half(int(q > HALF0_END))
            return [(pair, 0, rows, rows_half(0)), (pair, 1, rows, rows_half(1))]

        LATE = B - 2

        def values_in(weights):
            return weights.rearrange("p a b c -> p (a b c)")[:, 0:R * VW].rearrange("p (r w) -> p r w", w=VW)

        def c_buffers(final):
            return (par_end, x_rows, values_in(wi_hi[:]), values_in(wi_lo[:])) if final else (par_l3, x3_rows, val_hi, val_lo)

        def out_bank(t, mode):
            if mode == "late":
                return ps_net[:, t // 2, t % 2, 0:VW]
            if mode == "final" and t >= 2:
                return ps_hid[:, t - 2, 0:VW]
            return ps_side[:, t % 2, 0:VW]

        @block.sync
        def _(sp):
            lang_row, subj_row, type_row = (a.rearrange("(o b) -> o b", o=1) for a in (lang_id, subj_id, type_id))

            def load_x(i):
                sp.dma_start(x_rows[:], x[bass.ds(i, 1)].rearrange("o (r p) d -> p (o r) d", p=P)).then_inc(x_in, 16)

            def load_params(i):
                lang = sp.value_load(lang_row[0:1, bass.ds(i, 1)], min_val=0, max_val=L0_W1.shape[0] - 1)
                la = bass.ds(lang, 1)
                with nc.allow_non_contiguous_dma(reason="a few vectors, one element to a partition"):
                    sp.dma_start(w1[:], L0_W1[la].rearrange("o (k p) a -> p (o k) a", p=P)).then_inc(w1_in, 16)
                    sp.dma_start(b1[:], L0_b1[la].rearrange("o a -> a o")).then_inc(w1_in, 16)
                    sp.dma_start(w2[0:A], L0_W2[la].rearrange("o a d -> (o a) d")).then_inc(a_in, 16)
                    sp.dma_start(w2[A:A + 1], L0_b2[la]).then_inc(a_in, 16)
                    sp.dma_start(gamma[:], L0_gamma[la].rearrange("o (k p) -> p (o k)", p=P)).then_inc(a_in, 16)
                    sp.dma_start(beta[:], L0_beta[la].rearrange("o (k p) -> p (o k)", p=P)).then_inc(a_in, 16)
                    subj = sp.value_load(subj_row[0:1, bass.ds(i, 1)], min_val=0, max_val=L1_weight.shape[0] - 1)
                    su = bass.ds(subj, 1)
                    sp.dma_start(subj_w[:], L1_weight[su].rearrange("o (k p) d -> p (o k) d", p=P)).then_inc(subj_in, 16)
                    sp.dma_start(subj_b[:], L1_bias[su].rearrange("o (k p) -> p (o k)", p=P)).then_inc(subj_in, 16)

            def load_resident():
                sp.dma_start(type_bc_i[:], type_id.rearrange("(o b) -> o b", o=1).to_broadcast([P, B])).then_inc(types_in, 16)
                sp.dma_start(gate_vecs[:], L2_gate_vecs.rearrange("(o t) e -> o (t e)", o=1).to_broadcast([P, NT * NE])).then_inc(small_in, 16)
                with nc.allow_non_contiguous_dma(reason="two vectors, one element to a partition"):
                    sp.dma_start(att_b[:], L3_b1.rearrange("(a o) -> a o", o=1)).then_inc(small_in, 16)
                    sp.dma_start(att_v[:], L3_v.rearrange("(a o) -> a o", o=1)).then_inc(small_in, 16)
                sp.dma_start(att_w[:], L3_W1.rearrange("(k p) a -> p k a", p=P)).then_inc(small_in, 16)
                sp.dma_start(gate_w2[:], L2_gate_w2.rearrange("(k p) g -> p k g", p=P)).then_inc(gate_in, 16)
                sp.dma_start(gate_w1[:], L2_gate_w1.rearrange("(c p) d -> p c d", p=P)).then_inc(gate_in, 16)

            def load_half(b, h, kind):
                slot, net, part = h % 2, h // 2, h % 2
                if not (isinstance(b, int) and b == 0 and h < 2):
                    sp.wait_ge(w_lo_ready, b * PAIRS + HP * (h - 1))
                cols = slice(part * (F // 2), (part + 1) * (F // 2))
                if net < 2:
                    e = bass.ds(kind + net, 1)
                    wi, wo = L2_expert_wi[e, :, cols], L2_expert_wo[e, cols]
                else:
                    wi, wo = L2_share_wi[net - 2:net - 1, :, cols], L2_share_wo[net - 2:net - 1, cols]
                sp.dma_start(raw_wi[:, slot], wi.rearrange("o (k p) f -> p (o k) f", p=P)).then_inc(raw_in[slot], 16)
                sp.dma_start(raw_wo[:, slot], wo.rearrange("o (c p) d -> p (o c) d", p=P)).then_inc(raw_in[slot], 16)

            def store(i, half, final=False):
                _, _, dve_s, _, n = c_steps(i, final)
                sp.wait_ge(dve_s.sem, dve_s.at(n, f"out{2 * half + 1}"))
                store_rows(i, half, out_rows)

            def store_rows(i, half, src):
                rows = slice(half * (S // 2), (half + 1) * (S // 2))
                sp.dma_start(out[bass.ds(i, 1), rows].rearrange("o (r p) d -> p (o r) d", p=P),
                             src[:, 2 * half:2 * half + 2]).then_inc(out_stored, 16)

            def batch(b, first, last):
                kind = sp.value_load(type_row[0:1, bass.ds(b, 1)], min_val=0, max_val=NT - 1)
                for h in range(HALVES):
                    if not (first and h == 0):
                        load_half(b, h, kind)
                    if first and h == 1:
                        load_resident()
                    if h == 4 and not last:
                        if first:
                            sp.wait_ge(p_dve.sem, p_dve.at(0, "x2T1"))
                        else:
                            sp.wait_ge(a_dve.sem, a_dve.at(b, "x2T1"))
                        load_x(b + 1)
                        load_params(b + 1)
                    if h == 8 and not first and not last:
                        for half in range(2):
                            store(b - 1, half)

            for h in range(2):
                rows = slice(h * R // 2, (h + 1) * R // 2)
                sp.dma_start(x_rows[:, rows], x[0:1, rows_half(h)].rearrange("o (r p) d -> p (o r) d", p=P)).then_inc(x0_in[h], 16)
            load_params(0)
            batch(0, True, False)
            with sp.Fori(1, B - 1) as b:
                batch(b, False, False)
            batch(B - 1, False, True)
            for half in range(2):
                sp.wait_ge(e_pool.sem, e_pool.at(0, f"late{2 * half + 1}"))
                store_rows(LATE, half, norm)
                store(B - 1, half, True)
            sp.wait_ge(out_stored, 32 * B)

        @block.tensor
        def _(pe):
            mm = nc.tensor.matmul

            def product(dst, pairs, before_lo=None, before_last_hi=None):
                for t, (lh, ll, rh, _) in enumerate(pairs):
                    if before_last_hi and t == len(pairs) - 1:
                        pe.wait_ge(*before_last_hi)
                    mm(dst, ll, rh, start=(t == 0), stop=False)
                    mm(dst, lh, rh, start=False, stop=False)
                if before_lo:
                    pe.wait_ge(*before_lo)
                for t, (lh, _, _, rl) in enumerate(pairs):
                    last = mm(dst, lh, rl, start=False, stop=(t == len(pairs) - 1))
                return last

            def transpose_half(bank, src, h):
                for k in range(KD):
                    for r in range(R // 2):
                        c = k * HS + r * P
                        last = nc.tensor.transpose(bank[:, c:c + P], src[:, h * R // 2 + r, k * P:(k + 1) * P], ident[:])
                return last

            def transpose_subj(bank):
                for k in range(KD):
                    for o in range(KD):
                        c = k * D + o * P
                        last = nc.tensor.transpose(bank[:, c:c + P], subj_w[:, o, k * P:(k + 1) * P], ident[:])
                return last

            def adapt_half(bank, h):
                for r in (2 * h, 2 * h + 1):
                    c = slice((r % 2) * D, (r % 2 + 1) * D)
                    rows = slice(r * P, (r + 1) * P)
                    last = product(bank[:, c], [(hT_hi[:, rows], hT_lo[:, rows], w2_hi[:], w2_lo[:])])
                return last

            def stage_a(slot, i, after_c):
                if 0 <= slot - A_SLOT["xT"] < KD:
                    k = slot - A_SLOT["xT"]
                    if k == 0:
                        pe.wait_ge(x_in, 16 * i)
                    if after_c:
                        pe.wait_ge(c_dve.sem, c_dve.at(i - 2, "out3"))
                    for r in range(R):
                        last = nc.tensor.transpose(ps_side[:, k, r * P:(r + 1) * P], x_rows[:, r, k * P:(k + 1) * P], ident[:])
                    last.then_inc(a_pe.sem, 1)
                if slot == A_SLOT["subj_w"]:
                    pe.wait_ge(subj_in, 32 * (i + 1))
                    pe.wait_ge(a_dve.sem, a_dve.at(i, "xlo1"))
                    transpose_subj(ps_side[:, 1]).then_inc(a_pe.sem, 1)
                if slot == A_SLOT["hid"]:
                    pe.wait_ge(a_act.sem, a_act.at(i, "xhi1"))
                    pe.wait_ge(a_dve.sem, a_dve.at(i, "xlo0"))
                    pe.wait_ge(a_pool.sem, a_pool.at(i, "w1_lo"))
                    product(ps_side[0:A, 0], [(w1_hi[:, k], w1_lo[:, k], opT_hi[:, k], opT_lo[:, k]) for k in range(KD)],
                            (a_dve.sem, a_dve.at(i, "xlo1"))).then_inc(a_pe.sem, 1)
                if slot == A_SLOT["adapt"]:
                    for t in range(2):
                        if t == 0:
                            pe.wait_ge(a_pool.sem, a_pool.at(i, "w2_lo"))
                            pe.wait_ge(a_dve.sem, a_dve.at(i, "hid_lo"))
                        else:
                            pe.wait_ge(a_dve.sem, a_dve.at(i, "subj_w_lo"))
                        adapt_half(ps_side[:, t], t).then_inc(a_pe.sem, 1)
                if 0 <= slot - A_SLOT["normT"] < KD:
                    k = slot - A_SLOT["normT"]
                    pe.wait_ge(a_dve.sem, a_dve.at(i, "norm"))
                    for r in range(R):
                        last = nc.tensor.transpose(ps_side[:, k, r * P:(r + 1) * P], norm[:, r, k * P:(k + 1) * P], ident[:])
                    last.then_inc(a_pe.sem, 1)
                if 0 <= slot - A_SLOT["y"] < KD:
                    o = slot - A_SLOT["y"]
                    pe.wait_ge(a_act.sem, a_act.at(i, "x1hi0"))
                    product(ps_side[:, o], [(subj_wT_hi[:, k, o * P:(o + 1) * P], subj_wT_lo[:, k, o * P:(o + 1) * P],
                                             opT_hi[:, k], opT_lo[:, k]) for k in range(KD)],
                            (a_dve.sem, a_dve.at(i, "x1lo1")), (a_act.sem, a_act.at(i, "x1hi1"))).then_inc(a_pe.sem, 1)

            def prologue():
                warm = ps_net[:, 1, 1]
                pe.wait_ge(zeros_ready, 1)
                keep_warm(WARM_XT, warm)
                pe.wait_ge(const_ready, 2)
                for h in range(2):
                    pe.wait_ge(x0_in[h], 16)
                    transpose_half(ps_side[:, h], x_rows, h).then_inc(p_pe.sem, 1)
                keep_warm(WARM_HID, warm)
                for h in range(2):
                    rows = rows_half(h)
                    pe.wait_ge(p_act.sem, p_act.at(0, f"xhi{h}"))
                    pe.wait_ge(p_pool.sem, p_pool.at(0, "w1_lo"))
                    product(ps_hid[0:A, h, 0:HS], [(w1_hi[:, k], w1_lo[:, k], opT_hi[:, k, rows], opT_lo[:, k, rows]) for k in range(KD)],
                            (p_dve.sem, p_dve.at(0, f"xlo{h}"))).then_inc(p_pe.sem, 1)
                keep_warm(WARM_ADAPT, warm)
                for h in range(2):
                    pe.wait_ge(p_pool.sem, p_pool.at(0, "w2_lo"))
                    pe.wait_ge(p_dve.sem, p_dve.at(0, f"hlo{h}"))
                    adapt_half(ps_net[:, 0, h], h).then_inc(p_pe.sem, 1)
                keep_warm(WARM_SUBJ, warm)
                pe.wait_ge(subj_in, 32)
                transpose_subj(ps_net[:, 1, 0]).then_inc(p_pe.sem, 1)
                keep_warm(WARM_NORM, warm)
                for h in range(2):
                    if h == 1:
                        keep_warm(WARM_HALF, warm)
                    pe.wait_ge(p_dve.sem, p_dve.at(0, f"norm{h}"))
                    pe.wait_ge(p_act.sem, p_act.at(0, f"xb{h}"))
                    transpose_half(ps_side[:, h], norm, h).then_inc(p_pe.sem, 1)
                for h in range(2):
                    rows = rows_half(h)
                    pe.wait_ge(p_act.sem, p_act.at(0, f"x1hi{h}"))
                    pe.wait_ge(p_pool.sem, p_pool.at(0, "subj_w_lo"))
                    for o in range(KD):
                        cols = slice(o * P, (o + 1) * P)
                        last = product(ps_hid[:, h, o * HS:(o + 1) * HS],
                                       [(subj_wT_hi[:, k, cols], subj_wT_lo[:, k, cols], opT_hi[:, k, rows], opT_lo[:, k, rows]) for k in range(KD)],
                                       (p_dve.sem, p_dve.at(0, f"x1lo{h}")))
                    last.then_inc(p_pe.sem, 1)

            def keep_warm(n, bank):
                for _ in range(n):
                    mm(bank, zeros[:, 0:P], zeros[:], start=True, stop=True)

            def nets_in_sbuf(i, nets):
                pe.wait_ge(evac_act, NG * i + nets)
                pe.wait_ge(evac_dve, NG * i + nets)

            def gate_terms(first_net, end_net):
                if first_net == 0:
                    pe.wait_ge(gate_in, 32)
                for o in range(KD):
                    for c in range(first_net * KD, end_net * KD):
                        last = mm(ps_side[:, 0, o:o + 1], gate_w1[:, c, o * P:(o + 1) * P], netT[:, c // KD, c % KD, 0:1],
                                  start=(o == 0 and c == 0), stop=(c == NG * KD - 1), skip_group_check=True)
                return last

            def gate_logits():
                for o in range(KD):
                    last = mm(ps_side[:, 1, 0:NG], gate_h[:, o], gate_w2[:, o], start=(o == 0), stop=(o == KD - 1))
                return last

            def transpose_rows(t):
                for r in (2 * t, 2 * t + 1):
                    for k in range(KD):
                        c = (r % 2) * D + k * P
                        last = nc.tensor.transpose(ps_side[:, t, c:c + P], x3T[:, k, r * P:(r + 1) * P], ident[:])
                return last

            def stage_c(slot, i):
                if slot == C_SLOT["gate"]:
                    nets_in_sbuf(i, NG)
                    gate_terms(NG - 1, NG).then_inc(c_pe.sem, 1)
                if slot == C_SLOT["logits"]:
                    pe.wait_ge(c_dve.sem, c_dve.at(i, "gate_h"))
                    gate_logits().then_inc(c_pe.sem, 1)
                if 0 <= slot - C_SLOT["rows"] < 2:
                    t = slot - C_SLOT["rows"]
                    if t == 0:
                        pe.wait_ge(c_dve.sem, c_dve.at(i, "comb13"))
                    transpose_rows(t).then_inc(c_pe.sem, 1)
                if slot == C_SLOT["att"]:
                    pe.wait_ge(att_w_ready, 2)
                    pe.wait_ge(c_act.sem, c_act.at(i, "rows0"))
                    product(ps_side[0:A, 0], [(att_w_hi[:, k], att_w_lo[:, k], opT_hi[:, k], opT_lo[:, k]) for k in range(KD)],
                            (c_dve.sem, c_dve.at(i, "x3lo1"))).then_inc(c_pe.sem, 1)
                attention(slot, i, False)

            def attention(slot, i, final):
                pe_s, act_s, dve_s, pool_s, n = c_steps(i, final)
                if slot == C_SLOT["scores"]:
                    pe.wait_ge(act_s.sem, act_s.at(n, "att1" if final else "att"))
                    row, col = score_banks(final)
                    mm(row, att_v_bc[:], attT[:], start=True, stop=True).then_inc(pe_s.sem, 1)
                    for r in range(R):
                        last = mm(col[:, r:r + 1], attT[:, r * P:(r + 1) * P], att_v[:], start=True, stop=True)
                    last.then_inc(pe_s.sem, 1)
                if 0 <= slot - C_SLOT["out"] < 2 and not final:
                    t = 2 * (slot - C_SLOT["out"])
                    pooled((t, t + 1), i, "loop")

            def pooled(tiles, i, mode, score_tiles=range(R)):
                pe_s, _, dve_s, pool_s, n = c_steps(i, False)
                _, _, vh, vl = c_buffers(False)
                for l in score_tiles:
                    if tiles[0] == 0 and mode != "late":
                        pe.wait_ge(dve_s.sem, dve_s.at(n, f"phi{l}"))
                    for t in tiles:
                        if l == 0 and tiles[0] == 2 and mode == "loop":
                            pe.wait_ge(dve_s.sem, dve_s.at(n, f"out{t - 2}"))
                        hi = prob_hi[:, l, t * P:(t + 1) * P]
                        mm(out_bank(t, mode), hi, vh[:, l], start=(l == 0), stop=False)
                        mm(out_bank(t, mode), hi, vl[:, l], start=False, stop=False)
                    if tiles[0] == 0:
                        by = pool_s if l == 1 else dve_s
                        pe.wait_ge(by.sem, by.at(n, f"plo{l}"))
                    for t in tiles:
                        last = mm(out_bank(t, mode), prob_lo[:, l, t * P:(t + 1) * P], vh[:, l], start=False, stop=(l == R - 1))
                        if l == R - 1:
                            last.then_inc(pe_s.sem, 1)

            def last_pooled():
                _, _, vh, vl = c_buffers(True)
                pe.wait_ge(e_pool.sem, e_pool.at(0, "val_lo"))
                for h, order in enumerate(["hi0 hi2 lo0 lo2", "hi0 lo0 hi2 lo2"]):
                    for part in order.split():
                        l0 = int(part[2])
                        terms = [(t, l, slice(t * P, (t + 1) * P)) for l in (l0, l0 + 1) for t in (2 * h, 2 * h + 1)]
                        if part[:2] == "hi":
                            pe.wait_ge(e_dve.sem, e_dve.at(0, f"phi{l0}{h}"))
                            for t, l, rows in terms:
                                mm(out_bank(t, "final"), prob_hi[:, l, rows], vh[:, l], start=(l == 0), stop=False)
                                mm(out_bank(t, "final"), prob_hi[:, l, rows], vl[:, l], start=False, stop=False)
                        else:
                            by = e_pool if (l0, h) == (2, 0) else e_dve
                            pe.wait_ge(by.sem, by.at(0, f"plo{l0}{h}"))
                            for t, l, rows in terms:
                                last = mm(out_bank(t, "final"), prob_lo[:, l, rows], vh[:, l], start=False, stop=(l == R - 1))
                                if l == R - 1:
                                    last.then_inc(e_pe.sem, 1)

            def late_pooled():
                pooled((1,), LATE, "late")
                pe.wait_ge(e_dve.sem, e_dve.at(0, "suffix"))
                pe.wait_ge(e_act.sem, e_act.at(0, "score_col"))
                pooled((2, 3), LATE, "late")

            def last_gates(slot):
                if slot == END_GATE:
                    pe.wait_ge(e_act.sem, e_act.at(0, "last0"))
                    gate_terms(NG - 1, NG).then_inc(e_pe.sem, 1)
                if slot == END_GATE + 1:
                    pe.wait_ge(e_dve.sem, e_dve.at(0, "gate_h"))
                    gate_logits().then_inc(e_pe.sem, 1)

            def last_rows():
                for h in range(2):
                    pe.wait_ge(e_dve.sem, e_dve.at(0, "last1" if h else "comb3"))
                    transpose_rows(h).then_inc(e_pe.sem, 1)
                    pe.wait_ge(att_w_ready, 2)
                    pe.wait_ge(e_act.sem, e_act.at(0, f"x3hi{h}"))
                    rows = rows_half(h)
                    if h == 0:
                        pooled((0,), LATE, "late", range(0, R // 2))
                    product(ps_hid[0:A, h, 0:HS], [(att_w_hi[:, k], att_w_lo[:, k], opT_hi[:, k, rows], opT_lo[:, k, rows]) for k in range(KD)],
                            (e_dve.sem, e_dve.at(0, f"x3lo{h}"))).then_inc(e_pe.sem, 1)
                pooled((0,), LATE, "late", range(R // 2, R))

            def first_product(b, q, first, halved):
                tiles = chunks(q, halved)
                by_rows = first and q == 0
                if by_rows:
                    tiles = [(0, 0, rows_half(h), rows_half(h)) for h in range(2)]
                if len(tiles) == 2 or q % 2 == 0:
                    pe.wait_ge(w_lo_ready, b * PAIRS + tiles[0][0] + 1)
                if not (first and q < 2):
                    pe.wait_ge(hid_lo_ready, b * SLOTS + q - 1)
                for t, (pair, n, rows, cols) in enumerate(tiles):
                    w, c = pair % RING, slice(n * P, (n + 1) * P)
                    dst = ps_hid[:, q % 2, cols]
                    for k in range(KD):
                        if q == 0:
                            pe.wait_ge(x2_hi_ready, KD * b + (t if by_rows else k) + 1)
                        mm(dst, wi_lo[:, w, k, c], x2T_hi[:, k, rows], start=(k == 0), stop=False)
                        mm(dst, wi_hi[:, w, k, c], x2T_hi[:, k, rows], start=False, stop=False)
                    for k in range(KD):
                        if q == 0:
                            pe.wait_ge(x2_lo_ready, KD * b + (t if by_rows else k) + 1)
                        last = mm(dst, wi_hi[:, w, k, c], x2T_lo[:, k, rows], start=False, stop=(k == KD - 1))
                last.then_inc(hid_done, 1)

            def second_product_halved(b, q):
                net, tiles, c = q // CH, chunks(q, True), q % (CH // 2)
                if q == SLOTS - CH:
                    pe.wait_ge(evac_act, NG * b + net - 2)
                    pe.wait_ge(evac_dve, NG * b + net - 2)
                w, half = tiles[0][0] % RING, int(q > HALF0_END)

                def term(wo, hid, n, k, start=False, stop=False):
                    return mm(ps_net[:, net % 2, half, k * HS:(k + 1) * HS], wo[:, w, n, k * P:(k + 1) * P], hid[:, q % 2, tiles[n][3]],
                              start=start, stop=stop, skip_group_check=True)

                pe.wait_ge(hid_hi_ready, b * SLOTS + q + 1)
                for n in range(2):
                    for k in range(KD):
                        term(wo_hi, hid_hi, n, k, start=(c == 0 and n == 0 and k == 0))
                        term(wo_lo, hid_hi, n, k)
                pe.wait_ge(hid_lo_ready, b * SLOTS + q + 1)
                for n in range(2):
                    for k in range(KD):
                        last = term(wo_hi, hid_lo, n, k, stop=(c == CH // 2 - 1 and n == 1))
                last.then_inc(net_chunk_done, 1)

            def second_product(b, q, first, halved):
                if halved and q >= SLOTS - CH:
                    return second_product_halved(b, q)
                net, c = q // CH, q % CH
                if c == 0:
                    if net == 0 and not first:
                        pe.wait_ge(evac_act, NG * b)
                        pe.wait_ge(evac_dve, NG * b)
                    if net == 2:
                        pe.wait_ge(evac_act, NG * b + 1)
                    if net >= 3:
                        pe.wait_ge(evac_act, NG * b + net - 2)
                        pe.wait_ge(evac_dve, NG * b + net - 2)
                pe.wait_ge(hid_hi_ready, b * SLOTS + q + 1)
                w = (q // 2) % RING
                for k in range(KD):
                    cols = slice(k * P, (k + 1) * P)
                    mm(ps_net[:, net % 2, k], wo_hi[:, w, q % 2, cols], hid_hi[:, q % 2], start=(c == 0), stop=False)
                    mm(ps_net[:, net % 2, k], wo_lo[:, w, q % 2, cols], hid_hi[:, q % 2], start=False, stop=False)
                pe.wait_ge(hid_lo_ready, b * SLOTS + q + 1)
                for k in range(KD):
                    cols = slice(k * P, (k + 1) * P)
                    last = mm(ps_net[:, net % 2, k], wo_hi[:, w, q % 2, cols], hid_lo[:, q % 2], start=False, stop=(c == CH - 1))
                last.then_inc(net_chunk_done, 1)

            def batch(b, first, last):
                for q in range(SLOTS):
                    first_product(b, q, first, last)
                    if not first and not (last and q >= C_SLOT["out"]):
                        stage_c(q, b - 1)
                    if not last:
                        stage_a(q, b + 1, not first)
                    net = q - (END_GATE_PART if last else GATE_PART)
                    if 0 <= net < NG - 1:
                        if net == 0 and not last:
                            pe.wait_ge(a_dve.sem, a_dve.at(b + 1, "x2T0"))
                        nets_in_sbuf(b, net + 1)
                        gate_terms(net, net + 1)
                    if last and q == END_GATE:
                        last_gates(q)
                    if q >= 1:
                        second_product(b, q - 1, first, last)
                    if last and q == END_GATE:
                        last_gates(q + 1)
                second_product(b, SLOTS - 1, first, last)

            prologue()
            keep_warm(WARM_X2, ps_net[:, 1, 1])
            batch(0, True, False)
            with pe.Fori(1, B - 1) as b:
                batch(b, False, False)
            batch(B - 1, False, True)
            last_rows()
            attention(C_SLOT["scores"], B - 1, True)
            late_pooled()
            keep_warm(WARM_OUT, ps_side[:, 1])
            last_pooled()

        @block.scalar
        def _(act):
            fn = nc.scalar.activation

            def stage_a(slot, i, after_c):
                if 0 <= slot - A_SLOT["xT"] < KD:
                    k = slot - A_SLOT["xT"]
                    act.wait_ge(a_pe.sem, a_pe.at(i, f"xT{k}"))
                    if after_c:
                        act.wait_ge(c_pe.sem, c_pe.at(i - 2, "att"))
                    fn(opT_hi[:, k], ps_side[:, k], ACT.Copy).then_inc(a_act.sem, 1)
                if slot == A_SLOT["hid"]:
                    act.wait_ge(a_pe.sem, a_pe.at(i, "hid"))
                    fn(hT[:], ps_side[0:A, 0], ACT.Relu, bias=b1[:]).then_inc(a_act.sem, 1)
                if slot == A_SLOT["subj_w"]:
                    act.wait_ge(a_pe.sem, a_pe.at(i, "subj_wT"))
                    fn(subj_wT_hi[:].rearrange("p k d -> p (k d)"), ps_side[:, 1], ACT.Copy).then_inc(a_act.sem, 1)
                if 0 <= slot - A_SLOT["x1_hi"] < KD:
                    k = slot - A_SLOT["x1_hi"]
                    act.wait_ge(a_dve.sem, a_dve.at(i, f"x1T{k}"))
                    fn(opT_hi[:, k], x1T[:, k], ACT.Copy).then_inc(a_act.sem, 1)

            def stage_c(slot, i):
                if slot == C_SLOT["logits"]:
                    act.wait_ge(c_dve.sem, c_dve.at(i, "gate_max"))
                    fn(gate_e[:], ps_side[:, 1, 0:NG], ACT.Exp, bias=neg_gmax[:], accum_out=gate_sum[:]).then_inc(c_act.sem, 1)
                if slot == C_SLOT["x3_split"]:
                    for k in range(KD):
                        act.wait_ge(c_dve.sem, c_dve.at(i, f"comb{k}3"))
                        fn(opT_hi[:, k], x3T[:, k], ACT.Copy).then_inc(c_act.sem, 1)
                if 0 <= slot - C_SLOT["rows"] < 2:
                    t = slot - C_SLOT["rows"]
                    act.wait_ge(c_pe.sem, c_pe.at(i, f"rows{t}"))
                    copy_rows(t, x3_rows).then_inc(c_act.sem, 1)
                if slot == C_SLOT["att"]:
                    act.wait_ge(c_pe.sem, c_pe.at(i, "att"))
                    fn(attT[:], ps_side[0:A, 0], ACT.Tanh, bias=att_b[:]).then_inc(c_act.sem, 1)
                attention(slot, i, False)

            def attention(slot, i, final):
                pe_s, act_s, dve_s, pool_s, n = c_steps(i, final)
                if slot == C_SLOT["scores"]:
                    act.wait_ge(pe_s.sem, pe_s.at(n, "score_col"))
                    fn(score_col[:], score_banks(final)[1][:, 0:R], ACT.Copy).then_inc(act_s.sem, 1)
                if slot == C_SLOT["suffix"]:
                    act.wait_ge(dve_s.sem, dve_s.at(n, "prefix"))
                    fn(max_row[:], prefix_max[:, 1:S + 1], ACT.Identity, bias=c_buffers(final)[0][:, 3:4]).then_inc(act_s.sem, 1)
                if 0 <= slot - C_SLOT["exp"] < R:
                    l = slot - C_SLOT["exp"]
                    act.wait_ge(act_s.sem, act_s.at(n, "score_col"))
                    by = dve_s if l < R - 1 else pool_s
                    act.wait_ge(by.sem, by.at(n, f"arg{l}"))
                    fn(prob[:, l], prob[:, l], ACT.Exp, bias=score_col[:, l:l + 1]).then_inc(act_s.sem, 1)

            def copy_rows(t, dst):
                return fn(dst[:, 2 * t:2 * t + 2].rearrange("p r d -> p (r d)"), ps_side[:, t], ACT.Copy)

            def last_gates(slot):
                if slot == END_GATE - 1:
                    act.wait_ge(net_chunk_done, (B - 1) * SLOTS + HALF0_END + 1)
                    fn(netT[:, NG - 1, :, 0:HS], ps_net[:, (NETS - 1) % 2, 0].rearrange("p (k s) -> p k s", k=KD), ACT.Copy).then_inc(e_act.sem, 1)
                if slot == END_GATE:
                    act.wait_ge(e_dve.sem, e_dve.at(0, "gate_max"))
                    fn(gate_e[:], ps_side[:, 1, 0:NG], ACT.Exp, bias=neg_gmax[:], accum_out=gate_sum[:]).then_inc(e_act.sem, 1)
                if slot == END_GATE + 1:
                    act.wait_ge(e_dve.sem, e_dve.at(0, "gates"))
                    for n in range(NG - 1):
                        half = netT[:, n, :, rows_half(1)]
                        fn(half, half, ACT.Copy, scale=gates[:, n:n + 1]).then_inc(e_act.sem, 1)

            def last_rows():
                _, x3_end, vh, _ = c_buffers(True)
                for h in range(2):
                    act.wait_ge(e_dve.sem, e_dve.at(0, "last1" if h else "comb3"))
                    fn(opT_hi[:, :, rows_half(h)], x3T[:, :, rows_half(h)], ACT.Copy).then_inc(e_act.sem, 1)
                for h in range(2):
                    act.wait_ge(e_pe.sem, e_pe.at(0, f"att{h}"))
                    fn(attT[:, rows_half(h)], ps_hid[0:A, h, 0:HS], ACT.Tanh, bias=att_b[:]).then_inc(e_act.sem, 1)
                    act.wait_ge(e_pe.sem, e_pe.at(0, f"rows{h}"))
                    copy_rows(h, x3_end).then_inc(e_act.sem, 1)
                act.wait_ge(e_act.sem, e_act.at(0, "rows1"))
                fn(vh[:, :, 0:D], x3_end[:], ACT.Copy).then_inc(e_act.sem, 1)

            def split_weights(b, p, free):
                w, half = p % RING, p // HP
                act.wait_ge(raw_in[half % 2], 32 * ((HALVES // 2) * b + half // 2 + 1))
                if free:
                    act.wait_ge(net_chunk_done, b * SLOTS + 2 * (p - RING) + 2)
                c = slice((p % HP) * 2 * P, (p % HP + 1) * 2 * P)
                fn(wi_hi[:, w], raw_wi[:, half % 2, :, c], ACT.Copy)
                fn(wo_hi[:, w], raw_wo[:, half % 2, 2 * (p % HP):2 * (p % HP) + 2], ACT.Copy).then_inc(w_hi_ready, 1)

            def split_x2(b):
                for k in range(KD):
                    act.wait_ge(a_dve.sem, a_dve.at(b, f"x2T{k}"))
                    fn(x2T_hi[:, k], next_x2T[:, k], ACT.Copy).then_inc(x2_hi_ready, 1)

            def evacuate(b, net):
                act.wait_ge(net_chunk_done, b * SLOTS + (net + 1) * CH)
                if net == 0:
                    act.wait_ge(par_l2_ready, b + 1)
                    if not (isinstance(b, int) and b == 0):
                        act.wait_ge(c_dve.sem, c_dve.at(b - 1, "comb13"))
                    for k in range(KD):
                        last = fn(netT[:, 0, k], ps_net[:, 0, k], ACT.Copy, scale=par_l2[:, 0:1])
                    last.then_inc(evac_act, 1)
                if net >= 2:
                    fn(netT[:, net - 1, 0], ps_net[:, net % 2, 0], ACT.Copy).then_inc(evac_act, 1)

            def batch(b, first, last):
                for q in range(SLOTS):
                    act.wait_ge(hid_done, b * SLOTS + q + 1)
                    if not (first and q < 2):
                        act.wait_ge(net_chunk_done, b * SLOTS + q - 1)
                    fn(hid_hi[:, q % 2], ps_hid[:, q % 2], ACT.Relu).then_inc(hid_hi_ready, 1)
                    if first and q == 0:
                        act.wait_ge(par_step, 2)
                        fn(gate_prob[:], gate_prob[:], ACT.Exp, scale=1.0 / GATE_TEMP).then_inc(par_exp_done, 1)
                    p = pair_to_split(q, last)
                    if p is not None and p < PAIRS:
                        split_weights(b, p, not (first and p < RING))
                    elif p is not None:
                        split_weights(b + 1, p - PAIRS, True)
                    if not first and not (last and q >= C_SLOT["out"]):
                        stage_c(q, b - 1)
                    if not last:
                        stage_a(q, b + 1, not first)
                    if q % CH == 0 and q >= CH:
                        evacuate(b, q // CH - 1)
                    if last:
                        last_gates(q)
                if not last:
                    act.wait_ge(base_ready, b + 1)
                    split_x2(b + 1)
                    evacuate(b, NETS - 1)

            def halves(bank):
                return bank.rearrange("p (k s) -> p k s", k=KD)

            kind = act.value_load(type_id.rearrange("(o b) -> o b", o=1)[0:1, 0:1], min_val=0, max_val=NT - 1)
            for h in range(2):
                act.wait_ge(p_pe.sem, p_pe.at(0, f"xT{h}"))
                fn(opT_hi[:, :, rows_half(h)], halves(ps_side[:, h]), ACT.Copy).then_inc(p_act.sem, 1)
            e, cols = bass.ds(kind, 1), slice(0, F // 2)
            act.dma_start(raw_wi[:, 0], L2_expert_wi[e, :, cols].rearrange("o (k p) f -> p (o k) f", p=P)).then_inc(raw_in[0], 16)
            act.dma_start(raw_wo[:, 0], L2_expert_wo[e, cols].rearrange("o (c p) d -> p (o c) d", p=P)).then_inc(raw_in[0], 16)
            for h in range(2):
                act.wait_ge(p_pe.sem, p_pe.at(0, f"hid{h}"))
                fn(hT[:, rows_half(h)], ps_hid[0:A, h, 0:HS], ACT.Relu, bias=b1[:]).then_inc(p_act.sem, 1)
            act.wait_ge(a_in, 64)
            for h in range(2):
                for k in range(KD):
                    last = fn(xbT[:, k, rows_half(h)], halves(ps_side[:, h])[:, k], ACT.Identity, bias=beta[:, k:k + 1])
                last.then_inc(p_act.sem, 1)
            act.wait_ge(p_pe.sem, p_pe.at(0, "subj_wT"))
            fn(subj_wT_hi[:].rearrange("p k d -> p (k d)"), ps_net[:, 1, 0], ACT.Copy).then_inc(p_act.sem, 1)
            fn(prob[:, 0], ps_net[:, 1, 0], ACT.Copy).then_inc(p_act.sem, 1)
            split_weights(0, 0, False)
            for h in range(2):
                act.wait_ge(p_dve.sem, p_dve.at(0, f"x1T{h}"))
                fn(opT_hi[:, :, rows_half(h)], x1T[:, :, rows_half(h)], ACT.Copy).then_inc(p_act.sem, 1)
            split_weights(0, 1, False)
            for h in range(2):
                act.wait_ge(p_dve.sem, p_dve.at(0, f"x2T{h}"))
                fn(x2T_hi[:, :, rows_half(h)], next_x2T[:, :, rows_half(h)], ACT.Copy).then_inc(x2_hi_ready, 1)
            split_weights(0, 2, False)
            batch(0, True, False)
            with act.Fori(1, B - 1) as b:
                batch(b, False, False)
            batch(B - 1, False, True)
            last_rows()
            for q in range(C_SLOT["max"]):
                attention(q, B - 1, True)
            for h in range(2):
                for l in range(R):
                    by = e_dve if l < R - 1 else e_pool
                    act.wait_ge(by.sem, by.at(0, f"arg{l}{h}"))
                    act.wait_ge(e_act.sem, e_act.at(0, "score_col"))
                    fn(prob[:, l, rows_half(h)], prob[:, l, rows_half(h)], ACT.Exp, bias=score_col[:, l:l + 1]).then_inc(e_act.sem, 1)
            for t in range(R):
                act.wait_ge(e_dve.sem, e_dve.at(0, "late_rden"))
                fn(norm[:, t], out_bank(t, "late")[:, 0:D], ACT.Copy, scale=rden_late[:, t:t + 1]).then_inc(e_act.sem, 1)

        @block.vector
        def _(dve):
            v = nc.vector

            def stage_a(slot, i):
                def here(name):
                    dve.wait_ge(a_dve.sem, a_dve.at(i, name))

                if slot == A_SLOT["xT"]:
                    dve.wait_ge(w1_in, 32 * (i + 1))
                    v.tensor_copy(w1_hi[:], w1[:]).then_inc(a_dve.sem, 1)
                if 0 <= slot - A_SLOT["xT"] < KD:
                    k = slot - A_SLOT["xT"]
                    dve.wait_ge(a_act.sem, a_act.at(i, f"xhi{k}"))
                    v.tensor_tensor(opT_lo[:, k], ps_side[:, k], f32(opT_hi[:, k]), ALU.subtract).then_inc(a_dve.sem, 1)
                if slot == A_SLOT["xT"] + 1:
                    dve.wait_ge(a_in, 64 * (i + 1))
                    v.tensor_copy(w2_hi[:], w2[:]).then_inc(a_dve.sem, 1)
                if slot == A_SLOT["hid"]:
                    dve.wait_ge(a_act.sem, a_act.at(i, "hid"))
                    v.tensor_copy(hT_hi[0:A], hT[:]).then_inc(a_dve.sem, 1)
                    here("hid_hi")
                    v.tensor_tensor(hT_lo[0:A], hT[:], f32(hT_hi[0:A]), ALU.subtract).then_inc(a_dve.sem, 1)
                if slot == A_SLOT["subj_w"]:
                    dve.wait_ge(a_act.sem, a_act.at(i, "subj_w_hi"))
                    v.tensor_tensor(subj_wT_lo[:].rearrange("p k d -> p (k d)"), ps_side[:, 1],
                                    f32(subj_wT_hi[:].rearrange("p k d -> p (k d)")), ALU.subtract).then_inc(a_dve.sem, 1)
                if slot == A_SLOT["adapt"]:
                    for t in range(2):
                        dve.wait_ge(a_pe.sem, a_pe.at(i, f"adapt{t}"))
                        rows = slice(2 * t, 2 * t + 2)
                        v.tensor_tensor(norm[:, rows].rearrange("p r d -> p (r d)"), ps_side[:, t],
                                        x_rows[:, rows].rearrange("p r d -> p (r d)"), ALU.add).then_inc(a_dve.sem, 1)
                if slot == A_SLOT["stats"]:
                    here("sum1")
                    norm_steps(slice(0, R), here, lambda ins: ins.then_inc(a_dve.sem, 1))
                if slot == A_SLOT["xb"]:
                    here("xlo1")
                    for k in range(KD):
                        v.scalar_tensor_tensor(out=xbT[:, k], in0=f32(opT_hi[:, k]), scalar=beta[:, k:k + 1], in1=f32(opT_lo[:, k]),
                                               op0=ALU.add, op1=ALU.add).then_inc(a_dve.sem, 1)
                if slot == A_SLOT["norm"]:
                    dve.wait_ge(a_pool.sem, a_pool.at(i, "rstd"))
                    for r in range(R):
                        last = v.tensor_scalar(norm[:, r], norm[:, r], mean[:, r:r + 1], rstd[:, r:r + 1], ALU.subtract, ALU.mult)
                    last.then_inc(a_dve.sem, 1)
                if 0 <= slot - A_SLOT["normT"] < KD:
                    k = slot - A_SLOT["normT"]
                    dve.wait_ge(a_pe.sem, a_pe.at(i, f"normT{k}"))
                    here(f"xb{k}")
                    v.scalar_tensor_tensor(out=x1T[:, k], in0=ps_side[:, k], scalar=gamma[:, k:k + 1], in1=xbT[:, k],
                                           op0=ALU.mult, op1=ALU.add).then_inc(a_dve.sem, 1)
                if slot == A_SLOT["x1_lo"]:
                    here("x1T1")
                    for k in range(KD):
                        dve.wait_ge(a_act.sem, a_act.at(i, f"x1hi{k}"))
                        v.tensor_tensor(opT_lo[:, k], x1T[:, k], f32(opT_hi[:, k]), ALU.subtract).then_inc(a_dve.sem, 1)
                if 0 <= slot - A_SLOT["y"] < KD:
                    k = slot - A_SLOT["y"]
                    dve.wait_ge(a_pe.sem, a_pe.at(i, f"y{k}"))
                    v.scalar_tensor_tensor(out=next_x2T[:, k], in0=ps_side[:, k], scalar=subj_b[:, k:k + 1], in1=x1T[:, k],
                                           op0=ALU.add, op1=ALU.add).then_inc(a_dve.sem, 1)

            def make_mask(i, final):
                _, _, dve_s, _, n = c_steps(i, final)
                par_c = c_buffers(final)[0]
                v.tensor_copy(par_c[:], par[:, bass.ds(i * NPAR, NPAR)]).then_inc(dve_s.sem, 1)
                dve.wait_ge(dve_s.sem, dve_s.at(n, "par"))
                v.tensor_scalar(mask[:], rel_sign[:], par_c[:, 2:3], NEG, ALU.is_equal, ALU.mult).then_inc(dve_s.sem, 1)

            def gate_chain(part, i, final):
                pe_s, act_s, dve_s, _, n = c_steps(i, final)
                if part == 0:
                    dve.wait_ge(pe_s.sem, pe_s.at(n, "gate_h"))
                    for o in range(KD):
                        last = v.tensor_scalar(gate_h[:, o], ones[:], ps_side[:, 0, o:o + 1], 0.0, ALU.mult, ALU.max)
                    last.then_inc(dve_s.sem, 1)
                if part == 1:
                    dve.wait_ge(pe_s.sem, pe_s.at(n, "logits"))
                    v.tensor_reduce(neg_gmax[:], ps_side[:, 1, 0:NG], AX.X, ALU.max, negate=True).then_inc(dve_s.sem, 1)
                if part == 2:
                    dve.wait_ge(act_s.sem, act_s.at(n, "gate_exp"))
                    v.reciprocal(gate_rec[:], gate_sum[:]).then_inc(dve_s.sem, 1)
                    dve.wait_ge(dve_s.sem, dve_s.at(n, "gate_rec"))
                    v.tensor_scalar(gates[:], gate_e[:], gate_rec[:, 0:1], None, ALU.mult).then_inc(dve_s.sem, 1)
                    dve.wait_ge(dve_s.sem, dve_s.at(n, "gates"))
                    dve.wait_ge(base_ready, i + 1)

            def last_gates(slot):
                if slot == SLOTS - CH + 1:
                    make_mask(B - 1, True)
                if slot == END_GATE - 1:
                    gate_chain(0, B - 1, True)
                if slot == END_GATE:
                    for part in (1, 2):
                        gate_chain(part, B - 1, True)
                for n in {END_GATE: (0,), END_GATE + 1: (1, 2), END_GATE + 2: (3,)}.get(slot, ()):
                    if n > 0:
                        dve.wait_ge(e_dve.sem, e_dve.at(0, f"comb{n - 1}"))
                    half = x3T[:, :, rows_half(0)]
                    v.scalar_tensor_tensor(out=half, in0=netT[:, n, :, rows_half(0)], scalar=gates[:, n:n + 1], in1=half,
                                           op0=ALU.mult, op1=ALU.add).then_inc(e_dve.sem, 1)

            def last_rows():
                half = x3T[:, :, rows_half(1)]
                dve.wait_ge(e_pool.sem, e_pool.at(0, "comb2"))
                dve.wait_ge(net_chunk_done, B * SLOTS)
                v.scalar_tensor_tensor(out=half, in0=ps_net[:, (NETS - 1) % 2, 1].rearrange("p (k s) -> p k s", k=KD),
                                       scalar=gates[:, NG - 1:NG], in1=half, op0=ALU.mult, op1=ALU.add).then_inc(e_dve.sem, 1)
                _, _, vh, vl = c_buffers(True)
                v.memset(f32(vh[:, :, D:VW]), 1.0)
                v.memset(f32(vl[:, :, D:VW]), 0.0).then_inc(e_dve.sem, 1)
                for h in range(2):
                    dve.wait_ge(e_act.sem, e_act.at(0, f"x3hi{h}"))
                    v.tensor_tensor(opT_lo[:, :, rows_half(h)], x3T[:, :, rows_half(h)], f32(opT_hi[:, :, rows_half(h)]), ALU.subtract).then_inc(e_dve.sem, 1)

            def stage_c(slot, i):
                def here(name):
                    dve.wait_ge(c_dve.sem, c_dve.at(i, name))

                if slot == C_SLOT["gate"]:
                    make_mask(i, False)
                    gate_chain(0, i, False)
                if slot == C_SLOT["logits"]:
                    gate_chain(1, i, False)
                if slot == C_SLOT["gates"]:
                    gate_chain(2, i, False)
                if 0 <= slot - C_SLOT["comb"] < 2:
                    for n in (2 * (slot - C_SLOT["comb"]), 2 * (slot - C_SLOT["comb"]) + 1):
                        for k in range(KD):
                            if n > 0:
                                here(f"comb{k}{n - 1}")
                            v.scalar_tensor_tensor(out=x3T[:, k], in0=netT[:, n, k], scalar=gates[:, n:n + 1], in1=x3T[:, k],
                                                   op0=ALU.mult, op1=ALU.add).then_inc(c_dve.sem, 1)
                if slot == C_SLOT["x3_split"]:
                    for k in range(KD):
                        dve.wait_ge(c_act.sem, c_act.at(i, f"x3hi{k}"))
                        v.tensor_tensor(opT_lo[:, k], x3T[:, k], f32(opT_hi[:, k]), ALU.subtract).then_inc(c_dve.sem, 1)
                if slot == C_SLOT["val"]:
                    dve.wait_ge(c_act.sem, c_act.at(i, "rows1"))
                    v.tensor_copy(val_hi[:, :, 0:D], x3_rows[:]).then_inc(c_dve.sem, 1)
                    here("val_hi")
                    v.tensor_tensor(val_lo[:, :, 0:D], x3_rows[:], f32(val_hi[:, :, 0:D]), ALU.subtract).then_inc(c_dve.sem, 1)
                attention(slot, i, False)

            def attention(slot, i, final):
                pe_s, act_s, dve_s, _, m = c_steps(i, final)
                score_row = score_banks(final)[0]
                par_c = c_buffers(final)[0]

                def here(name):
                    dve.wait_ge(dve_s.sem, dve_s.at(m, name))

                if slot == C_SLOT["prefix"]:
                    dve.wait_ge(pe_s.sem, pe_s.at(m, "score_row"))
                    v.tensor_tensor_scan(prefix_max[:, 1:S + 1], score_row, floor[:], NEG, ALU.max, ALU.max).then_inc(dve_s.sem, 1)
                if slot == C_SLOT["suffix"]:
                    v.tensor_tensor_scan(suffix_max[:, S - 1::-1], score_row[:, ::-1], floor[:], NEG, ALU.max, ALU.max).then_inc(dve_s.sem, 1)
                if slot == C_SLOT["max"]:
                    dve.wait_ge(act_s.sem, act_s.at(m, "max0"))
                    for n, (side, c) in enumerate([(prefix_max[:, 0:S], 5), (suffix_max[:, 0:S], 4), (suffix_max[:, 1:S + 1], 5)]):
                        here(f"max{n}" if n else "suffix")
                        v.scalar_tensor_tensor(out=max_row[:], in0=side, scalar=par_c[:, c:c + 1], in1=max_row[:],
                                               op0=ALU.add, op1=ALU.max).then_inc(dve_s.sem, 1)
                if slot == C_SLOT["arg"]:
                    here("max3")
                    for l in range(R - 1):
                        v.tensor_tensor(prob[:, l], mask[:, l], max_row[:], ALU.subtract).then_inc(dve_s.sem, 1)
                if 0 <= slot - C_SLOT["prob_hi"] < R:
                    l = slot - C_SLOT["prob_hi"]
                    dve.wait_ge(act_s.sem, act_s.at(m, f"exp{l}"))
                    v.tensor_copy(prob_hi[:, l], prob[:, l]).then_inc(dve_s.sem, 1)
                    if l != 1:
                        here(f"phi{l}")
                        v.tensor_tensor(prob_lo[:, l], prob[:, l], f32(prob_hi[:, l]), ALU.subtract).then_inc(dve_s.sem, 1)
                if 0 <= slot - C_SLOT["out"] < 2:
                    output(slot - C_SLOT["out"], i, "final" if final else "loop")

            def last_probabilities():
                def here(name):
                    dve.wait_ge(e_dve.sem, e_dve.at(0, name))

                def maxima(h):
                    j, after = rows_half(h), slice(h * HS + 1, (h + 1) * HS + 1)
                    for n, (side, c) in enumerate([(prefix_max[:, j], 5), (suffix_max[:, j], 4), (suffix_max[:, after], 5)]):
                        here(f"max{n}{h}" if n else "suffix")
                        v.scalar_tensor_tensor(out=max_row[:, j], in0=side, scalar=par_end[:, c:c + 1], in1=max_row[:, j],
                                               op0=ALU.add, op1=ALU.max).then_inc(e_dve.sem, 1)

                def exponents(h):
                    here(f"max3{h}")
                    for l in range(R - 1):
                        v.tensor_tensor(prob[:, l, rows_half(h)], mask[:, l, rows_half(h)], max_row[:, rows_half(h)], ALU.subtract).then_inc(e_dve.sem, 1)

                def leading(l0, h):
                    part = (slice(None), slice(l0, l0 + 2), rows_half(h))
                    dve.wait_ge(e_act.sem, e_act.at(0, f"exp{l0 + 1}{h}"))
                    v.tensor_copy(prob_hi[part], prob[part]).then_inc(e_dve.sem, 1)

                def trailing(l0, h):
                    part = (slice(None), slice(l0, l0 + 2), rows_half(h))
                    here(f"phi{l0}{h}")
                    v.tensor_tensor(prob_lo[part], prob[part], f32(prob_hi[part]), ALU.subtract).then_inc(e_dve.sem, 1)

                dve.wait_ge(e_act.sem, e_act.at(0, "max0"))
                maxima(0)
                exponents(0)
                maxima(1)
                dve.wait_ge(c_pe.sem, c_pe.at(LATE, "out3"))
                leading(0, 0)
                leading(2, 0)
                trailing(0, 0)
                exponents(1)
                for n in range(2):
                    last = divisors(n, "late", par_l3, den_late)
                last.then_inc(e_dve.sem, 1)
                dve.wait_ge(e_dve.sem, e_dve.at(0, "late_den"))
                v.reciprocal(rden_late[:], den_late[:]).then_inc(e_dve.sem, 1)
                for l0 in (0, 2):
                    leading(l0, 1)
                    trailing(l0, 1)

            def divisors(n, mode, par_c, den):
                t = slice(2 * n, 2 * n + 2)
                banks = {"late": ps_net[:, n], "final": (ps_side, ps_hid)[n][:], "loop": ps_side[:]}[mode]
                return v.tensor_tensor(den[:, t], banks[:, :, D:D + 1].rearrange("p t o -> p (t o)"), par_c[:, 6 + 2 * n:8 + 2 * n], ALU.mult)

            def output(n, i, mode):
                pe_s, _, dve_s, _, m = c_steps(i, mode == "final")
                par_c, x3_c, _, _ = c_buffers(mode == "final")
                tiles = (2 * n, 2 * n + 1)
                dve.wait_ge(pe_s.sem, pe_s.at(m, f"out{tiles[1]}"))
                divisors(n, mode, par_c, den).then_inc(dve_s.sem, 1)
                dve.wait_ge(dve_s.sem, dve_s.at(m, f"den{n}"))
                v.reciprocal(rden[:, 2 * n:2 * n + 2], den[:, 2 * n:2 * n + 2]).then_inc(dve_s.sem, 1)
                dve.wait_ge(dve_s.sem, dve_s.at(m, f"rden{n}"))
                if n == 0 and not (isinstance(i, int) and i == 0):
                    dve.wait_ge(out_stored, 32 * (LATE if mode == "final" else i))
                for t in tiles:
                    v.scalar_tensor_tensor(out=out_rows[:, t], in0=out_bank(t, mode)[:, 0:D], scalar=rden[:, t:t + 1], in1=x3_c[:, t],
                                           op0=ALU.mult, op1=ALU.add).then_inc(dve_s.sem, 1)

            step = [0]

            def link(ins):
                step[0] += 1
                ins.then_inc(par_step, 1)
                dve.wait_ge(par_step, step[0])

            def parameters(slot):
                par_v = par[:].rearrange("p (b n) -> p b n", n=NPAR)
                if slot == 0:
                    dve.wait_ge(small_in, 64)
                    link(v.tensor_reduce(gv_max[:], gate_vecs[:].rearrange("p (t e) -> p t e", e=NE), AX.X, ALU.max))
                    for t in range(NT):
                        ins = v.tensor_scalar(gate_prob[:, t * NE:(t + 1) * NE], gate_vecs[:, t * NE:(t + 1) * NE], gv_max[:, t:t + 1], None, ALU.subtract)
                    link(ins)
                if slot == 1:
                    dve.wait_ge(par_exp_done, 1)
                    link(v.tensor_reduce(gv_sum[:], gate_prob[:].rearrange("p (t e) -> p t e", e=NE), AX.X, ALU.add))
                    link(v.reciprocal(gv_sum[:], gv_sum[:]))
                    for t in range(NT):
                        ins = v.tensor_scalar(gate_prob[:, t * NE:(t + 1) * NE], gate_prob[:, t * NE:(t + 1) * NE],
                                              gv_sum[:, t:t + 1], None, ALU.mult)
                    link(ins)
                if slot == 2:
                    dve.wait_ge(types_in, 16)
                    link(v.tensor_copy(type_bc[:], type_bc_i[:]))
                    for t in range(NT):
                        ins = v.tensor_scalar(onehot[:, :, t], type_bc[:], float(t), None, ALU.is_equal)
                    link(ins)
                if slot == 3:
                    for e in range(2):
                        diag = gate_prob[:, e:e + (NT - 1) * (NE + 1) + 1:NE + 1]
                        for t in range(NT):
                            ins = v.tensor_scalar(pick[:, :, t], onehot[:, :, t], diag[:, t:t + 1], None, ALU.mult)
                        link(ins)
                        link(v.tensor_reduce(par_v[:, :, e:e + 1], pick[:], AX.X, ALU.add))
                if slot == 4:
                    v.tensor_tensor(par_v[:, :, 2], onehot[:, :, 1], onehot[:, :, 0], ALU.subtract)
                    for t in range(NT):
                        ins = v.tensor_scalar(par_v[:, :, 3 + t], onehot[:, :, t], -NEG, NEG, ALU.mult, ALU.add)
                    link(ins)
                if slot in (5, 6):
                    dve.wait_ge(rel_ready, 1)
                    for r in (2 * (slot - 5), 2 * (slot - 5) + 1):
                        cnt = par_v[:, :, 6 + r]
                        link(v.tensor_scalar(cnt, onehot[:, :, 0], jcol[:, 0, r:r + 1], None, ALU.mult))
                        link(v.scalar_tensor_tensor(out=cnt, in0=onehot[:, :, 1], scalar=jcol[:, 1, r:r + 1], in1=cnt, op0=ALU.mult, op1=ALU.add))
                        link(v.scalar_tensor_tensor(out=cnt, in0=onehot[:, :, 2], scalar=float(S - 1), in1=cnt, op0=ALU.mult, op1=ALU.add))
                if 7 <= slot < 7 + R:
                    r = slot - 7
                    link(v.tensor_scalar(rel_sign[:, r], prob[:, r].bitcast(I32), 1.0, -1.0, ALU.min, ALU.max))

            def norm_steps(rows, here, done):
                for r in range(rows.start, rows.stop):
                    last = v.bn_stats(stats[:, r], norm[:, r])
                done(last)
                here("stats")
                v.tensor_tensor(mean[:, rows], stats[:, rows, 1], stats[:, rows, 4], ALU.add)
                v.tensor_tensor(mean_gap[:, rows], stats[:, rows, 1], stats[:, rows, 4], ALU.subtract)
                done(v.tensor_tensor(var_eps[:, rows], stats[:, rows, 2], stats[:, rows, 5], ALU.add))
                here("sums")
                v.tensor_scalar(mean[:, rows], mean[:, rows], 0.5, None, ALU.mult)
                v.scalar_tensor_tensor(out=mean_gap[:, rows], in0=mean_gap[:, rows], scalar=0.25, in1=mean_gap[:, rows], op0=ALU.mult, op1=ALU.mult)
                done(v.tensor_scalar(var_eps[:, rows], var_eps[:, rows], 1.0 / D, LN_EPS, ALU.mult, ALU.add))
                here("mean")
                done(v.tensor_tensor(var_eps[:, rows], var_eps[:, rows], mean_gap[:, rows], ALU.add))

            def prologue():
                def here(name):
                    dve.wait_ge(p_dve.sem, p_dve.at(0, name))

                def done(ins):
                    ins.then_inc(p_dve.sem, 1)

                def halves(bank):
                    return bank.rearrange("p (k s) -> p k s", k=KD)

                def add_x(h):
                    dve.wait_ge(p_pe.sem, p_pe.at(0, f"adapt{h}"))
                    t = slice(2 * h, 2 * h + 2)
                    done(v.tensor_tensor(norm[:, t].rearrange("p r d -> p (r d)"), ps_net[:, 0, h], x_rows[:, t].rearrange("p r d -> p (r d)"), ALU.add))
                    here(f"sum{h}")

                def statistics(h):
                    norm_steps(slice(2 * h, 2 * h + 2), lambda name: here(f"{name}{h}"), done)

                def normalise(h):
                    dve.wait_ge(p_pool.sem, p_pool.at(0, f"rstd{h}"))
                    for r in (2 * h, 2 * h + 1):
                        last = v.tensor_scalar(norm[:, r], norm[:, r], mean[:, r:r + 1], rstd[:, r:r + 1], ALU.subtract, ALU.mult)
                    done(last)

                def add_norm(h):
                    dve.wait_ge(p_pe.sem, p_pe.at(0, f"normT{h}"))
                    dve.wait_ge(p_act.sem, p_act.at(0, f"xb{h}"))
                    for k in range(KD):
                        last = v.scalar_tensor_tensor(out=x1T[:, k, rows_half(h)], in0=halves(ps_side[:, h])[:, k], scalar=gamma[:, k:k + 1],
                                                      in1=xbT[:, k, rows_half(h)], op0=ALU.mult, op1=ALU.add)
                    done(last)

                def x1_lo(h):
                    rows = rows_half(h)
                    dve.wait_ge(p_act.sem, p_act.at(0, f"x1hi{h}"))
                    done(v.tensor_tensor(opT_lo[:, :, rows], x1T[:, :, rows], f32(opT_hi[:, :, rows]), ALU.subtract))

                def add_y(h):
                    dve.wait_ge(p_pe.sem, p_pe.at(0, f"y{h}"))
                    for k in range(KD):
                        last = v.scalar_tensor_tensor(out=next_x2T[:, k, rows_half(h)], in0=halves(ps_hid[:, h])[:, k], scalar=subj_b[:, k:k + 1],
                                                      in1=x1T[:, k, rows_half(h)], op0=ALU.add, op1=ALU.add)
                    done(last)

                def x2_lo(h):
                    rows = rows_half(h)
                    dve.wait_ge(x2_hi_ready, h + 1)
                    v.tensor_tensor(x2T_lo[:, :, rows], next_x2T[:, :, rows], f32(x2T_hi[:, :, rows]), ALU.subtract).then_inc(x2_lo_ready, 1)

                dve.wait_ge(w1_in, 32)
                done(v.tensor_copy(w1_hi[:], w1[:]))
                for h in range(2):
                    dve.wait_ge(p_act.sem, p_act.at(0, f"xhi{h}"))
                    done(v.tensor_tensor(opT_lo[:, :, rows_half(h)], halves(ps_side[:, h]), f32(opT_hi[:, :, rows_half(h)]), ALU.subtract))
                dve.wait_ge(a_in, 64)
                done(v.tensor_copy(w2_hi[:], w2[:]))
                for h in range(2):
                    rows = rows_half(h)
                    dve.wait_ge(p_act.sem, p_act.at(0, f"hid{h}"))
                    done(v.tensor_copy(hT_hi[0:A, rows], hT[:, rows]))
                    here(f"hhi{h}")
                    done(v.tensor_tensor(hT_lo[0:A, rows], hT[:, rows], f32(hT_hi[0:A, rows]), ALU.subtract))
                add_x(0)
                statistics(0)
                add_x(1)
                normalise(0)
                statistics(1)
                add_norm(0)
                normalise(1)
                x1_lo(0)
                add_norm(1)
                x1_lo(1)
                add_y(0)
                add_y(1)
                x2_lo(0)
                x2_lo(1)

            def split_x2(b):
                for k in range(KD):
                    dve.wait_ge(x2_hi_ready, KD * b + k + 1)
                    v.tensor_tensor(x2T_lo[:, k], next_x2T[:, k], f32(x2T_hi[:, k]), ALU.subtract).then_inc(x2_lo_ready, 1)

            def evacuate(b, net):
                dve.wait_ge(net_chunk_done, b * SLOTS + (net + 1) * CH)
                if net == 1:
                    dve.wait_ge(evac_act, NG * b + 1)
                    both = netT[:, 0].rearrange("p k s -> p (k s)")
                    v.scalar_tensor_tensor(out=both, in0=ps_net[:, 1].rearrange("p k s -> p (k s)"), scalar=par_l2[:, 1:2], in1=both,
                                           op0=ALU.mult, op1=ALU.add).then_inc(evac_dve, 1)
                if net >= 2:
                    v.tensor_copy(netT[:, net - 1, 1], ps_net[:, net % 2, 1]).then_inc(evac_dve, 1)

            def batch(b, first, last):
                for q in range(SLOTS):
                    dve.wait_ge(hid_hi_ready, b * SLOTS + q + 1)
                    v.scalar_tensor_tensor(out=hid_lo[:, q % 2], in0=ps_hid[:, q % 2], scalar=0.0, in1=f32(hid_hi[:, q % 2]),
                                           op0=ALU.max, op1=ALU.subtract).then_inc(hid_lo_ready, 1)
                    if first:
                        parameters(q)
                    if q == CH - 1:
                        v.tensor_copy(par_l2[:], par[:, bass.ds(b * NPAR, NPAR)]).then_inc(par_l2_ready, 1)
                        dve.wait_ge(par_l2_ready, b + 1)
                    if not first and not (last and q >= C_SLOT["out"]):
                        stage_c(q, b - 1)
                    if not last:
                        stage_a(q, b + 1)
                    if q % CH == 0 and q >= 2 * CH:
                        evacuate(b, q // CH - 1)
                    if last:
                        last_gates(q)
                if not last:
                    split_x2(b + 1)
                    evacuate(b, NETS - 1)

            v.memset(zeros[:], 0.0).then_inc(zeros_ready, 1)
            v.memset(ones[:], 1.0)
            v.memset(floor[:], NEG)
            v.memset(prefix_max[:, 0:1], NEG)
            v.memset(suffix_max[:, S:S + 1], NEG)
            v.memset(f32(hT_hi[A:A + 1]), 1.0)
            v.memset(f32(hT_lo[A:A + 1]), 0.0)
            v.memset(f32(val_hi[:, :, D:VW]), 1.0)
            v.memset(f32(val_lo[:, :, D:VW]), 0.0).then_inc(const_step, 1)
            dve.wait_ge(const_step, 1)
            prologue()
            batch(0, True, False)
            with dve.Fori(1, B - 1) as b:
                batch(b, False, False)
            batch(B - 1, False, True)
            last_rows()
            for q in range(C_SLOT["max"]):
                attention(q, B - 1, True)
            last_probabilities()
            output(0, B - 1, "final")
            output(1, B - 1, "final")

        @block.gpsimd
        def _(pool):
            g = nc.gpsimd

            def stage_a(slot, i):
                if slot == A_SLOT["xT"]:
                    pool.wait_ge(a_dve.sem, a_dve.at(i, "w1_hi"))
                    g.tensor_tensor(w1_lo[:], w1[:], f32(w1_hi[:]), ALU.subtract).then_inc(a_pool.sem, 1)
                    pool.wait_ge(a_dve.sem, a_dve.at(i, "w2_hi"))
                    g.tensor_tensor(w2_lo[:], w2[:], f32(w2_hi[:]), ALU.subtract).then_inc(a_pool.sem, 1)
                if slot == A_SLOT["stats"]:
                    pool.wait_ge(a_dve.sem, a_dve.at(i, "var_eps"))
                    g.tensor_tensor(rstd[:], var_eps[:], half_pow[:], ALU.pow).then_inc(a_pool.sem, 1)

            def attention(slot, i, final):
                _, _, dve_s, pool_s, n = c_steps(i, final)
                if slot == C_SLOT["arg"]:
                    pool.wait_ge(dve_s.sem, dve_s.at(n, "max3"))
                    g.tensor_tensor(prob[:, R - 1], mask[:, R - 1], max_row[:], ALU.subtract).then_inc(pool_s.sem, 1)
                if slot == C_SLOT["prob_lo"] + 1:
                    l = 1
                    pool.wait_ge(dve_s.sem, dve_s.at(n, f"phi{l}"))
                    g.tensor_tensor(prob_lo[:, l], prob[:, l], f32(prob_hi[:, l]), ALU.subtract).then_inc(pool_s.sem, 1)

            def last_rows():
                pool.wait_ge(base_ready, B)
                half = x3T[:, :, rows_half(1)]
                for n in range(NG - 1):
                    if n > 0:
                        pool.wait_ge(e_pool.sem, e_pool.at(0, f"comb{n - 1}"))
                    pool.wait_ge(e_act.sem, e_act.at(0, f"gated{n}"))
                    g.tensor_tensor(half, netT[:, n, :, rows_half(1)], half, ALU.add).then_inc(e_pool.sem, 1)
                _, x3_end, vh, vl = c_buffers(True)
                pool.wait_ge(e_act.sem, e_act.at(0, "val_hi"))
                g.tensor_tensor(vl[:, :, 0:D], x3_end[:], f32(vh[:, :, 0:D]), ALU.subtract).then_inc(e_pool.sem, 1)

            def split_weights(b, p):
                w, half = p % RING, p // HP
                pool.wait_ge(w_hi_ready, b * PAIRS + p + 1)
                c = slice((p % HP) * 2 * P, (p % HP + 1) * 2 * P)
                t = slice(2 * (p % HP), 2 * (p % HP) + 2)
                g.tensor_tensor(wi_lo[:, w], raw_wi[:, half % 2, :, c], f32(wi_hi[:, w]), ALU.subtract)
                g.tensor_tensor(wo_lo[:, w], raw_wo[:, half % 2, t], f32(wo_hi[:, w]), ALU.subtract).then_inc(w_lo_ready, 1)

            def batch(b, first, last):
                for q in range(SLOTS):
                    p = pair_to_split(q, last)
                    if p is not None and p < PAIRS:
                        split_weights(b, p)
                    elif p is not None:
                        split_weights(b + 1, p - PAIRS)
                    if not first:
                        attention(q, b - 1, False)
                    if not last:
                        stage_a(q, b + 1)
                    if q == (END_BASE if last else A_SLOT["base"]):
                        pool.wait_ge(x2_lo_ready, KD * (b + 1))
                        if not first:
                            pool.wait_ge(c_pe.sem, c_pe.at(b - 1, "rows1"))
                        g.tensor_tensor(x3T[:], f32(x2T_hi[:]), f32(x2T_lo[:]), ALU.add).then_inc(base_ready, 1)

            g.memset(ident[:], 0.0).then_inc(const_ready, 1)
            pool.wait_ge(const_ready, 1)
            g.affine_select(out=ident[:], in_=ident[:], compare_op=ALU.not_equal, fill=1.0, base=0,
                            pattern=[[-1, P]], channel_multiplier=1).then_inc(const_ready, 1)
            g.memset(half_pow[:], -0.5)
            g.iota(jcol_i[:], pattern=[[P, R]], base=0, channel_multiplier=1).then_inc(const_ready, 1)
            pool.wait_ge(const_ready, 3)
            pool.wait_ge(p_dve.sem, p_dve.at(0, "w1_hi"))
            g.tensor_tensor(w1_lo[:], w1[:], f32(w1_hi[:]), ALU.subtract).then_inc(p_pool.sem, 1)
            pool.wait_ge(p_dve.sem, p_dve.at(0, "w2_hi"))
            g.tensor_tensor(w2_lo[:], w2[:], f32(w2_hi[:]), ALU.subtract).then_inc(p_pool.sem, 1)
            for h in range(2):
                rows = slice(2 * h, 2 * h + 2)
                pool.wait_ge(p_dve.sem, p_dve.at(0, f"var_eps{h}"))
                g.tensor_tensor(rstd[:, rows], var_eps[:, rows], half_pow[:, rows], ALU.pow).then_inc(p_pool.sem, 1)
            pool.wait_ge(p_act.sem, p_act.at(0, "subj_w"))
            g.tensor_tensor(subj_wT_lo[:].rearrange("p k d -> p (k d)"), prob[:, 0], f32(subj_wT_hi[:].rearrange("p k d -> p (k d)")),
                            ALU.subtract).then_inc(p_pool.sem, 1)
            for p in range(AHEAD):
                split_weights(0, p)
            pool.wait_ge(small_in, 64)
            g.tensor_copy(att_v_bc[:], att_v[:].to_broadcast([A, P]))
            g.tensor_copy(att_w_hi[:], att_w[:]).then_inc(att_w_ready, 1)
            pool.wait_ge(att_w_ready, 1)
            g.tensor_tensor(att_w_lo[:], att_w[:], f32(att_w_hi[:]), ALU.subtract).then_inc(att_w_ready, 1)
            rel = prob[:].bitcast(I32)
            g.iota(rel, pattern=[[-P, R], [1, S]], base=0, channel_multiplier=-1).then_inc(const_ready, 1)
            pool.wait_ge(const_ready, 4)
            g.tensor_scalar(jcol[:, 0], jcol_i[:], 1.0, None, ALU.add)
            g.tensor_scalar(jcol[:, 1], jcol_i[:], -1.0, float(S), ALU.mult, ALU.add).then_inc(rel_ready, 1)
            batch(0, True, False)
            with pool.Fori(1, B - 1) as b:
                batch(b, False, False)
            batch(B - 1, False, True)
            last_rows()
            for h in range(2):
                rows = rows_half(h)
                pool.wait_ge(e_dve.sem, e_dve.at(0, f"max3{h}"))
                g.tensor_tensor(prob[:, R - 1, rows], mask[:, R - 1, rows], max_row[:, rows], ALU.subtract).then_inc(e_pool.sem, 1)
            pool.wait_ge(e_dve.sem, e_dve.at(0, "phi20"))
            part = (slice(None), slice(2, 4), rows_half(0))
            g.tensor_tensor(prob_lo[part], prob[part], f32(prob_hi[part]), ALU.subtract).then_inc(e_pool.sem, 1)
            for t in range(R):
                pool.wait_ge(e_act.sem, e_act.at(0, f"late{t}"))
                g.tensor_tensor(norm[:, t], norm[:, t], x3_rows[:, t], ALU.add).then_inc(e_pool.sem, 1)


_INS = ["x", "itok_B_0_8", "itok_B_0_7", "itok_B_0_2",
        "L0_cond_W1", "L0_cond_b1", "L0_cond_W2", "L0_cond_b2", "L0_cond_gamma", "L0_cond_beta",
        "L1_cond_weight", "L1_cond_bias",
        "L2_cond_expert_wi", "L2_cond_expert_wo", "L2_cond_share_wi", "L2_cond_share_wo",
        "L2_cond_gate_vecs", "L2_cond_gate_w1", "L2_cond_gate_w2",
        "L3_cond_W1", "L3_cond_b1", "L3_cond_v"]


def kernel(**inputs):
    import numpy as _np
    import concourse.bacc as _bacc
    from concourse import mybir as _mybir
    from concourse.bass_utils import run_bass_kernel_spmd as _run

    nc = _bacc.Bacc("TRN2", target_bir_lowering=False, num_devices=1)
    arrays, args = {}, []
    for name in _INS:
        a = _np.ascontiguousarray(inputs[name])
        arrays[f"in_{name}_dram"] = a
        args.append(nc.dram_tensor(f"in_{name}_dram", a.shape, _mybir.dt.from_np(a.dtype), kind="ExternalInput").ap())
    shape = inputs["x"].shape
    args.append(nc.dram_tensor("out_0_dram", shape, _mybir.dt.float32, kind="ExternalOutput").ap())
    cond_resid_program(nc, *args)
    r = _run(nc, [arrays], core_ids=[0])
    return r.results[0]["out_0_dram"]
```
